# Optimizing a Trainium2 kernel written in Bass

```python
import numpy as np
import jax
import jax.numpy as jnp

def _softmax(x, axis=-1):
    return jax.nn.softmax(x, axis=axis)

def _gelu(x):
    return jax.nn.gelu(x, approximate=True)

def _silu(x):
    return jax.nn.silu(x)

def _sigmoid(x):
    return jax.nn.sigmoid(x)

def _layernorm(x, axis=-1, eps=1e-05):
    m = jnp.mean(x, axis=axis, keepdims=True)
    v = jnp.var(x, axis=axis, keepdims=True)
    return (x - m) / jnp.sqrt(v + eps)

def _scatter_add(tgt, idx, src, axis=0):
    return tgt.at[idx].add(src)

def _segment_sum(src, seg, n):
    return jax.ops.segment_sum(src, seg, n)
kernel_name = 'mk_adaln_ffn_d4_seqx_r8_6ba9fa'

def setup_inputs(seed: int=0):
    np.random.seed(seed)
    _w = jnp.asarray

    def _rec_inputs():
        import jax
        import jax.numpy as jnp
        _rk = jax.random.key(seed)
        x = 7.22e-05 + 1 * jax.random.normal(jax.random.fold_in(_rk, 1), (64, 32, 128), jnp.float32)
        _lenS = 32 - jax.random.randint(jax.random.fold_in(_rk, 7), (64,), 0, max(1, 32 // 4) + 1, jnp.int32)
        _lenS2 = 32 - jax.random.randint(jax.random.fold_in(_rk, 8), (64,), 0, max(1, 32 // 4) + 1, jnp.int32)
        cond_8 = jax.random.uniform(jax.random.fold_in(_rk, 11), (64, 8), jnp.float32, 0.0, 0.999837)
        return (x, cond_8)
    x, cond_8 = _rec_inputs()

    def _L0_cond_setup():
        import jax, jax.numpy as jnp
        import numpy as np
        key = jax.random.key(seed)
        k1, k2, k3, k4, k5 = jax.random.split(key, 5)
        B, N, T, O, G = (32, 32, 128, 128, 8)
        x = jax.random.normal(k1, (B, N, T), dtype=jnp.float32)
        y = jax.random.uniform(k2, (B, G), dtype=jnp.float32)
        weight = jax.random.normal(k3, (G, O, T), dtype=jnp.float32) * (1.0 / np.sqrt(T))
        mask = jax.random.uniform(k4, (O, T), dtype=jnp.float32)
        bias = jax.random.normal(k5, (O,), dtype=jnp.float32)
        return {'x': x, 'y': y, 'weight': weight, 'mask': mask, 'bias': bias}
    _L0_cond_all = _L0_cond_setup()
    _L0_cond_in = {k: v for k, v in _L0_cond_all.items() if k in ('weight', 'mask', 'bias')}
    del _L0_cond_all

    def _L0_ffn_setup():
        import jax, jax.numpy as jnp
        import numpy as np
        B, T, D, E, H = (8, 256, 128, 8, 32)
        LN_EPS = 1e-05
        key = jax.random.key(seed)
        ks = jax.random.split(key, 4)
        return {'x': jax.random.normal(ks[0], (B, T, D), dtype=jnp.float32), 'Wg': jax.random.normal(ks[1], (E, D), dtype=jnp.float32) * 0.02, 'ln_scale': jnp.ones((E, D), dtype=jnp.float32), 'ln_bias': jnp.zeros((E, D), dtype=jnp.float32), 'W1': jax.random.normal(ks[2], (E, D, H), dtype=jnp.float32) * 0.02, 'b1': jnp.zeros((E, H), dtype=jnp.float32), 'W2': jax.random.normal(ks[3], (E, H, D), dtype=jnp.float32) * 0.02, 'b2': jnp.zeros((E, D), dtype=jnp.float32)}
    _L0_ffn_all = _L0_ffn_setup()
    _L0_ffn_in = {k: v for k, v in _L0_ffn_all.items() if k in ('Wg', 'ln_scale', 'ln_bias', 'W1', 'b1', 'W2', 'b2')}
    del _L0_ffn_all

    def _L1_cond_setup():
        import jax, jax.numpy as jnp
        import numpy as np
        TOP_K = 2
        NUM_MOE_LAYERS = 12

        def _gemma_mlp(x, gate_w, up_w, down_w):
            g = jnp.einsum('bsh,hi->bsi', x, gate_w)
            u = jnp.einsum('bsh,hi->bsi', x, up_w)
            return jnp.einsum('bsi,ih->bsh', jax.nn.gelu(g, approximate=True) * u, down_w)
        key = jax.random.key(seed)
        ks = jax.random.split(key, 8)
        B, S, H, I, E = (32, 32, 128, 512, 8)
        std = 0.02
        return {'x': jax.random.normal(ks[0], (B, S, H), jnp.float32), 'router_logits': jax.random.normal(ks[1], (B, E), jnp.float32), 'skill_gate': jax.random.normal(ks[2], (E, H, I), jnp.float32) * std, 'skill_up': jax.random.normal(ks[3], (E, H, I), jnp.float32) * std, 'skill_down': jax.random.normal(ks[4], (E, I, H), jnp.float32) * std, 'shared_gate': jax.random.normal(ks[5], (H, I), jnp.float32) * std, 'shared_up': jax.random.normal(ks[6], (H, I), jnp.float32) * std, 'shared_down': jax.random.normal(ks[7], (I, H), jnp.float32) * std}
    _L1_cond_all = _L1_cond_setup()
    _L1_cond_in = {k: v for k, v in _L1_cond_all.items() if k in ('skill_gate', 'skill_up', 'skill_down', 'shared_gate', 'shared_up', 'shared_down')}
    del _L1_cond_all

    def _L1_ffn_setup():
        import jax, jax.numpy as jnp
        import numpy as np
        H = 128
        I = 256
        E = 32
        B, S = (4, 256)

        def _grouped_mm(a, w, group_sizes):
            return jax.lax.ragged_dot(a, w, group_sizes)

        def _swiglu(x, gw, uw, dw):
            return jax.nn.silu(x @ gw) * (x @ uw) @ dw
        key = jax.random.key(seed)
        ks = jax.random.split(key, 8)
        scale = 0.02
        inp = {'hidden_states': jax.random.normal(ks[0], (B, S, H), dtype=jnp.float32), 'gate_w': jax.random.normal(ks[1], (H, E), dtype=jnp.float32) * scale, 'shared_gate_w': jax.random.normal(ks[2], (H, I), dtype=jnp.float32) * scale, 'shared_up_w': jax.random.normal(ks[3], (H, I), dtype=jnp.float32) * scale, 'shared_down_w': jax.random.normal(ks[4], (I, H), dtype=jnp.float32) * scale, 'routed_gate_w': jax.random.normal(ks[5], (E, H, I), dtype=jnp.float32) * scale, 'routed_up_w': jax.random.normal(ks[6], (E, H, I), dtype=jnp.float32) * scale, 'routed_down_w': jax.random.normal(ks[7], (E, I, H), dtype=jnp.float32) * scale}
        return inp
    _L1_ffn_all = _L1_ffn_setup()
    _L1_ffn_in = {k: v for k, v in _L1_ffn_all.items() if k in ('gate_w', 'shared_gate_w', 'shared_up_w', 'shared_down_w', 'routed_gate_w', 'routed_up_w', 'routed_down_w')}
    del _L1_ffn_all

    def _L2_cond_setup():
        import jax, jax.numpy as jnp
        import numpy as np
        R = 16
        ALPHA = 32.0
        SCALING = ALPHA / R
        key = jax.random.key(seed)
        ks = jax.random.split(key, 6)
        B, T, C, O, E = (16, 1500, 128, 128, 8)
        x = jax.random.normal(ks[0], (B, T, C), dtype=jnp.float32)
        w = jax.random.uniform(ks[1], (B, E), dtype=jnp.float32)
        W_base = jax.random.normal(ks[2], (O, C), dtype=jnp.float32) * 0.02
        b_base = jax.random.normal(ks[3], (O,), dtype=jnp.float32) * 0.02
        As = jax.random.normal(ks[4], (E, R, C), dtype=jnp.float32) * 0.02
        Bs = jax.random.normal(ks[5], (E, O, R), dtype=jnp.float32) * 0.02
        return {'x': x, 'w': w, 'W_base': W_base, 'b_base': b_base, 'As': As, 'Bs': Bs}
    _L2_cond_all = _L2_cond_setup()
    _L2_cond_in = {k: v for k, v in _L2_cond_all.items() if k in ('W_base', 'b_base', 'As', 'Bs')}
    del _L2_cond_all

    def _L2_ffn_setup():
        import jax, jax.numpy as jnp
        import numpy as np
        LN_EPS = 0.001
        EPS = 1e-05
        QB = 128.0

        def ste_round(x):
            return x + jax.lax.stop_gradient(jnp.round(x) - x)
        key = jax.random.key(seed)
        k1, k2 = jax.random.split(key)
        x = jax.random.normal(k1, (4, 1024, 128), dtype=jnp.float32)
        weight = jax.random.normal(k2, (128, 128), dtype=jnp.float32) * 0.02
        ln_gamma = jnp.ones((128,), dtype=jnp.float32)
        ln_beta = jnp.zeros((128,), dtype=jnp.float32)
        return {'x': x, 'weight': weight, 'ln_gamma': ln_gamma, 'ln_beta': ln_beta}
    _L2_ffn_all = _L2_ffn_setup()
    _L2_ffn_in = {k: v for k, v in _L2_ffn_all.items() if k in ('weight', 'ln_gamma', 'ln_beta')}
    del _L2_ffn_all

    def _L3_cond_setup():
        import jax, jax.numpy as jnp
        import numpy as np
        B, S, D = (16, 256, 128)
        E, H = (8, 256)
        key = jax.random.key(seed)
        ks = jax.random.split(key, 8)
        scale = 0.02
        x = jax.random.normal(ks[0], (B, S, D), dtype=jnp.float32)
        opcode_onehot = jax.random.uniform(ks[1], (B, E), dtype=jnp.float32)
        W_up = jax.random.normal(ks[2], (E, H, D), dtype=jnp.float32) * scale
        b_up = jnp.zeros((E, H), dtype=jnp.float32)
        W_gate = jax.random.normal(ks[3], (E, H, D), dtype=jnp.float32) * scale
        b_gate = jnp.zeros((E, H), dtype=jnp.float32)
        W_down = jax.random.normal(ks[4], (E, D, H), dtype=jnp.float32) * scale
        b_down = jnp.zeros((E, D), dtype=jnp.float32)
        return {'x': x, 'opcode_onehot': opcode_onehot, 'W_up': W_up, 'b_up': b_up, 'W_gate': W_gate, 'b_gate': b_gate, 'W_down': W_down, 'b_down': b_down}
    _L3_cond_all = _L3_cond_setup()
    _L3_cond_in = {k: v for k, v in _L3_cond_all.items() if k in ('W_up', 'b_up', 'W_gate', 'b_gate', 'W_down', 'b_down')}
    del _L3_cond_all

    def _L3_ffn_setup():
        import jax, jax.numpy as jnp
        import numpy as np
        import math
        D_IN = 128
        FEATURES = (512, 512, 128)
        BATCH, SEQ = (8, 256)

        def _conn_dense(kernel_bool, x):
            w = jnp.where(kernel_bool, jnp.float32(1.0), jnp.float32(-1.0))
            return x @ w
        key = jax.random.key(seed)
        kx, kk0, kk1, kk2 = jax.random.split(key, 4)
        x = jax.random.normal(kx, (BATCH, SEQ, D_IN), dtype=jnp.float32)
        k0 = jax.random.randint(kk0, (2 * D_IN, FEATURES[0]), 0, 2).astype(jnp.bool_)
        k1 = jax.random.randint(kk1, (FEATURES[0], FEATURES[1]), 0, 2).astype(jnp.bool_)
        k2 = jax.random.randint(kk2, (FEATURES[1], FEATURES[2]), 0, 2).astype(jnp.bool_)
        s0 = jnp.asarray(1.0 / math.sqrt(2 * D_IN), dtype=jnp.float32)
        s1 = jnp.asarray(1.0 / math.sqrt(FEATURES[0]), dtype=jnp.float32)
        s2 = jnp.asarray(1.0 / math.sqrt(FEATURES[1]), dtype=jnp.float32)
        return {'x': x, 'k0': k0, 'k1': k1, 'k2': k2, 's0': s0, 's1': s1, 's2': s2}
    _L3_ffn_all = _L3_ffn_setup()
    _L3_ffn_in = {k: v for k, v in _L3_ffn_all.items() if k in ('k0', 'k1', 'k2', 's0', 's1', 's2')}
    del _L3_ffn_all
    return {'x': x, 'cond_8': cond_8, 'L0_cond_weight': _L0_cond_in['weight'], 'L0_cond_mask': _L0_cond_in['mask'], 'L0_cond_bias': _L0_cond_in['bias'], 'L0_ffn_Wg': _L0_ffn_in['Wg'], 'L0_ffn_ln_scale': _L0_ffn_in['ln_scale'], 'L0_ffn_ln_bias': _L0_ffn_in['ln_bias'], 'L0_ffn_W1': _L0_ffn_in['W1'], 'L0_ffn_b1': _L0_ffn_in['b1'], 'L0_ffn_W2': _L0_ffn_in['W2'], 'L0_ffn_b2': _L0_ffn_in['b2'], 'L1_cond_skill_gate': _L1_cond_in['skill_gate'], 'L1_cond_skill_up': _L1_cond_in['skill_up'], 'L1_cond_skill_down': _L1_cond_in['skill_down'], 'L1_cond_shared_gate': _L1_cond_in['shared_gate'], 'L1_cond_shared_up': _L1_cond_in['shared_up'], 'L1_cond_shared_down': _L1_cond_in['shared_down'], 'L1_ffn_gate_w': _L1_ffn_in['gate_w'], 'L1_ffn_shared_gate_w': _L1_ffn_in['shared_gate_w'], 'L1_ffn_shared_up_w': _L1_ffn_in['shared_up_w'], 'L1_ffn_shared_down_w': _L1_ffn_in['shared_down_w'], 'L1_ffn_routed_gate_w': _L1_ffn_in['routed_gate_w'], 'L1_ffn_routed_up_w': _L1_ffn_in['routed_up_w'], 'L1_ffn_routed_down_w': _L1_ffn_in['routed_down_w'], 'L2_cond_W_base': _L2_cond_in['W_base'], 'L2_cond_b_base': _L2_cond_in['b_base'], 'L2_cond_As': _L2_cond_in['As'], 'L2_cond_Bs': _L2_cond_in['Bs'], 'L2_ffn_weight': _L2_ffn_in['weight'], 'L2_ffn_ln_gamma': _L2_ffn_in['ln_gamma'], 'L2_ffn_ln_beta': _L2_ffn_in['ln_beta'], 'L3_cond_W_up': _L3_cond_in['W_up'], 'L3_cond_b_up': _L3_cond_in['b_up'], 'L3_cond_W_gate': _L3_cond_in['W_gate'], 'L3_cond_b_gate': _L3_cond_in['b_gate'], 'L3_cond_W_down': _L3_cond_in['W_down'], 'L3_cond_b_down': _L3_cond_in['b_down'], 'L3_ffn_k0': _L3_ffn_in['k0'], 'L3_ffn_k1': _L3_ffn_in['k1'], 'L3_ffn_k2': _L3_ffn_in['k2'], 'L3_ffn_s0': _L3_ffn_in['s0'], 'L3_ffn_s1': _L3_ffn_in['s1'], 'L3_ffn_s2': _L3_ffn_in['s2']}

def reference(x, cond_8, L0_cond_weight, L0_cond_mask, L0_cond_bias, L0_ffn_Wg, L0_ffn_ln_scale, L0_ffn_ln_bias, L0_ffn_W1, L0_ffn_b1, L0_ffn_W2, L0_ffn_b2, L1_cond_skill_gate, L1_cond_skill_up, L1_cond_skill_down, L1_cond_shared_gate, L1_cond_shared_up, L1_cond_shared_down, L1_ffn_gate_w, L1_ffn_shared_gate_w, L1_ffn_shared_up_w, L1_ffn_shared_down_w, L1_ffn_routed_gate_w, L1_ffn_routed_up_w, L1_ffn_routed_down_w, L2_cond_W_base, L2_cond_b_base, L2_cond_As, L2_cond_Bs, L2_ffn_weight, L2_ffn_ln_gamma, L2_ffn_ln_beta, L3_cond_W_up, L3_cond_b_up, L3_cond_W_gate, L3_cond_b_gate, L3_cond_W_down, L3_cond_b_down, L3_ffn_k0, L3_ffn_k1, L3_ffn_k2, L3_ffn_s0, L3_ffn_s1, L3_ffn_s2):
    import jax
    import jax.numpy as jnp

    def _L0_cond_ref(x, y, weight, mask, bias):
        import jax, jax.numpy as jnp
        import numpy as np
        masked_w = weight * mask[None, :, :]
        w_bot = jnp.einsum('bg,got->bot', y, masked_w)
        return jnp.einsum('bnt,bot->bno', x, w_bot) + bias

    def _L0_ffn_ref(x, Wg, ln_scale, ln_bias, W1, b1, W2, b2):
        import jax, jax.numpy as jnp
        import numpy as np
        B, T, D, E, H = (8, 256, 128, 8, 32)
        LN_EPS = 1e-05
        Bs, Ts, Ds = x.shape
        xt = x.reshape(Bs * Ts, Ds)
        logits = xt @ Wg.T
        top1 = jnp.argmax(logits, axis=-1)
        mu = jnp.mean(xt, axis=-1, keepdims=True)
        var = jnp.mean(jnp.square(xt - mu), axis=-1, keepdims=True)
        xhat = (xt - mu) * jax.lax.rsqrt(var + LN_EPS)
        n_experts = Wg.shape[0]

        def body(y, p):
            s_e, b_e, w1, bb1, w2, bb2, eid = p
            h = jax.nn.gelu((xhat * s_e + b_e) @ w1 + bb1, approximate=False)
            out = h @ w2 + bb2
            mask = (top1 == eid)[:, None].astype(out.dtype)
            return (y + mask * out, None)
        y0 = jnp.zeros_like(xt)
        y, _ = jax.lax.scan(body, y0, (ln_scale, ln_bias, W1, b1, W2, b2, jnp.arange(n_experts)))
        return y.reshape(Bs, Ts, Ds)

    def _L1_cond_ref(x, router_logits, skill_gate, skill_up, skill_down, shared_gate, shared_up, shared_down):
        import jax, jax.numpy as jnp
        import numpy as np
        TOP_K = 2
        NUM_MOE_LAYERS = 12

        def _gemma_mlp(x, gate_w, up_w, down_w):
            g = jnp.einsum('bsh,hi->bsi', x, gate_w)
            u = jnp.einsum('bsh,hi->bsi', x, up_w)
            return jnp.einsum('bsi,ih->bsh', jax.nn.gelu(g, approximate=True) * u, down_w)
        B = x.shape[0]
        E = skill_gate.shape[0]
        rw = jax.nn.softmax(router_logits.astype(jnp.float32), axis=-1)
        w, sel = jax.lax.top_k(rw, TOP_K)
        w = w / w.sum(axis=-1, keepdims=True)
        w = w.astype(x.dtype)
        scale = 1.0 / NUM_MOE_LAYERS
        w = scale * w + (1.0 - scale) * jax.lax.stop_gradient(w)
        dense_w = jnp.zeros((B, E), x.dtype).at[jnp.arange(B)[:, None], sel].add(w)

        def step(acc, params):
            g, u, d, we = params
            return (acc + we[:, None, None] * _gemma_mlp(x, g, u, d), None)
        out, _ = jax.lax.scan(step, jnp.zeros_like(x), (skill_gate, skill_up, skill_down, dense_w.T))
        out = out + _gemma_mlp(x, shared_gate, shared_up, shared_down)
        return out

    def _L1_ffn_ref(hidden_states, gate_w, shared_gate_w, shared_up_w, shared_down_w, routed_gate_w, routed_up_w, routed_down_w):
        import jax, jax.numpy as jnp
        import numpy as np
        H = 128
        I = 256
        E = 32
        B, S = (4, 256)

        def _grouped_mm(a, w, group_sizes):
            return jax.lax.ragged_dot(a, w, group_sizes)

        def _swiglu(x, gw, uw, dw):
            return jax.nn.silu(x @ gw) * (x @ uw) @ dw
        b, s, h = hidden_states.shape
        x = hidden_states.reshape(-1, h)
        shared_out = _swiglu(x, shared_gate_w, shared_up_w, shared_down_w)
        logits = x @ gate_w
        topk_ids = jnp.argmax(logits, axis=-1)
        topk_val = jnp.max(logits, axis=-1)
        scores = jax.nn.sigmoid(topk_val)[:, None]
        xs = x * scores
        tokens_per_expert = jnp.zeros((E,), jnp.int32).at[topk_ids].add(1)
        order = jnp.argsort(topk_ids)
        sorted_x = xs[order]
        g = _grouped_mm(sorted_x, routed_gate_w, tokens_per_expert)
        u = _grouped_mm(sorted_x, routed_up_w, tokens_per_expert)
        d = _grouped_mm(jax.nn.silu(g) * u, routed_down_w, tokens_per_expert)
        inv = jnp.argsort(order)
        routed_out = d[inv]
        return (shared_out + routed_out).reshape(b, s, h)

    def _L2_cond_ref(x, w, W_base, b_base, As, Bs):
        import jax, jax.numpy as jnp
        import numpy as np
        R = 16
        ALPHA = 32.0
        SCALING = ALPHA / R
        out = jnp.einsum('btc,oc->bto', x, W_base) + b_base
        h = jnp.einsum('btc,erc->bter', x, As)
        lora = jnp.einsum('bter,eor,be->bto', h, Bs, w)
        return out + lora * SCALING

    def _L2_ffn_ref(x, weight, ln_gamma, ln_beta):
        import jax, jax.numpy as jnp
        import numpy as np
        LN_EPS = 0.001
        EPS = 1e-05
        QB = 128.0

        def ste_round(x):
            return x + jax.lax.stop_gradient(jnp.round(x) - x)
        mu = jnp.mean(x, axis=-1, keepdims=True)
        var = jnp.var(x, axis=-1, keepdims=True)
        xn = (x - mu) * jax.lax.rsqrt(var + LN_EPS) * ln_gamma + ln_beta
        beta = jnp.mean(jnp.abs(weight))
        w_q = jnp.clip(ste_round(weight / (beta + EPS)), -1.0, 1.0)
        gamma = jnp.max(jnp.abs(xn))
        xq = jnp.clip(xn * QB / gamma, -QB + EPS, QB - EPS)
        y = jnp.einsum('bsd,du->bsu', xq, w_q)
        return y * (gamma * beta / QB)

    def _L3_cond_ref(x, opcode_onehot, W_up, b_up, W_gate, b_gate, W_down, b_down):
        import jax, jax.numpy as jnp
        import numpy as np
        B, S, D = (16, 256, 128)
        E, H = (8, 256)
        expert = jnp.argmax(opcode_onehot, axis=-1)
        wu, bu = (W_up[expert], b_up[expert])
        wg, bg = (W_gate[expert], b_gate[expert])
        wd, bd = (W_down[expert], b_down[expert])
        up = jnp.einsum('bsd,bhd->bsh', x, wu) + bu[:, None, :]
        gate = jnp.einsum('bsd,bhd->bsh', x, wg) + bg[:, None, :]
        hidden = jax.nn.silu(up) * gate
        out = jnp.einsum('bsh,bdh->bsd', hidden, wd) + bd[:, None, :]
        return out

    def _L3_ffn_ref(x, k0, k1, k2, s0, s1, s2):
        import jax, jax.numpy as jnp
        import numpy as np
        import math
        D_IN = 128
        FEATURES = (512, 512, 128)
        BATCH, SEQ = (8, 256)

        def _conn_dense(kernel_bool, x):
            w = jnp.where(kernel_bool, jnp.float32(1.0), jnp.float32(-1.0))
            return x @ w
        h = jnp.concatenate([x, -x], axis=-1)
        h = s0 * _conn_dense(k0, h)
        h = jax.nn.relu(h) * 2
        h = s1 * _conn_dense(k1, h)
        h = jax.nn.relu(h) * 2
        h = s2 * _conn_dense(k2, h)
        return h
    x = x + _L0_ffn_ref(_L0_cond_ref(x, cond_8, L0_cond_weight, L0_cond_mask, L0_cond_bias), L0_ffn_Wg, L0_ffn_ln_scale, L0_ffn_ln_bias, L0_ffn_W1, L0_ffn_b1, L0_ffn_W2, L0_ffn_b2)
    x = x + _L1_ffn_ref(_L1_cond_ref(x, cond_8, L1_cond_skill_gate, L1_cond_skill_up, L1_cond_skill_down, L1_cond_shared_gate, L1_cond_shared_up, L1_cond_shared_down), L1_ffn_gate_w, L1_ffn_shared_gate_w, L1_ffn_shared_up_w, L1_ffn_shared_down_w, L1_ffn_routed_gate_w, L1_ffn_routed_up_w, L1_ffn_routed_down_w)
    x = x + _L2_ffn_ref(_L2_cond_ref(x, cond_8, L2_cond_W_base, L2_cond_b_base, L2_cond_As, L2_cond_Bs), L2_ffn_weight, L2_ffn_ln_gamma, L2_ffn_ln_beta)
    x = x + _L3_ffn_ref(_L3_cond_ref(x, cond_8, L3_cond_W_up, L3_cond_b_up, L3_cond_W_gate, L3_cond_b_gate, L3_cond_W_down, L3_cond_b_down), L3_ffn_k0, L3_ffn_k1, L3_ffn_k2, L3_ffn_s0, L3_ffn_s1, L3_ffn_s2)
    return x

_drawn_inputs = setup_inputs


def setup_inputs(seed=0):
    import zlib

    import numpy as np

    out = dict(_drawn_inputs(seed))
    spreads = {'L0_ffn_ln_scale': (1.0, 0.2),
     'L0_ffn_ln_bias': (0.0, 0.1),
     'L0_ffn_b1': (0.0, 0.1),
     'L0_ffn_b2': (0.0, 0.1),
     'L2_ffn_ln_gamma': (1.0, 0.2),
     'L2_ffn_ln_beta': (0.0, 0.1),
     'L3_cond_b_up': (0.0, 0.1),
     'L3_cond_b_gate': (0.0, 0.1),
     'L3_cond_b_down': (0.0, 0.1)}
    factors = {}
    for name, (base, spread) in spreads.items():
        noise = np.random.default_rng([zlib.crc32(name.encode()), seed]).standard_normal(out[name].shape)
        drawn = base * np.exp(spread * noise) if base else spread * noise
        out[name] = jnp.asarray(drawn.astype(out[name].dtype))
    for name, factor in factors.items():
        out[name] = (out[name] * factor).astype(out[name].dtype)
    return out
```

```python
from contextlib import ExitStack

import numpy as np

import concourse.bass as bass
from concourse import mybir

F32 = mybir.dt.float32
F32R = mybir.dt.float32r
BF16 = mybir.dt.bfloat16
I32 = mybir.dt.int32
U8 = mybir.dt.uint8
ALU = mybir.AluOpType
ACT = mybir.ActivationFunctionType
AX_X = mybir.AxisListType.X

P = 128
NSEQ, SEQ = 64, 32
NTOK = NSEQ * SEQ
NT = NTOK // P
SPT = P // SEQ
CH = 512
NC = NTOK // CH
TPC = CH // P
E = 8
H0 = 32
I1 = 512
EF, IF = 32, 256
I3 = 256
R2 = 16
F3 = 512


def worst_groups(rows, experts, size):
    return (rows + experts * (size - 1)) // size


G1 = worst_groups(2 * NSEQ, E, SPT)
GF = worst_groups(NTOK, EF, P)
G3 = worst_groups(NSEQ, E, SPT)
W1C = 3 * I1
W1F = 3 * IF
W3C = 3 * I3
B3C = 2 * I3 + P
SPILL1 = 2 * NTOK


def f32_constants():
    p = np.arange(P)[:, None]
    q = np.arange(P)[None, :]
    return {
        "ident": (p == q),
        "ones": np.ones((P, P)),
        "quad": np.concatenate([(q // SEQ == r) & (p >= 0) for r in range(SPT)], 1),
        "pick": np.concatenate([(p == SPT * np.arange(NT)[None, :] + r) for r in range(SPT)], 1),
        "rank_up": np.repeat(np.arange(E)[None, :] == p, R2, 1),
        "place": np.tile(np.arange(SPT * G1)[None, :], (P, 1)),
        "group": np.tile(np.arange(max(G1, GF, G3))[None, :], (P, 1)),
        "steps_seq": np.tile(SPT * np.arange(NSEQ // SPT)[None, :], (P, 1)),
        "steps_tile": np.tile(P * np.arange(NT)[None, :], (P, 1)),
        "rev": np.tile(EF - np.arange(EF)[None, :], (P, 1)),
        "spill": SPILL1 + P * np.arange(G1)[None, :] + p,
        "within": p % SEQ,
        "first": p < NSEQ,
        "second": p >= NSEQ,
        "absent": -1000.0 * (p >= NSEQ),
        "inner": np.tile((np.arange(EF * NT)[None, :] % NT != 0), (P, 1)),
    }


def bf16_constants():
    p = np.arange(P)[:, None]
    q = np.arange(P)[None, :]
    return {
        "ident": (p == q),
        "before": (p < q),
        "ones": np.ones((P, P)),
        "quad": np.concatenate([(q // SEQ == r) & (p >= 0) for r in range(SPT)], 1),
        "pair": np.concatenate([p * (q // SEQ == r) for r in range(SPT)], 1),
        "spread": np.repeat(np.arange(E)[None, :] == p, H0, 1),
    }


def packed(parts, dtype):
    at, where = 0, {}
    for name, a in parts.items():
        where[name] = (at, a.shape[1])
        at += a.shape[1]
    return np.ascontiguousarray(np.concatenate([np.asarray(a, np.float32) for a in parts.values()], 1)).astype(dtype), where


def constants():
    return packed(f32_constants(), np.float32), packed(bf16_constants(), mybir.dt.np(BF16))


class Lane:

    def __init__(self, sem):
        self.sem, self.count, self.todo, self.passed = sem, 0, [], {}

    def do(self, make, *waits):
        self.wait(*waits)
        self.count += 1
        self.todo.append(lambda e: make(e).then_inc(self.sem, 1))
        return (self.sem, self.count)

    def go(self, make, *waits):
        self.wait(*waits)
        self.todo.append(make)

    def wait(self, *waits):
        for w in waits:
            if w is None:
                continue
            if isinstance(w, list):
                self.wait(*w)
                continue
            sem, value = w
            if self.passed.get(id(sem), 0) < value:
                self.passed[id(sem)] = value
                self.todo.append(lambda e, sem=sem, value=value: e.wait_ge(sem, value))

    def last(self):
        return (self.sem, self.count) if self.count else None

    def play(self, e):
        for make in self.todo:
            make(e)


class Arrivals:

    def __init__(self, sem):
        self.sem, self.count = sem, 0

    def dma(self, lane, make, *waits):
        lane.wait(*waits)
        self.count += 16
        lane.todo.append(lambda e: make(e).then_inc(self.sem, 16))
        return (self.sem, self.count)


def bc(ap, n):
    return ap.unsqueeze(2).broadcast_to([ap.shape[0], ap.shape[1], n])


def bm(ap, m):
    return ap.unsqueeze(1).broadcast_to([ap.shape[0], m, ap.shape[1]])


def split(ap, m):
    return ap.rearrange("p (m n) -> p m n", m=m)


def tiles_of(ap):
    return ap.rearrange("(t p) d -> p t d", p=P)


def run(steps):
    last = None
    for last in steps:
        pass
    return last


def interleave(chains, lag):
    chains = list(chains)
    for step in range(10 ** 6):
        going = [c for i, c in enumerate(chains) if step >= i * lag and c is not None]
        if not going and step >= lag * len(chains):
            return
        for i, c in enumerate(chains):
            if c is not None and step >= i * lag and next(c, run) is run:
                chains[i] = None


class Core:
    pass


def start(nc, ctx, A, out, where32, where16):
    core = Core()
    core.nc, core.ctx, core.A, core.out = nc, ctx, A, out
    core.where32, core.where16 = where32, where16
    core.pe, core.act, core.dve, core.pool, core.sp = (
        Lane(semaphore(core, "done_" + n)) for n in ("pe", "act", "dve", "pool", "sp"))
    core.arrivals = {}
    memory(core)
    return core


def semaphore(core, name):
    return core.ctx.enter_context(core.nc.semaphore(name))


def arrival(core, name):
    if name not in core.arrivals:
        core.arrivals[name] = Arrivals(semaphore(core, "moved_" + name))
    return core.arrivals[name]


def move(core, lane, name, to, of, *waits):
    return arrival(core, name).dma(lane, lambda e: e.dma_start(to, of), *waits)


def gather(core, name, to, of, index, *waits):
    at = bass.IndirectOffsetOnAxis(index, 0)
    return arrival(core, name).dma(core.pool, lambda e: e.indirect_dma_start(to, None, of, at), *waits)


def scatter(core, name, to, index, of, *waits):
    at = bass.IndirectOffsetOnAxis(index, 0)
    return arrival(core, name).dma(core.pool, lambda e: e.indirect_dma_start(to, at, of, None), *waits)


def memory(core):
    nc = core.nc
    base = -(-nc.sbuf_base // 64) * 64
    end = nc.sbuf_usable_end
    core.ctx.enter_context(nc.sbuf_tensor("arena", [P, (nc.sbuf_bytes_remaining - 128) // 4], F32))
    size_of = {F32: 4, F32R: 4, BF16: 2, I32: 4, U8: 1}
    top = [base]

    def put(name, shape, dt=F32, at=top):
        tensor = nc.alloc_sbuf_tensor_at(name, shape, dt, offset=at[0])
        at[0] += -(-int(np.prod(shape[1:])) * size_of[dt] // 32) * 32
        return tensor

    core.cst = put("cst", [P, sum(n for _, n in core.where32.values())])
    core.csb = put("csb", [P, sum(n for _, n in core.where16.values())], BF16)
    core.x_tok = put("x_tok", [P, NT, P])
    core.mix = put("mix", [P, NT, P])
    core.xT = put("xT", [P, NTOK])
    core.small = put("small", [P, 1500])
    core.ints = put("ints", [P, 4 * G1 + 4 * NT + GF + 2 * G3 + 16], I32)
    core.hotb1 = put("hotb1", [P, E], BF16)
    core.hotb3 = put("hotb3", [P, E], BF16)
    core.at1 = put("at1", [P, SPT * G1], BF16)
    core.at3 = put("at3", [P, SPT * G3], BF16)
    core.rows = put("rows", [P, 4, P])
    core.rowsT = put("rowsT", [P, 2, P])
    core.gated = put("gated", [P, 2, I1])
    core.hid = put("hid", [P, 2, I1])
    core.hidT = put("hidT", [P, 2, I1])
    core.result = put("result", [P, 3, P])
    feed = top[0]
    core.w1f = put("w1f", [P, (EF + 1) * W1F])
    core.late = -(-(top[0] + (E + 1) * W1C * 4 - end) // (W1F * 4))
    mixture = top[0] - core.late * W1F * 4
    top = [mixture]
    core.w1c = put("w1c", [P, (E + 1) * W1C], at=top)
    assert top[0] <= end and core.late > 0

    at = [feed]
    core.cw = put("cw", [P, P // 4 * P], at=at)
    core.cond4 = put("cond4", [P, NSEQ], at=at)
    core.maskT = put("maskT", [P, P], at=at)
    core.wbot = put("wbot", [P, NSEQ, P], at=at)
    core.l0b = put("l0b", [P, 1], at=at)
    core.lnsT = put("lnsT", [P, 2 * E], at=at)
    core.w10 = put("w10", [P, E * H0], at=at)
    core.w10s = put("w10s", [P, E * H0], at=at)
    core.w10b = put("w10b", [P, E * H0], at=at)
    core.b10 = put("b10", [P, 4], at=at)
    core.w20 = put("w20", [P, 2, P], at=at)
    core.wg0 = put("wg0", [P, E], at=at)
    core.b20 = put("b20", [E, 3 * P], at=at)
    core.b20p = put("b20p", [E, 3 * P], BF16, at=at)
    core.oh0 = put("oh0", [P, NT * E], BF16, at=at)
    core.ohT = put("ohT", [E, NTOK], BF16, at=at)
    core.h0 = put("h0", [P, 2, NTOK], at=at)
    core.yT = put("yT", [P, NTOK], at=at)
    assert at[0] <= mixture, (at[0], mixture)
    core.xhat = put("xhat", [P, NT, P], at=[feed])

    core.bhi = put("bhi", [P, 2, 4 * CH], F32R, at=[mixture])
    core.blo = put("blo", [P, 2, 4 * CH], F32R, at=[mixture + 8 * CH * 4])
    at = [mixture + core.late * W1F * 4]
    core.w3c = put("w3c", [P, E * W3C], at=at)
    tokens = [at[0]]
    core.counts, core.running, core.compared = (
        put(name, [P, NT * EF], at=tokens) for name in ("counts", "running", "compared"))
    core.hotF = put("hotF", [P, NT * EF], BF16, at=tokens)
    core.bias3 = put("bias3", [3, E * W3C], BF16, at=at)
    assert tokens[0] <= at[0]
    core.adaT = put("adaT", [P, P], at=at)
    core.wbT = put("wbT", [P, P], at=at)
    core.adbT = put("adbT", [P, P], at=at)
    core.bb2 = put("bb2", [P, P], at=at)
    core.lng2 = put("lng2", [P, 2], at=at)
    core.wraw = put("wraw", [P, P], at=at)
    core.wq = put("wq", [P, P], at=at)
    core.s3 = put("s3", [P, 3], at=at)
    assert at[0] <= end, (at[0], end)
    at = [feed]
    core.b3 = put("b3", [E, B3C], at=at)
    core.b3rest = put("b3rest", [E, 2 * B3C], at=at)
    core.b3p = put("b3p", [E, 3 * B3C], BF16, at=at)
    core.hsT = put("hsT", [P, 2, CH], at=at)
    core.z2 = put("z2", [P, 2, CH], at=at)
    core.kraw = put("kraw", [P, 2 * F3 + 4 * F3 + 4 * P], U8, at=at)
    core.kf = put("kf", [P, 2 * F3], at=at)
    core.w3a = put("w3a", [P, F3], F32R, at=at)
    core.w3b = put("w3b", [P, 4 * F3], F32R, at=at)
    core.w3d = put("w3d", [P, 4 * P], F32R, at=at)
    core.uhi = put("uhi", [P, 2, CH], F32R, at=at)
    core.ulo = put("ulo", [P, 2, CH], F32R, at=at)
    core.hf = put("hf", [P, 2, CH], at=at)
    core.ahi = put("ahi", [P, 2, 4 * CH], F32R, at=at)
    core.alo = put("alo", [P, 2, 4 * CH], F32R, at=at)
    assert at[0] <= mixture, (at[0], mixture)
    core.bank = [core.ctx.enter_context(nc.psum_tensor(f"bank{i}", [P, CH], F32)) for i in range(8)]
    core.freed = [None] * 8
    core.small_at = core.ints_at = 0
    core.rows_free, core.rowsT_free, core.result_sent = [None] * 4, [None] * 2, [None] * 3
    core.gated_free, core.hid_free, core.hidT_free = [None] * 2, [None] * 2, [None] * 2

    def dram(name, n):
        return nc.dram_tensor(name, [n, P], F32).ap()

    core.x1_rows = dram("x1_rows", NTOK)
    core.mix1_rows = dram("mix1_rows", SPILL1 + P * G1)
    core.sorted_rows = dram("sorted_rows", P * GF)
    core.ffn1_rows = dram("ffn1_rows", P * GF)
    core.x3_rows = dram("x3_rows", NTOK)
    core.mix3_rows = dram("mix3_rows", P * G3)


def c32(core, name, rows=P):
    at, n = core.where32[name]
    return core.cst[0:rows, at:at + n]


def c16(core, name, rows=P):
    at, n = core.where16[name]
    return core.csb[0:rows, at:at + n]


def some(core, n):
    core.small_at += n
    assert core.small_at <= core.small.shape[1], core.small_at
    return core.small[:, core.small_at - n:core.small_at]


def some_ints(core, n):
    core.ints_at += n
    assert core.ints_at <= core.ints.shape[1], core.ints_at
    return core.ints[:, core.ints_at - n:core.ints_at]


def first_loads(core):
    A, sp, act = core.A, core.sp, core.act
    core.got_csb = move(core, act, "csb", core.csb[:, :], A["csb"])
    core.got_cond4 = [move(core, sp, f"cond4_{r}", core.cond4[32 * r:32 * r + E, :], A["condT"]) for r in range(4)]
    q = P // 4 * P
    core.got_cw = [move(core, act if r % 2 else sp, f"cw_{r}", core.cw[32 * r:32 * r + E, :],
                             A["cw"][:, r * q:(r + 1) * q]) for r in range(4)]
    core.got_mask = move(core, act, "maskT", core.maskT[:, :], A["maskT"])
    core.got_cst = move(core, sp, "cst", core.cst[:, :], A["cst"])
    core.cond2 = some(core, E)
    core.got_cond = [move(core, sp, "cond_a", core.cond2[0:NSEQ, :], A["cond"]),
                     move(core, sp, "cond_b", core.cond2[NSEQ:P, :], A["cond"])]
    core.got_xT = move(core, act, "xT", core.xT[:, :], A["xT"])
    core.got0 = [move(core, act, "l0", to, of) for to, of in (
        (core.l0b[:, :], A["l0b"]), (core.lnsT[:, :], A["lnsT"]), (core.w10[:, :], A["w10"]),
        (core.b10[:, 0:2], A["b10"]), (core.w20[:, :, :], A["w20"].rearrange("(c p) d -> p c d", p=P)),
        (core.wg0[:, :], A["wg0"]), (core.b20[:, 0:P], A["b20"]))][-1]
    core.condT, core.gate_w = some(core, NSEQ), some(core, EF)
    core.got_kept = [move(core, act, "kept", to, of) for to, of in (
        (core.condT[0:E, :], A["condT"]), (core.gate_w, A["gate_w"]))][-1]
    core.got_x = move(core, sp, "x_tok", core.x_tok[:, :, :], tiles_of(A["x"]))
    core.got_w1c = {}
    for e in range(E + 1):
        core.got_w1c[e] = move(core, sp, f"w1c_{e}", core.w1c[:, e * W1C:(e + 1) * W1C], A["w1c"][e])
    core.halves = some(core, NT)
    core.have_halves = core.pool.do(lambda e: e.memset(core.halves, -0.5))
    zero = core.pool.do(lambda e: e.memset(core.rows[:, 0, :], 0.0))
    core.zeroed = move(core, sp, "zeroed", tiles_of(core.sorted_rows), bm(core.rows[:, 0, :], GF), zero)
    core.rows_free[0] = core.zeroed


def first_max(core, logits, m, n, best, tmp, hot, *waits):
    dve, top = core.dve, some(core, m)
    s = dve.do(lambda e: e.tensor_reduce(best, logits, AX_X, ALU.max), *waits)
    yield
    s = dve.do(lambda e: e.tensor_tensor(tmp, logits, bc(best, n), ALU.is_ge), s)
    yield
    s = dve.do(lambda e: e.tensor_tensor(tmp, tmp, bm(c32(core, "rev")[:, 0:n], m), ALU.mult), s)
    yield
    s = dve.do(lambda e: e.tensor_reduce(top, tmp, AX_X, ALU.max), s)
    yield
    yield dve.do(lambda e: e.tensor_tensor(hot, tmp, bc(top, n), ALU.is_equal), s)


def mean_rstd(core, stats, n, eps, *waits):
    dve = core.dve
    v = stats.rearrange("p (j k) -> p k j", k=6)
    total, apart, var, rstd, minus = (some(core, n) for _ in range(5))
    a = dve.do(lambda e: e.tensor_tensor(total, v[:, 1, :], v[:, 4, :], ALU.add), *waits)
    b = dve.do(lambda e: e.tensor_tensor(apart, v[:, 1, :], v[:, 4, :], ALU.subtract))
    c = dve.do(lambda e: e.tensor_tensor(var, v[:, 2, :], v[:, 5, :], ALU.add))
    a = dve.do(lambda e: e.tensor_scalar(minus, total, -0.5, None, ALU.mult), a)
    b = dve.do(lambda e: e.tensor_tensor(apart, apart, apart, ALU.mult), b)
    c = dve.do(lambda e: e.tensor_scalar(var, var, 1.0 / P, eps, ALU.mult, ALU.add), c)
    c = dve.do(lambda e: e.scalar_tensor_tensor(var, apart, 0.25, var, ALU.mult, ALU.add), b, c)
    c = core.pool.do(lambda e: e.tensor_tensor(rstd, var, core.halves[:, 0:n], ALU.pow), c, core.have_halves)
    return [a, c], minus, rstd


def bf16_parts(core, x, parts, rest, *waits):
    dve, n = core.dve, x.shape[-1]
    s = dve.do(lambda e: e.tensor_copy(parts[:, 0:n], x), *waits)
    s = dve.do(lambda e: e.tensor_tensor(rest[:, 0:n], x, parts[:, 0:n], ALU.subtract), s)
    s = dve.do(lambda e: e.tensor_copy(parts[:, n:2 * n], rest[:, 0:n]), s)
    s = dve.do(lambda e: e.tensor_tensor(rest[:, n:2 * n], rest[:, 0:n], parts[:, n:2 * n], ALU.subtract), s)
    return dve.do(lambda e: e.tensor_copy(parts[:, 2 * n:3 * n], rest[:, n:2 * n]), s)


def products(core, make, n, *waits):
    core.pe.wait(*waits)
    for i in range(n - 1):
        core.pe.go(lambda e, i=i: make(e, i))
    return core.pe.do(lambda e: make(e, n - 1))


def transposes(core, k, of, *waits):
    return products(core, lambda e, t: e.transpose(core.bank[k][:, t * P:(t + 1) * P], of(t), c32(core, "ident")),
                    TPC, *waits)


def choose(core):
    dve, act = core.dve, core.act
    cond = core.cond2
    best1, hot1, tmp = some(core, 1), some(core, E), some(core, E)
    h1 = run(first_max(core, bm(cond, 1), 1, E, best1, bm(tmp, 1), bm(hot1, 1), core.got_cond, core.got_cst))
    left, best2, hot2 = some(core, E), some(core, 1), some(core, E)
    s = dve.do(lambda e: e.tensor_scalar(left, hot1, -3.0e38, None, ALU.mult), h1)
    s = dve.do(lambda e: e.tensor_tensor(left, left, cond, ALU.add), s)
    h2 = run(first_max(core, bm(left, 1), 1, E, best2, bm(tmp, 1), bm(hot2, 1), s))
    minus, ex, total, rw = some(core, 1), some(core, E), some(core, 1), some(core, E)
    s = dve.do(lambda e: e.tensor_scalar(minus, best1, -1.0, None, ALU.mult))
    s = act.do(lambda e: e.activation(ex, cond, ACT.Exp, bias=minus, scale=1.0), s, core.got_cond)
    s = dve.do(lambda e: e.tensor_reduce(total, ex, AX_X, ALU.add), s)
    s = dve.do(lambda e: e.reciprocal(total, total), s)
    s = dve.do(lambda e: e.tensor_scalar(rw, ex, total, None, ALU.mult), s)
    t1, t2, w, scaled = some(core, E), some(core, E), some(core, 2), some(core, 2)
    a = dve.do(lambda e: e.tensor_tensor(t1, rw, hot1, ALU.mult), s)
    b = dve.do(lambda e: e.tensor_tensor(t2, rw, hot2, ALU.mult), h2)
    a = dve.do(lambda e: e.tensor_reduce(w[:, 0:1], t1, AX_X, ALU.add), a)
    b = dve.do(lambda e: e.tensor_reduce(w[:, 1:2], t2, AX_X, ALU.add), b)
    both = some(core, 1)
    s = dve.do(lambda e: e.tensor_tensor(both, w[:, 0:1], w[:, 1:2], ALU.add), a, b)
    s = dve.do(lambda e: e.reciprocal(both, both), s)
    s = dve.do(lambda e: e.tensor_scalar(w, w, both, None, ALU.mult), s)
    s = dve.do(lambda e: e.tensor_scalar(scaled, w, 1.0 / 12, None, ALU.mult), s)
    s = dve.do(lambda e: e.scalar_tensor_tensor(w, w, 1.0 - 1.0 / 12, scaled, ALU.mult, ALU.add), s)
    core.wpair, core.hpair, core.hfirst = some(core, 1), some(core, E), some(core, E)
    first, second = c32(core, "first"), c32(core, "second")
    s = dve.do(lambda e: e.tensor_scalar(core.wpair, w[:, 1:2], second, None, ALU.mult), s)
    s = dve.do(lambda e: e.scalar_tensor_tensor(core.wpair, w[:, 0:1], first, core.wpair, ALU.mult, ALU.add), s)
    s = dve.do(lambda e: e.tensor_scalar(core.hpair, hot2, second, None, ALU.mult))
    s = dve.do(lambda e: e.scalar_tensor_tensor(core.hpair, hot1, first, core.hpair, ALU.mult, ALU.add), s)
    core.have_pairs = dve.do(lambda e: e.tensor_scalar(core.hfirst, hot1, first, None, ALU.mult))


def route(core, hot, hotb, at, groups, columns, weights, absent):
    dve = core.dve
    b, k = core.bank[7], 7
    s = dve.do(lambda e: e.tensor_copy(hotb[:, :], hot), core.have_pairs)
    m = products(core, lambda e, i: e.matmul(b[:, i * E:(i + 1) * E], c16(core, ("before", "ones")[i]), hotb[:, :],
                                              start=True, stop=True), 2, s, core.got_csb, core.freed[k])
    n = core.where32["steps_seq"][1]
    below = core.hidT[:, 0, 0:E * n]
    ngroups, upto, place = some(core, E), some(core, E), some(core, 1)
    start, pos = some(core, E), some(core, E)
    s = dve.do(lambda e: e.tensor_tensor(split(below, E), bc(b[:, E:2 * E], n), bm(c32(core, "steps_seq"), E), ALU.is_gt), m)
    s = dve.do(lambda e: e.tensor_reduce(ngroups, split(below, E), AX_X, ALU.add), s)
    s = dve.do(lambda e: e.tensor_tensor_scan(upto, c32(core, "ones")[:, 0:E], ngroups, 0.0, ALU.mult, ALU.add), s)
    s = dve.do(lambda e: e.tensor_tensor(start, upto, ngroups, ALU.subtract), s)
    s = dve.do(lambda e: e.scalar_tensor_tensor(pos, start, float(SPT), b[:, 0:E], ALU.mult, ALU.add), s)
    s = dve.do(lambda e: e.tensor_tensor(pos, pos, hot, ALU.mult), s)
    s = dve.do(lambda e: e.tensor_reduce(place, pos, AX_X, ALU.add), s)
    if absent:
        s = dve.do(lambda e: e.tensor_tensor(place, place, c32(core, "absent"), ALU.add), s)
    have_place = s
    s = dve.do(lambda e: e.tensor_scalar(at[:, :], c32(core, "place")[:, 0:SPT * groups], place, None, ALU.is_equal), s)
    at4 = at[:, :].rearrange("p (g r) -> p r g", r=SPT)
    m = products(core, lambda e, i: e.matmul(
        b[:, 64 * (i // SPT):64 * (i // SPT) + groups],
        c16(core, ("pair", "quad")[i // SPT])[:, i % SPT * P:(i % SPT + 1) * P], at4[:, i % SPT, :],
        start=i % SPT == 0, stop=i % SPT == SPT - 1), 2 * SPT, s, core.freed[k])
    pair, filled, high = some(core, groups), some(core, groups), some(core, groups)
    src, first = some_ints(core, groups), some_ints(core, groups)
    s = dve.do(lambda e: e.tensor_copy(pair, b[:, 0:groups]), m)
    f = core.freed[k] = dve.do(lambda e: e.tensor_copy(filled, b[:, 64:64 + groups]))
    s = dve.do(lambda e: e.tensor_scalar(high, pair, float(NSEQ), -float(NSEQ), ALU.is_ge, ALU.mult), s)
    s = dve.do(lambda e: e.tensor_tensor(high, high, pair, ALU.add), s)
    have_src = dve.do(lambda e: e.tensor_scalar(src, high, float(SEQ), c32(core, "within"), ALU.mult, ALU.add), s)
    dst = scale = have_dst = None
    if weights is not None:
        dst, scale = some_ints(core, groups), some(core, groups)
        spill = c32(core, "spill")
        s = dve.do(lambda e: e.tensor_scalar(pair, pair, float(SEQ), c32(core, "within"), ALU.mult, ALU.add), have_src)
        s = dve.do(lambda e: e.tensor_tensor(pair, pair, spill, ALU.subtract), s)
        s = dve.do(lambda e: e.tensor_tensor(pair, pair, filled, ALU.mult), s, f)
        have_dst = dve.do(lambda e: e.tensor_tensor(dst, pair, spill, ALU.add), s)
        wquad, atf = core.hid[:, 0, :], core.hid[:, 1, 0:SPT * groups]
        dve.do(lambda e: e.tensor_scalar(wquad, c32(core, "quad"), weights, None, ALU.mult))
        s = dve.do(lambda e: e.tensor_copy(atf, at[:, :]))
        f4 = atf.rearrange("p (g r) -> p r g", r=SPT)
        m = products(core, lambda e, r: e.matmul(b[:, 0:groups], wquad[:, r * P:(r + 1) * P], f4[:, r, :],
                                                  start=r == 0, stop=r == SPT - 1), SPT, s, core.freed[k])
        core.freed[k] = dve.do(lambda e: e.tensor_copy(scale, b[:, 0:groups]), m)
        have_dst = [have_dst, core.freed[k]]
    past, expert = core.hidT[:, 1, 0:groups * E], some(core, groups)
    s = dve.do(lambda e: e.tensor_tensor(split(past, groups), bm(upto, groups), bc(c32(core, "group")[:, 0:groups], E), ALU.is_le),
               have_place)
    s = dve.do(lambda e: e.tensor_reduce(expert, split(past, groups), AX_X, ALU.add), s)
    s = dve.do(lambda e: e.tensor_scalar(expert, expert, float(E - 1), float(columns), ALU.min, ALU.mult), s)
    s = dve.do(lambda e: e.tensor_copy(first, expert), s)
    return dict(src=src, dst=dst, scale=scale, first=first, place=place, have_src=have_src,
                have_dst=have_dst, have_first=s, have_place=have_place)


def route_mixtures(core):
    choose(core)
    core.route1 = route(core, core.hpair, core.hotb1, core.at1, G1, W1C, core.wpair, False)
    core.route3 = route(core, core.hfirst, core.hotb3, core.at3, G3, W3C, None, True)
    wplace = core.hid[:, 0, :]
    s = core.dve.do(lambda e: e.tensor_scalar(wplace, c32(core, "quad"), core.route3["place"], None, ALU.mult),
                    core.route3["have_place"], core.pe.last())
    m = products(core, lambda e, r: e.matmul(core.bank[7][:, 0:NT], wplace[:, r * P:(r + 1) * P],
                                              c32(core, "pick")[:, r * NT:(r + 1) * NT], start=r == 0, stop=r == SPT - 1),
                     SPT, s, core.freed[7])
    core.back3 = some_ints(core, NT)
    core.have_back3 = core.freed[7] = core.dve.do(lambda e: e.tensor_scalar(
        core.back3, core.bank[7][:, 0:NT], float(SEQ), c32(core, "within"), ALU.mult, ALU.add), m)


def sequence_maps(core):
    per = CH // NSEQ
    for i in range(P // 4 // per):
        banks = [4 * (i % 2) + r for r in range(4)]
        core.pe.wait(core.got_cw, core.got_cond4, *(core.freed[k] for k in banks))
        for j in range(per):
            for r in range(4):
                def product(e, r=r, o=i * per + j, j=j, k=banks[r]):
                    return e.matmul(core.bank[k][:, j * NSEQ:(j + 1) * NSEQ],
                                    core.cw[32 * r:32 * r + E, o * P:(o + 1) * P],
                                    core.cond4[32 * r:32 * r + E, :], start=True, stop=True)
                m = core.pe.do(product)
        for r in range(4):
            def masked(e, k=banks[r], o=r * (P // 4) + i * per):
                return e.tensor_tensor(core.wbot[:, :, o:o + per].rearrange("p s o -> p o s"),
                                       split(core.bank[k][:, :], per), bc(core.maskT[:, o:o + per], NSEQ), ALU.mult)
            core.freed[banks[r]] = core.dve.do(masked, m, core.got_mask)
    have_wbot = core.dve.last()
    core.have_yT = []
    for c in range(NC):
        def mapped(e, i, c=c):
            q = c * (CH // SEQ) + i
            return e.matmul(core.bank[c][:, i * SEQ:(i + 1) * SEQ], core.wbot[:, q, :],
                            core.xT[:, q * SEQ:(q + 1) * SEQ], start=True, stop=True)
        m = products(core, mapped, CH // SEQ, have_wbot, core.got_xT, core.freed[c])
        core.freed[c] = core.act.do(lambda e, c=c: e.activation(
            core.yT[:, c * CH:(c + 1) * CH], core.bank[c][:, :], ACT.Identity, bias=core.l0b[:, 0:1], scale=1.0), m, core.got0)
        core.have_yT.append(core.freed[c])
    core.xT_free = core.pe.last()


def layer0_ffn(core):
    pe, act, dve = core.pe, core.act, core.dve
    yT, bank = core.yT, core.bank
    a = dve.do(lambda e: e.tensor_tensor(split(core.w10s[:, :], E), split(core.w10[:, :], E), bc(core.lnsT[:, 0:E], H0), ALU.mult), core.got0)
    b = dve.do(lambda e: e.tensor_tensor(split(core.w10b[:, :], E), split(core.w10[:, :], E), bc(core.lnsT[:, E:2 * E], H0), ALU.mult))
    have_w10s = a
    m = products(core, lambda e, h: e.matmul(bank[6][:, h:h + 1], core.w10b[:, h * P:(h + 1) * P], c32(core, "ones")[:, 0:1],
                                              start=True, stop=True), 2, b, core.freed[6])
    have_b10 = core.freed[6] = dve.do(lambda e: e.tensor_tensor(core.b10[:, 2:4], core.b10[:, 0:2], bank[6][:, 0:2], ALU.add), m)
    have_b20 = bf16_parts(core, core.b20[:, 0:P], core.b20p, core.b20[:, P:3 * P], core.got0)
    stats = some(core, 6 * NT)
    have_lg = products(core, lambda e, j: e.matmul(bank[4][:, j * E:(j + 1) * E], yT[:, j * P:(j + 1) * P], core.wg0[:, :],
                                                    start=True, stop=True), NT, core.have_yT, core.got0, core.freed[4])
    for c in range(NC):
        m = transposes(core, c, lambda t, c=c: yT[:, (c * TPC + t) * P:(c * TPC + t + 1) * P], core.have_yT[c], core.freed[c])
        for t in range(TPC):
            j = c * TPC + t
            dve.do(lambda e, c=c, t=t, j=j: e.bn_stats(stats[:, 6 * j:6 * j + 6], bank[c][:, t * P:(t + 1) * P]), m)
    ok, minus, rstd = mean_rstd(core, stats, NT, 1e-5, dve.last())
    best = some(core, NT)
    hot = run(first_max(core, split(bank[4][:, 0:NT * E], NT), NT, E, best, split(core.gated[:, 0, 0:NT * E], NT),
                             split(core.oh0[:, :], NT), have_lg))
    core.freed[4] = hot
    have_xhat = []
    for c in range(NC):
        for t in range(TPC):
            j = c * TPC + t
            m = dve.do(lambda e, c=c, t=t, j=j: e.tensor_scalar(
                core.xhat[:, j, :], bank[c][:, t * P:(t + 1) * P], minus[:, j:j + 1], rstd[:, j:j + 1], ALU.add, ALU.mult), ok)
        core.freed[c] = m
        have_xhat.append(m)
    have_ohT, have_xT = [], []
    for c in range(NC):
        k = 4 + c % 2
        half = bank[k][0:E, 0:CH // 2].bitcast(BF16)
        m = products(core, lambda e, t, c=c, half=half: e.transpose(
            half[:, t * P:(t + 1) * P], core.oh0[:, (c * TPC + t) * E:(c * TPC + t + 1) * E], c16(core, "ident")), TPC, hot, core.freed[k])
        core.freed[k] = act.do(lambda e, c=c, half=half: e.activation(core.ohT[:, c * CH:(c + 1) * CH], half, ACT.Copy), m)
        have_ohT.append(core.freed[k])
    for c in range(NC):
        m = transposes(core, c, lambda t, c=c: core.xhat[:, c * TPC + t, :], have_xhat[c], core.freed[c])
        core.freed[c] = act.do(lambda e, c=c: e.activation(core.xT[:, c * CH:(c + 1) * CH], bank[c][:, :], ACT.Copy), m, core.xT_free)
        have_xT.append(core.freed[c])
    spread = core.where16["spread"][0]
    gated_free = [None, None]

    def hidden(c):
        cols = slice(c * CH, (c + 1) * CH)
        for h in range(2):
            k, k2, g = 2 * (c % 2) + h, 4 + h, h
            m = products(core, lambda e, i, h=h, k=k: e.matmul(bank[k][:, :], core.w10s[:, h * P:(h + 1) * P], core.xT[:, cols],
                                                                start=True, stop=True), 1, have_xT[c], have_w10s, core.freed[k])
            m2 = products(core, lambda e, i, h=h, k2=k2: e.matmul(
                bank[k2][:, :], core.csb[0:E, spread + h * P:spread + (h + 1) * P], core.ohT[:, cols],
                start=True, stop=True), 1, have_ohT[c], core.freed[k2])
            core.freed[k] = act.do(lambda e, h=h, k=k, g=g: e.activation(
                core.gated[:, g, :], bank[k][:, :], ACT.Gelu, bias=core.b10[:, 2 + h:3 + h], scale=1.0), m, have_b10, gated_free[g])
            core.freed[k2] = gated_free[g] = dve.do(lambda e, h=h, k2=k2, g=g: e.tensor_tensor(
                core.h0[:, h, cols], core.gated[:, g, :], bank[k2][:, :], ALU.mult), core.freed[k], m2)
        return dve.last()

    def output(c, have_h):
        def product(e, i, c=c):
            t, n = divmod(i, 5)
            j = c * TPC + t
            to = bank[6 + c % 2][:, t * P:(t + 1) * P]
            if n < 2:
                return e.matmul(to, core.h0[:, n, j * P:(j + 1) * P], core.w20[:, n, :], start=n == 0, stop=False)
            return e.matmul(to, core.ohT[:, j * P:(j + 1) * P], core.b20p[:, (n - 2) * P:(n - 1) * P], start=False, stop=n == 4)
        m = products(core, product, 5 * TPC, have_h, have_b20, core.freed[6 + c % 2])
        rows = core.x_tok[:, c * TPC:(c + 1) * TPC, :]
        s = core.freed[6 + c % 2] = dve.do(lambda e: e.tensor_tensor(rows, rows, split(bank[6 + c % 2][:, :], TPC), ALU.add), m, core.got_x)
        core.have_x1.append(s)
        core.kept_x1 = move(core, core.sp, "x1_rows", tiles_of(core.x1_rows)[:, c * TPC:(c + 1) * TPC, :], rows, s)

    core.have_x1 = []
    have_h = hidden(0)
    for c in range(NC):
        after = hidden(c + 1) if c + 1 < NC else None
        output(c, have_h)
        have_h = after
    core.layer0_done = [core.pe.last(), core.dve.last(), core.act.last()]
    core.xT_free = core.pe.last()


def experts(core, items, width, func, between=None, bias=None):
    pe, act, dve, bank, freed = core.pe, core.act, core.dve, core.bank, core.freed
    n = len(items)
    blocks = width // P
    state = [dict() for _ in items]
    gu_banks = [(0, 2), (1, 3)] if width == I1 else [(0, 0), (1, 1)]
    up_at = 0 if width == I1 else width
    rowsT_free, gated_free, hid_free, hidT_free = core.rowsT_free, core.gated_free, core.hid_free, core.hidT_free

    def turn(i):
        it, s = items[i], state[i]
        if "turned" in it:
            s["xT"], s["have_xT"] = it["turned"]
            return
        rows, have = it["rows"]
        m = products(core, lambda e, _: e.transpose(bank[6][:, 0:P], rows, c32(core, "ident")), 1, have, core.freed[6])
        if "slot" in it:
            core.rows_free[it["slot"]] = m
        s["xT"] = core.rowsT[:, i % 2, :]
        s["have_xT"] = freed[6] = dve.do(lambda e: e.tensor_copy(s["xT"], bank[6][:, 0:P]), m, rowsT_free[i % 2])

    def first_products(i):
        it, s = items[i], state[i]
        g, u = gu_banks[i % 2]
        reg = s["first"] = {}
        if not isinstance(it["first"], int):
            column, have = it["first"]
            pe.wait(have)
            pe.go(lambda e: reg.setdefault("v", e.value_load(column, min_val=0, max_val=it["most"])))
        else:
            reg["v"] = it["first"]
        pe.wait(it.get("have_w"), s["have_xT"], freed[g], freed[u])
        if width == I1:
            pe.go(lambda e: e.matmul(bank[g][:, :], s["xT"], it["w"][:, bass.ds(reg["v"], CH)], start=True, stop=True))
            s["gu"] = pe.do(lambda e: e.matmul(bank[u][:, :], s["xT"], it["w"][:, bass.ds(reg["v"] + CH, CH)], start=True, stop=True))
        else:
            if bias is not None:
                pe.go(lambda e: e.matmul(bank[g][:, :], c16(core, "ones")[0:3, :], bias[:, bass.ds(reg["v"], CH)], start=True, stop=False))
            s["gu"] = pe.do(lambda e: e.matmul(bank[g][:, :], s["xT"], it["w"][:, bass.ds(reg["v"], CH)], start=bias is None, stop=True))
        rowsT_free[i % 2] = s["gu"]
        a = act.do(lambda e: e.activation(core.gated[:, i % 2, 0:width], bank[g][:, 0:width], func), s["gu"], gated_free[i % 2])
        d = dve.do(lambda e: e.tensor_tensor(core.hid[:, i % 2, 0:width], core.gated[:, i % 2, 0:width],
                                             bank[u][:, up_at:up_at + width], ALU.mult), a, hid_free[i % 2])
        gated_free[i % 2] = freed[u] = s["have_hid"] = d
        if g != u:
            freed[g] = a

    def turn_hidden(i):
        s, k = state[i], 4 + i % 2
        m = products(core, lambda e, b: e.transpose(bank[k][:, b * P:(b + 1) * P], core.hid[:, i % 2, b * P:(b + 1) * P], c32(core, "ident")),
                         blocks, s["have_hid"], core.freed[k])
        hid_free[i % 2] = m
        s["have_hidT"] = freed[k] = act.do(lambda e: e.activation(core.hidT[:, i % 2, 0:width], bank[k][:, 0:width], ACT.Copy), m, hidT_free[i % 2])

    def second_products(i):
        it, s = items[i], state[i]
        v = s["first"]
        to = bank[7][:, 0:P]
        pe.wait(s["have_hidT"], freed[7])
        if bias is not None:
            pe.go(lambda e: e.matmul(to, c16(core, "ones")[0:3, :], bias[:, bass.ds(v["v"] + 2 * width, P)], start=True, stop=False))
        for b in range(blocks):
            s["y"] = pe.do(lambda e, b=b: e.matmul(to, core.hidT[:, i % 2, b * P:(b + 1) * P],
                                                   it["w"][:, bass.ds(v["v"] + 2 * width + b * P, P)],
                                                   start=b == 0 and bias is None, stop=b == blocks - 1))
        hidT_free[i % 2] = s["y"]
        freed[7] = it["sink"](to, s["y"])

    turn(0)
    for i in range(n + 2):
        if i + 1 < n:
            turn(i + 1)
        if i < n:
            first_products(i)
        if 0 <= i - 2 < n:
            second_products(i - 2)
        if 0 <= i - 1 < n:
            turn_hidden(i - 1)
        if between is not None:
            between(i)


def gathered(core, source, route, g, *waits):
    slot = g % 4
    have = gather(core, f"rows_{slot}", core.rows[:, slot, :], source, route["src"][:, g:g + 1],
                       route["have_src"], core.rows_free[slot], *waits)
    return core.rows[:, slot, :], have


def layer1_mixture(core):
    items, r = [], core.route1
    for j in range(NT):
        def keep(y, m, j=j):
            return core.dve.do(lambda e: e.tensor_copy(core.mix[:, j, :], y), m)
        items.append(dict(rows=(core.x_tok[:, j, :], core.have_x1[j // TPC]), first=0, w=core.w1c, have_w=core.got_w1c[0], sink=keep))
    for g in range(G1):
        def send(y, m, g=g):
            slot = g % 3
            s = core.dve.do(lambda e: e.tensor_scalar(core.result[:, slot, :], y, r["scale"][:, g:g + 1], None, ALU.mult),
                            m, core.result_sent[slot], r["have_dst"])
            core.result_sent[slot] = scatter(core, f"scattered_{slot}", core.mix1_rows, r["dst"][:, g:g + 1], core.result[:, slot, :], s)
            return s
        items.append(dict(first=(r["first"][0:1, g:g + 1], r["have_first"]), most=(E - 1) * W1C, w=core.w1c[:, W1C:],
                          have_w=[core.got_w1c[e] for e in range(1, E + 1)], sink=send, slot=g % 4))

    def fetch(g):
        if g < G1:
            items[NT + g]["rows"] = gathered(core, core.x1_rows, r, g, core.kept_x1)

    core.got_w1f = []

    def between(i):
        if i >= NT:
            fetch(i - NT + 4)
        if i < EF + 1 - core.late:
            core.got_w1f.append(move(core, core.sp, f"w1f_{i % 4}", core.w1f[:, i * W1F:(i + 1) * W1F], core.A["w1f"][i], core.layer0_done))
    for g in range(4):
        fetch(g)
    experts(core, items, I1, ACT.Gelu_apprx_tanh, between=between)
    core.mixture1_sent = list(core.result_sent)


def layer1_weights(core):
    A, done = core.A, core.pe.last()
    for i in range(EF + 1 - core.late, EF + 1):
        core.got_w1f.append(move(core, core.act, "late", core.w1f[:, i * W1F:(i + 1) * W1F], A["w1f"][i], done))
    core.got2 = [move(core, core.sp, "w2", to, of, done) for to, of in (
        (core.adaT[:, :], A["adaT"]), (core.wbT[:, :], A["wbT"]), (core.adbT[:, :], A["adbT"]),
        (core.bb2[:, :], A["bb2"].partition_broadcast(P)), (core.lng2[:, :], A["lng2"]), (core.wraw[:, :], A["wraw"]))][-1]
    core.got_s3 = [move(core, core.sp, "s3", core.s3[:, i:i + 1], A[f"s{i}"].partition_broadcast(P), done) for i in range(3)][-1]
    for i in range(E):
        core.got_w3c = move(core, core.sp, "w3c", core.w3c[:, i * W3C:(i + 1) * W3C], A["w3c"][i], done)


def layer1_sum(core):
    core.have_mixT = []
    ring = [core.gated, core.hid]
    done = [core.pe.last(), core.dve.last(), core.act.last()]
    chosen_free = [done, done]
    for c in range(NC):
        got = []
        for k in range(2):
            rows = core.mix1_rows[k * NTOK + c * CH:k * NTOK + (c + 1) * CH]
            got.append(move(core, (core.sp, core.act)[k], f"chosen_{k}_{c % 2}", split(ring[k][:, c % 2, :], TPC), tiles_of(rows),
                                 chosen_free[c % 2], core.mixture1_sent))
        part = core.mix[:, c * TPC:(c + 1) * TPC, :]
        s = core.dve.do(lambda e, c=c, part=part: e.tensor_tensor(part, part, split(ring[0][:, c % 2, :], TPC), ALU.add), got[0])
        s = core.dve.do(lambda e, c=c, part=part: e.tensor_tensor(part, part, split(ring[1][:, c % 2, :], TPC), ALU.add), got[1], s)
        chosen_free[c % 2] = s
        m = transposes(core, 4 + c % 2, lambda t, c=c: core.mix[:, c * TPC + t, :], s, core.freed[4 + c % 2])
        core.freed[4 + c % 2] = core.act.do(lambda e, c=c: e.activation(core.xT[:, c * CH:(c + 1) * CH], core.bank[4 + c % 2][:, :], ACT.Copy), m, core.xT_free)
        core.have_mixT.append(core.freed[4 + c % 2])
    core.mixture_done = done
    core.mix_turned = core.pe.last()


def route_tokens(core):
    dve, bank = core.dve, core.bank
    wide = NT * EF
    have_lg = products(core, lambda e, j: e.matmul(bank[3][:, j * EF:(j + 1) * EF], core.xT[:, j * P:(j + 1) * P], core.gate_w,
                                                    start=True, stop=True), NT, core.have_mixT, core.got_kept, core.freed[3])
    best, score = some(core, NT), some(core, NT)
    tmp, hotb = core.compared, core.hotF
    yield
    steps = first_max(core, split(bank[3][:, :], NT), NT, EF, best, split(tmp[:, :], NT), split(hotb[:, :], NT), have_lg, core.mixture_done)
    for hot in steps:
        yield
    core.freed[3] = hot
    s = core.act.do(lambda e: e.activation(score, best, ACT.Sigmoid), hot)
    before = products(core, lambda e, i: e.matmul(bank[3][:, :], c16(core, "before"), hotb[:, :], start=True, stop=True), 1, hot, core.freed[3])
    total = products(core, lambda e, i: e.matmul(bank[2][:, :], c16(core, "ones"), hotb[:, :], start=True, stop=True), 1, core.freed[2])
    for c in range(NC):
        part = core.mix[:, c * TPC:(c + 1) * TPC, :]
        have_rows = dve.do(lambda e, c=c, part=part: e.tensor_tensor(part, part, bc(score[:, c * TPC:(c + 1) * TPC], P), ALU.mult), s, core.mix_turned)
        yield
    tot, cum = core.counts, core.running
    s = dve.do(lambda e: e.tensor_copy(split(tot[:, :], EF).rearrange("p e j -> p j e"), split(bank[2][:, :], NT)), total)
    core.freed[2] = s
    yield
    s = dve.do(lambda e: e.tensor_tensor_scan(cum[:, :], c32(core, "inner"), tot[:, :], 0.0, ALU.mult, ALU.add), s)
    yield
    counts = split(cum[:, :], EF)[:, :, NT - 1]
    n = core.where32["steps_tile"][1]
    ngroups, upto, start = some(core, EF), some(core, EF), some(core, EF)
    a = dve.do(lambda e: e.tensor_tensor(split(tmp[:, :], EF), bc(counts, n), bm(c32(core, "steps_tile"), EF), ALU.is_gt), s)
    b = dve.do(lambda e: e.tensor_tensor(tot[:, :], cum[:, :], tot[:, :], ALU.subtract), s)
    yield
    a = dve.do(lambda e: e.tensor_reduce(ngroups, split(tmp[:, :], EF), AX_X, ALU.add), a)
    a = dve.do(lambda e: e.tensor_tensor_scan(upto, c32(core, "ones")[:, 0:EF], ngroups, 0.0, ALU.mult, ALU.add), a)
    a = dve.do(lambda e: e.tensor_tensor(start, upto, ngroups, ALU.subtract), a)
    yield
    a = dve.do(lambda e: e.scalar_tensor_tensor(split(tot[:, :], EF), bc(start, NT), float(P), split(tot[:, :], EF), ALU.mult, ALU.add), a, b)
    yield
    a = dve.do(lambda e: e.tensor_tensor(split(cum[:, :], NT), split(tot[:, :], EF).rearrange("p e j -> p j e"), split(bank[3][:, :], NT), ALU.add), a, before)
    core.freed[3] = a
    yield
    a = dve.do(lambda e: e.tensor_tensor(cum[:, :], cum[:, :], hotb[:, :], ALU.mult), a)
    place, core.placeF = some(core, NT), some_ints(core, NT)
    a = dve.do(lambda e: e.tensor_reduce(place, split(cum[:, :], NT), AX_X, ALU.add), a)
    a = core.have_placeF = dve.do(lambda e: e.tensor_copy(core.placeF, place), a)
    for j in range(NT):
        core.sorted = scatter(core, f"sort_{j % 4}", core.sorted_rows, core.placeF[:, j:j + 1], core.mix[:, j, :], a, have_rows, core.zeroed)
        core.sorts[j % 4] = core.sorted
    yield
    core.firstF = some_ints(core, GF)
    expert = some(core, GF)
    at = 0
    while at < GF:
        m = min(NT, GF - at)
        past = tmp[:, 0:m * EF]
        a = dve.do(lambda e, at=at, m=m, past=past: e.tensor_tensor(
            split(past, m), bm(upto, m), bc(c32(core, "group")[:, at:at + m], EF), ALU.is_le), a)
        a = dve.do(lambda e, at=at, m=m, past=past: e.tensor_reduce(expert[:, at:at + m], split(past, m), AX_X, ALU.add), a)
        at += m
        yield
    a = dve.do(lambda e: e.tensor_scalar(expert, expert, float(EF - 1), float(W1F), ALU.min, ALU.mult), a)
    core.have_firstF = dve.do(lambda e: e.tensor_copy(core.firstF, expert), a)


def layer1_ffn(core):
    dve = core.dve
    routing = route_tokens(core)
    core.sorts = [None] * 4
    next(routing)
    items = []
    for j in range(NT):
        def add(y, m, j=j):
            return dve.do(lambda e: e.tensor_tensor(core.x_tok[:, j, :], core.x_tok[:, j, :], y, ALU.add), m, core.kept_x1)
        items.append(dict(turned=(core.xT[:, j * P:(j + 1) * P], core.have_mixT[j // TPC]), first=0, w=core.w1f, have_w=core.got_w1f, sink=add))
    experts(core, items, IF, ACT.Silu, between=lambda i: [next(routing, None) for _ in range(2)])
    run(routing)
    core.xT_free = core.pe.last()
    items = []
    for g in range(GF):
        def send(y, m, g=g):
            slot = g % 3
            s = dve.do(lambda e: e.tensor_copy(core.result[:, slot, :], y), m, core.result_sent[slot])
            core.result_sent[slot] = move(core, core.sp, f"sent_{slot}", core.ffn1_rows[g * P:(g + 1) * P], core.result[:, slot, :], s)
            return s
        items.append(dict(first=(core.firstF[0:1, g:g + 1], core.have_firstF), most=(EF - 1) * W1F, w=core.w1f[:, W1F:],
                          have_w=core.got_w1f, sink=send, slot=g % 4))

    def fetch(g):
        if g < GF:
            slot = g % 4
            have = move(core, core.sp, f"sorted_{slot}", core.rows[:, slot, :], core.sorted_rows[g * P:(g + 1) * P], core.sorts, core.rows_free[slot])
            items[g]["rows"] = (core.rows[:, slot, :], have)
    for g in range(4):
        fetch(g)
    experts(core, items, IF, ACT.Silu, between=lambda i: fetch(i + 4))
    core.ffn1_sent = list(core.result_sent)


def layer2(core):
    A, pe, act, dve, bank, freed = core.A, core.pe, core.act, core.dve, core.bank, core.freed
    done = [pe.last(), dve.last(), act.last()]
    core.got_k = [move(core, core.sp, "k", core.kraw[:, at:at + n], A[name], done) for name, at, n in (
        ("k0", 0, 2 * F3), ("k1", 2 * F3, 4 * F3), ("k2", 6 * F3, 4 * P))][-1]
    got_b3 = move(core, core.sp, "b3", core.b3[:, :], A["b3"], done)
    s = bf16_parts(core, core.b3[:, :], core.b3p, core.b3rest, got_b3)
    for part in range(3):
        for i in range(E):
            core.have_bias3 = move(core, core.sp, "bias3", core.bias3[part:part + 1, i * W3C:i * W3C + B3C],
                                        core.b3p[i:i + 1, part * B3C:(part + 1) * B3C], s, core.dve.last())
    wx, absw, beta, inv = some(core, NSEQ), some(core, 1), some(core, 1), some(core, 1)
    m = products(core, lambda e, i: e.matmul(bank[7][:, 0:NSEQ], c32(core, "rank_up", E), core.condT[0:E, :],
                                              start=True, stop=True), 1, core.got_kept, core.freed[7])
    s = freed[7] = dve.do(lambda e: e.tensor_scalar(wx, bank[7][:, 0:NSEQ], 2.0, None, ALU.mult), m)
    have_wx = s
    s = dve.do(lambda e: e.tensor_reduce(absw, core.wraw[:, :], AX_X, ALU.add, apply_absolute_value=True), core.got2)
    m = products(core, lambda e, i: e.matmul(bank[7][:, 0:1], c32(core, "ones"), absw, start=True, stop=True), 1, s, core.freed[7])
    have_beta = freed[7] = dve.do(lambda e: e.tensor_scalar(beta, bank[7][:, 0:1], 1.0 / (P * P), None, ALU.mult), m)
    s = dve.do(lambda e: e.tensor_scalar(inv, beta, 1e-5, None, ALU.add), have_beta)
    s = dve.do(lambda e: e.reciprocal(inv, inv), s)
    magic = 1.5 * 2.0 ** 23
    s = dve.do(lambda e: e.tensor_scalar(core.wq[:, :], core.wraw[:, :], inv, magic, ALU.mult, ALU.add), s)
    s = dve.do(lambda e: e.tensor_scalar(core.wq[:, :], core.wq[:, :], magic, -1.0, ALU.subtract, ALU.max), s)
    have_wq = dve.do(lambda e: e.tensor_scalar(core.wq[:, :], core.wq[:, :], 1.0, None, ALU.min), s)
    y = [core.gated, core.hid]
    peak = some(core, NC)
    y_free = [None] * 2
    core.have_x2 = []
    xnT = core.mix[:, :, :].rearrange("p a b -> p (a b)")
    have_xn = []
    stats = some(core, 6 * NT)
    z_free = [None] * 2
    hs_free = [None] * 2
    have_rows = [None] * NC

    def bring(c):
        have_rows[c] = [gather(core, f"back_{c * TPC + t}", y[c % 2][:, 0, t * P:(t + 1) * P], core.ffn1_rows,
                                    core.placeF[:, c * TPC + t:c * TPC + t + 1], core.ffn1_sent, done, y_free[c % 2], core.have_placeF)
                        for t in range(TPC)]

    def chunk(c):
        i = c % 2
        cols = slice(c * CH, (c + 1) * CH)
        rows = core.x_tok[:, c * TPC:(c + 1) * TPC, :]
        s = y_free[i] = dve.do(lambda e: e.tensor_tensor(rows, rows, split(y[i][:, 0, :], TPC), ALU.add), have_rows[c])
        if c + 2 < NC:
            bring(c + 2)
        m = transposes(core, i, lambda t: core.x_tok[:, c * TPC + t, :], s, core.freed[i])
        have_xT = freed[i] = act.do(lambda e: e.activation(core.xT[:, cols], bank[i][:, :], ACT.Copy), m, core.xT_free)
        yield
        m = products(core, lambda e, _: e.matmul(bank[2 + i][:, :], core.adaT[:, :], core.xT[:, cols], start=True, stop=True), 1, have_xT, core.got2, core.freed[2 + i])
        nseq = CH // SEQ
        have_hs = freed[2 + i] = dve.do(lambda e: e.tensor_tensor(
            split(core.hsT[:, i, :], nseq), split(bank[2 + i][:, :], nseq), bc(wx[:, c * nseq:(c + 1) * nseq], SEQ), ALU.mult),
            m, have_wx, hs_free[i])
        yield

        def product(e, n):
            t, n = divmod(n, 2)
            to = bank[4 + i][:, t * P:(t + 1) * P]
            if n == 0:
                return e.matmul(to, core.xT[:, (c * TPC + t) * P:(c * TPC + t + 1) * P], core.wbT[:, :], start=True, stop=False)
            return e.matmul(to, core.hsT[:, i, t * P:(t + 1) * P], core.adbT[:, :], start=False, stop=True)
        m = hs_free[i] = products(core, product, 2 * TPC, have_hs, core.freed[4 + i])
        z2 = core.z2[:, i, :]
        s = freed[4 + i] = dve.do(lambda e: e.tensor_tensor(
            split(z2, TPC), split(bank[4 + i][:, :], TPC), bm(core.bb2[:, :], TPC), ALU.add), m, z_free[i])
        for t in range(TPC):
            j = c * TPC + t
            dve.do(lambda e, t=t, j=j: e.bn_stats(stats[:, 6 * j:6 * j + 6], z2[:, t * P:(t + 1) * P]), s)
        ok, minus, rstd = mean_rstd(core, stats[:, 6 * c * TPC:6 * (c + 1) * TPC], TPC, 1e-3, dve.last())
        yield
        for t in range(TPC):
            tile = z2[:, t * P:(t + 1) * P]
            s = dve.do(lambda e, t=t, tile=tile: e.tensor_scalar(tile, tile, minus[:, t:t + 1], rstd[:, t:t + 1], ALU.add, ALU.mult), ok)
        m = z_free[i] = transposes(core, 6 + i, lambda t: z2[:, t * P:(t + 1) * P], s, core.freed[6 + i])
        s = freed[6 + i] = act.do(lambda e: e.activation(
            xnT[:, cols], bank[6 + i][:, :], ACT.Identity, bias=core.lng2[:, 1:2], scale=core.lng2[:, 0:1]), m, core.sorts)
        yield
        have_xn.append(dve.do(lambda e: e.tensor_reduce(peak[:, c:c + 1], xnT[:, cols], AX_X, ALU.max, apply_absolute_value=True), s))

    bring(0)
    bring(1)
    interleave([chunk(c) for c in range(NC)], lag=2)
    core.xT_free = pe.last()
    top, topr, gmax, ginv, back = some(core, 1), some(core, 1), some(core, 1), some(core, 1), some(core, 1)
    s = dve.do(lambda e: e.tensor_reduce(top, peak, AX_X, ALU.max), have_xn)
    m = products(core, lambda e, i: e.transpose(bank[6][0:1, 0:P], top, c32(core, "ident")), 1, s, core.freed[6])
    s = freed[6] = dve.do(lambda e: e.tensor_reduce(topr[0:1, :], bank[6][0:1, 0:P], AX_X, ALU.max), m)
    m = products(core, lambda e, i: e.matmul(bank[6][:, 0:1], c32(core, "ones")[0:1, :], topr[0:1, :], start=True, stop=True), 1, s, core.freed[6])
    s = freed[6] = dve.do(lambda e: e.tensor_copy(gmax, bank[6][:, 0:1]), m)
    a = dve.do(lambda e: e.reciprocal(ginv, gmax), s)
    b = dve.do(lambda e: e.scalar_tensor_tensor(back, gmax, 1.0 / 128.0, beta, ALU.mult, ALU.mult), s, have_beta)
    a = dve.do(lambda e: e.tensor_scalar(ginv, ginv, 128.0, None, ALU.mult), a)
    most = float(np.float32(128.0 - 1e-5))
    for c in range(NC):
        cols = slice(c * CH, (c + 1) * CH)
        s = dve.do(lambda e, cols=cols: e.tensor_scalar(xnT[:, cols], xnT[:, cols], ginv, most, ALU.mult, ALU.min), a, have_xn)
        s = dve.do(lambda e, cols=cols: e.tensor_scalar(xnT[:, cols], xnT[:, cols], -most, None, ALU.max), s)
        k = c % 2
        m = products(core, lambda e, t, c=c, k=k: e.matmul(
            bank[k][:, t * P:(t + 1) * P], xnT[:, (c * TPC + t) * P:(c * TPC + t + 1) * P], core.wq[:, :], start=True, stop=True), TPC, s, have_wq, core.freed[k])
        rows = core.x_tok[:, c * TPC:(c + 1) * TPC, :]
        s = freed[k] = dve.do(lambda e, k=k, rows=rows: e.scalar_tensor_tensor(rows, split(bank[k][:, :], TPC), back, rows, ALU.mult, ALU.add), m, b)
        core.have_x2.append(s)
        core.kept_x3 = move(core, core.sp, "x3_rows", tiles_of(core.x3_rows)[:, c * TPC:(c + 1) * TPC, :], rows, s)
    core.mix_free = pe.last()


def signs(core):
    dve, kf = core.dve, core.kf
    s = dve.do(lambda e: e.tensor_scalar(kf[:, :], core.kraw[:, 0:2 * F3], 2.0, None, ALU.mult), core.got_k)
    yield
    dve.do(lambda e: e.tensor_tensor(core.w3a[:, :], kf[:, 0:F3], kf[:, F3:2 * F3], ALU.subtract), s)
    yield
    for i in range(4):
        dve.do(lambda e, i=i: e.tensor_scalar(core.w3b[:, i * F3:(i + 1) * F3], core.kraw[:, (2 + i) * F3:(3 + i) * F3],
                                              2.0, -1.0, ALU.mult, ALU.add))
        yield
    dve.do(lambda e: e.tensor_scalar(core.w3d[:, :], core.kraw[:, 6 * F3:], 2.0, -1.0, ALU.mult, ALU.add))
    yield
    core.have_signs = dve.do(lambda e: e.tensor_scalar(core.s3[:, 1:3], core.s3[:, 1:3], 2.0, None, ALU.mult), core.got_s3)


def layer3_mixture(core):
    items, r = [], core.route3
    for g in range(G3):
        def send(y, m, g=g):
            slot = g % 3
            s = core.dve.do(lambda e: e.tensor_copy(core.result[:, slot, :], y), m, core.result_sent[slot])
            core.result_sent[slot] = move(core, core.sp, f"sent_{slot}", core.mix3_rows[g * P:(g + 1) * P], core.result[:, slot, :], s)
            return s
        items.append(dict(first=(r["first"][0:1, g:g + 1], r["have_first"]), most=(E - 1) * W3C, w=core.w3c,
                          have_w=[core.got_w3c, core.have_bias3], sink=send, slot=g % 4))

    def fetch(g):
        if g < G3:
            items[g]["rows"] = gathered(core, core.x3_rows, r, g, core.kept_x3)
    making = signs(core)

    def between(i):
        fetch(i + 4)
        next(making, None)
    for g in range(4):
        fetch(g)
    experts(core, items, I3, ACT.Silu, between=between, bias=core.bias3)
    run(making)
    core.mixture3_sent = list(core.result_sent)


def layer3_ffn(core):
    pe, act, dve, bank, freed = core.pe, core.act, core.dve, core.bank, core.freed
    u = core.mix
    got = [gather(core, f"back_{j}", u[:, j, :], core.mix3_rows, core.back3[:, j:j + 1], core.mixture3_sent, core.have_back3, core.mix_free) for j in range(NT)]
    hf_free, ahi_free = [None] * 2, [None] * 2
    count = [0]
    used = [0]

    def next_bank():
        used[0] += 1
        return used[0] % 6

    u_free = [None] * 2
    done = [pe.last(), dve.last(), act.last()]
    have_u = [None] * NC
    have_a = [[None] * 4 for _ in range(NC)]
    have_b = [[None] * 4 for _ in range(NC)]
    a_free, b_free = [None] * 2, [done] * 2
    bhi, blo = core.bhi, core.blo

    def halves_of(to_hi, to_lo, k, m, scale, *waits):
        i = count[0] % 2
        count[0] += 1
        h = act.do(lambda e: e.activation(to_hi, bank[k][:, :], ACT.Relu, scale=scale), m, *waits)
        f = act.do(lambda e: e.activation(core.hf[:, i, :], bank[k][:, :], ACT.Relu, scale=scale), hf_free[i])
        freed[k] = f
        hf_free[i] = dve.do(lambda e: e.tensor_tensor(to_lo, core.hf[:, i, :], to_hi.bitcast(F32), ALU.subtract), f, *waits)
        return hf_free[i]

    def input_(c):
        k = next_bank()
        m = transposes(core, k, lambda t: u[:, c * TPC + t, :], got[c * TPC:(c + 1) * TPC], core.freed[k])
        h = act.do(lambda e: e.activation(core.uhi[:, c % 2, :], bank[k][:, :], ACT.Copy), m, u_free[c % 2])
        have_u[c] = freed[k] = dve.do(lambda e: e.tensor_tensor(core.ulo[:, c % 2, :], bank[k][:, :], core.uhi[:, c % 2, :].bitcast(F32), ALU.subtract), h)

    def first(c):
        for f in range(4):
            k = next_bank()
            m = products(core, lambda e, i, f=f, k=k: e.matmul(
                bank[k][:, :], core.w3a[:, f * P:(f + 1) * P], (core.uhi, core.ulo)[i][:, c % 2, :], start=i == 0, stop=i == 1),
                2, have_u[c], core.have_signs, core.freed[k])
            at = slice(f * CH, (f + 1) * CH)
            have_a[c][f] = halves_of(core.ahi[:, c % 2, at], core.alo[:, c % 2, at], k, m, core.s3[:, 0:1], a_free[c % 2])
        u_free[c % 2] = pe.last()

    def second(c):
        for f in range(4):
            k = next_bank()

            def product(e, i, f=f, k=k):
                b, half = divmod(i, 2)
                return e.matmul(bank[k][:, :], core.w3b[:, b * F3 + f * P:b * F3 + (f + 1) * P],
                                (core.ahi, core.alo)[half][:, c % 2, b * CH:(b + 1) * CH], start=i == 0, stop=i == 7)
            m = products(core, product, 8, have_a[c], core.freed[k])
            at = slice(f * CH, (f + 1) * CH)
            have_b[c][f] = halves_of(bhi[:, c % 2, at], blo[:, c % 2, at], k, m, core.s3[:, 1:2], b_free[c % 2])
        a_free[c % 2] = pe.last()

    def third(c):
        k = 6 + c % 2

        def product(e, i):
            t, n = divmod(i, 8)
            b, half = divmod(n, 2)
            return e.matmul(bank[k][:, t * P:(t + 1) * P], (bhi, blo)[half][:, c % 2, b * CH + t * P:b * CH + (t + 1) * P],
                            core.w3d[:, b * P:(b + 1) * P], start=n == 0, stop=n == 7)
        m = b_free[c % 2] = products(core, product, 8 * TPC, have_b[c], core.freed[k])
        rows = core.x_tok[:, c * TPC:(c + 1) * TPC, :]
        s = freed[k] = dve.do(lambda e: e.scalar_tensor_tensor(rows, split(bank[k][:, :], TPC), core.s3[:, 2:3], rows, ALU.mult, ALU.add), m, core.kept_x3)
        core.stored = move(core, core.sp, "out", tiles_of(core.out)[:, c * TPC:(c + 1) * TPC, :], rows, s)

    input_(0)
    first(0)
    for c in range(NC):
        if c + 1 < NC:
            input_(c + 1)
            first(c + 1)
        if c:
            third(c - 1)
        second(c)
    third(NC - 1)
    core.sp.wait(core.stored)


def build(nc, A, out, where32, where16):
    with ExitStack() as ctx:
        core = start(nc, ctx, A, out, where32, where16)
        first_loads(core)
        sequence_maps(core)
        route_mixtures(core)
        layer0_ffn(core)
        layer1_mixture(core)
        layer1_weights(core)
        layer1_sum(core)
        layer1_ffn(core)
        layer2(core)
        layer3_mixture(core)
        layer3_ffn(core)
        with nc.Block() as block:
            block.sync(core.sp.play)
            block.scalar(core.act.play)
            block.vector(core.dve.play)
            block.gpsimd(core.pool.play)
            block.tensor(core.pe.play)


def laid_out(x):
    def get(n):
        return np.asarray(x[n])

    def side(blocks):
        a = blocks.reshape(*blocks.shape[:-2], -1, P, blocks.shape[-1])
        return np.moveaxis(a, -3, -2).reshape(*blocks.shape[:-2], P, -1)

    def turned(a):
        return np.swapaxes(a, -1, -2)

    (cst, where32), (csb, where16) = constants()
    tokens = get("x").reshape(NTOK, P)
    cond = get("cond_8")
    arrays = {
        "cst": cst, "csb": csb, "x": tokens, "xT": tokens.T, "cond": cond, "condT": cond.T,
        "cw": get("L0_cond_weight").reshape(E, P * P),
        "maskT": get("L0_cond_mask").T, "l0b": get("L0_cond_bias").reshape(P, 1),
        "lnsT": np.concatenate([get("L0_ffn_ln_scale").T, get("L0_ffn_ln_bias").T], 1),
        "w10": get("L0_ffn_W1").transpose(1, 0, 2).reshape(P, E * H0),
        "b10": get("L0_ffn_b1").reshape(2, P).T,
        "w20": get("L0_ffn_W2").reshape(E * H0, P),
        "wg0": get("L0_ffn_Wg").T, "b20": get("L0_ffn_b2"),
        "gate_w": get("L1_ffn_gate_w"),
        "adaT": get("L2_cond_As").reshape(E * R2, P).T, "wbT": get("L2_cond_W_base").T,
        "adbT": get("L2_cond_Bs").transpose(0, 2, 1).reshape(E * R2, P), "bb2": get("L2_cond_b_base"),
        "lng2": np.stack([get("L2_ffn_ln_gamma"), get("L2_ffn_ln_beta")], 1), "wraw": get("L2_ffn_weight"),
        "w1c": np.concatenate([np.concatenate([get("L1_cond_shared_" + n)[None], get("L1_cond_skill_" + n)])
                               if n != "down" else
                               side(np.concatenate([get("L1_cond_shared_down")[None], get("L1_cond_skill_down")]))
                               for n in ("gate", "up", "down")], 2),
        "w1f": np.concatenate([np.concatenate([get(f"L1_ffn_shared_{n}_w")[None], get(f"L1_ffn_routed_{n}_w")])
                               if n != "down" else
                               side(np.concatenate([get("L1_ffn_shared_down_w")[None], get("L1_ffn_routed_down_w")]))
                               for n in ("gate", "up", "down")], 2),
        "w3c": np.concatenate([turned(get("L3_cond_W_up")), turned(get("L3_cond_W_gate")),
                               side(turned(get("L3_cond_W_down")))], 2),
        "b3": np.concatenate([get("L3_cond_b_up"), get("L3_cond_b_gate"), get("L3_cond_b_down")], 1),
    }
    for i in range(3):
        arrays[f"k{i}"] = side(get(f"L3_ffn_k{i}"))
        arrays[f"s{i}"] = get(f"L3_ffn_s{i}").reshape(1)
    return {n: np.ascontiguousarray(a) for n, a in arrays.items()}, where32, where16


def kernel(**inputs):
    import concourse.bacc as bacc
    from concourse.bass_utils import run_bass_kernel_spmd

    arrays, where32, where16 = laid_out(inputs)
    nc = bacc.Bacc("TRN2", target_bir_lowering=False, num_devices=1)
    A = {n: nc.dram_tensor(f"in_{n}", a.shape, mybir.dt.from_np(a.dtype), kind="ExternalInput").ap()
         for n, a in arrays.items()}
    out = nc.dram_tensor("out_x", (NTOK, P), F32, kind="ExternalOutput").ap()
    build(nc, A, out, where32, where16)
    result = run_bass_kernel_spmd(nc, [{f"in_{n}": a for n, a in arrays.items()}], core_ids=[0]).results[0]["out_x"]
    return result.reshape(NSEQ, SEQ, P)
```

```python
from contextlib import ExitStack

import numpy as np

import concourse.bass as bass
from concourse import mybir

F32 = mybir.dt.float32
F32R = mybir.dt.float32r
BF16 = mybir.dt.bfloat16
I32 = mybir.dt.int32
U8 = mybir.dt.uint8
ALU = mybir.AluOpType
ACT = mybir.ActivationFunctionType
AX_X = mybir.AxisListType.X

P = 128
NSEQ, SEQ = 64, 32
NTOK = NSEQ * SEQ
NT = NTOK // P
SPT = P // SEQ
CH = 512
NC = NTOK // CH
TPC = CH // P
E = 8
H0 = 32
I1 = 512
EF, IF = 32, 256
I3 = 256
R2 = 16
F3 = 512


def worst_groups(rows, experts, size):
    return (rows + experts * (size - 1)) // size


G1 = worst_groups(2 * NSEQ, E, SPT)
GF = worst_groups(NTOK, EF, P)
G3 = worst_groups(NSEQ, E, SPT)
L0P = E * H0 + 2 * P + 3 * E + 3
W1C = 3 * I1
W1F = 3 * IF
W3C = 3 * I3
B3C = 2 * I3 + P
SPILL1 = 2 * NTOK


def f32_constants():
    p = np.arange(P)[:, None]
    q = np.arange(P)[None, :]
    return {
        "ident": (p == q),
        "ones": np.ones((P, P)),
        "quad": np.concatenate([(q // SEQ == r) & (p >= 0) for r in range(SPT)], 1),
        "pick": np.concatenate([(p == SPT * np.arange(NT)[None, :] + r) for r in range(SPT)], 1),
        "rank_up": np.repeat(np.arange(E)[None, :] == p, R2, 1),
        "place": np.tile(np.arange(SPT * G1)[None, :], (P, 1)),
        "group": np.tile(np.arange(max(G1, GF, G3))[None, :], (P, 1)),
        "steps_seq": np.tile(SPT * np.arange(NSEQ // SPT)[None, :], (P, 1)),
        "steps_tile": np.tile(P * np.arange(NT)[None, :], (P, 1)),
        "rev": np.tile(EF - np.arange(EF)[None, :], (P, 1)),
        "spill": SPILL1 + P * np.arange(G1)[None, :] + p,
        "within": p % SEQ,
        "first": p < NSEQ,
        "second": p >= NSEQ,
        "absent": -1000.0 * (p >= NSEQ),
        "inner": np.tile((np.arange(EF * NT)[None, :] % NT != 0), (P, 1)),
    }


def bf16_constants():
    p = np.arange(P)[:, None]
    q = np.arange(P)[None, :]
    return {
        "ident": (p == q),
        "before": (p < q),
        "ones": np.ones((P, P)),
        "quad": np.concatenate([(q // SEQ == r) & (p >= 0) for r in range(SPT)], 1),
        "pair": np.concatenate([p * (q // SEQ == r) for r in range(SPT)], 1),
        "spread": np.repeat(np.arange(E)[None, :] == p, H0, 1),
    }


def packed(parts, dtype):
    at, where = 0, {}
    for name, a in parts.items():
        where[name] = (at, a.shape[1])
        at += a.shape[1]
    return np.ascontiguousarray(np.concatenate([np.asarray(a, np.float32) for a in parts.values()], 1)).astype(dtype), where


def constants():
    return packed(f32_constants(), np.float32), packed(bf16_constants(), mybir.dt.np(BF16))


class Lane:

    def __init__(self, sem):
        self.sem, self.count, self.todo, self.passed = sem, 0, [], {}

    def do(self, make, *waits):
        self.wait(*waits)
        self.count += 1
        self.todo.append(lambda e: make(e).then_inc(self.sem, 1))
        return (self.sem, self.count)

    def go(self, make, *waits):
        self.wait(*waits)
        self.todo.append(make)

    def wait(self, *waits):
        for w in waits:
            if w is None:
                continue
            if isinstance(w, list):
                self.wait(*w)
                continue
            sem, value = w
            if self.passed.get(id(sem), 0) < value:
                self.passed[id(sem)] = value
                self.todo.append(lambda e, sem=sem, value=value: e.wait_ge(sem, value))

    def last(self):
        return (self.sem, self.count) if self.count else None

    def play(self, e):
        for make in self.todo:
            make(e)


class Arrivals:

    def __init__(self, sem):
        self.sem, self.count = sem, 0

    def dma(self, lane, make, *waits):
        lane.wait(*waits)
        self.count += 16
        lane.todo.append(lambda e: make(e).then_inc(self.sem, 16))
        return (self.sem, self.count)


def bc(ap, n):
    return ap.unsqueeze(2).broadcast_to([ap.shape[0], ap.shape[1], n])


def bm(ap, m):
    return ap.unsqueeze(1).broadcast_to([ap.shape[0], m, ap.shape[1]])


def split(ap, m):
    return ap.rearrange("p (m n) -> p m n", m=m)


def tiles_of(ap):
    return ap.rearrange("(t p) d -> p t d", p=P)


def run(steps):
    last = None
    for last in steps:
        pass
    return last


def last_of(steps):
    last = None
    for last in steps:
        yield
    return last


def interleave(chains, first):
    chains, now = list(zip(chains, first)), 0
    while chains:
        chains = [(c, at) for c, at in chains if now < at or next(c, run) is not run]
        now += 1


class Core:
    pass


def start(nc, ctx, A, out, where32, where16):
    core = Core()
    core.nc, core.ctx, core.A, core.out = nc, ctx, A, out
    core.where32, core.where16 = where32, where16
    core.pe, core.act, core.dve, core.pool, core.sp = (
        Lane(semaphore(core, "done_" + n)) for n in ("pe", "act", "dve", "pool", "sp"))
    core.arrivals = {}
    memory(core)
    return core


def semaphore(core, name):
    return core.ctx.enter_context(core.nc.semaphore(name))


def arrival(core, name):
    if name not in core.arrivals:
        core.arrivals[name] = Arrivals(semaphore(core, "moved_" + name))
    return core.arrivals[name]


def move(core, lane, name, to, of, *waits):
    return arrival(core, name).dma(lane, lambda e: e.dma_start(to, of), *waits)


def gather(core, name, to, of, index, *waits):
    at = bass.IndirectOffsetOnAxis(index, 0)
    return arrival(core, name).dma(core.pool, lambda e: e.indirect_dma_start(to, None, of, at), *waits)


def scatter(core, name, to, index, of, *waits):
    at = bass.IndirectOffsetOnAxis(index, 0)
    return arrival(core, name).dma(core.pool, lambda e: e.indirect_dma_start(to, at, of, None), *waits)


def memory(core):
    nc = core.nc
    base = -(-nc.sbuf_base // 64) * 64
    end = nc.sbuf_usable_end
    core.ctx.enter_context(nc.sbuf_tensor("arena", [P, (nc.sbuf_bytes_remaining - 128) // 4], F32))
    size_of = {F32: 4, F32R: 4, BF16: 2, I32: 4, U8: 1}
    top = [base]

    def put(name, shape, dt=F32, at=top):
        tensor = nc.alloc_sbuf_tensor_at(name, shape, dt, offset=at[0])
        at[0] += -(-int(np.prod(shape[1:])) * size_of[dt] // 32) * 32
        return tensor

    core.cst = put("cst", [P, sum(n for _, n in core.where32.values())])
    core.csb = put("csb", [P, sum(n for _, n in core.where16.values())], BF16)
    core.x_tok = put("x_tok", [P, NT, P])
    core.mix = put("mix", [P, NT, P])
    core.xT = put("xT", [P, NTOK])
    core.small = put("small", [P, 1700])
    core.ints = put("ints", [P, 4 * G1 + 4 * NT + GF + 2 * G3 + 16], I32)
    core.hotb1 = put("hotb1", [P, E], BF16)
    core.hotb3 = put("hotb3", [P, E], BF16)
    core.at1 = put("at1", [P, SPT * G1], BF16)
    core.at3 = put("at3", [P, SPT * G3], BF16)
    core.rows = put("rows", [P, 4, P])
    core.rowsT = put("rowsT", [P, 2, P])
    core.gated = put("gated", [P, 2, I1])
    core.hid = put("hid", [P, 2, I1])
    core.hidT = put("hidT", [P, 2, I1])
    core.compared = put("compared", [P, NT * EF])
    core.hotF = put("hotF", [P, NT * EF], BF16)
    at = [top[0]]
    core.counts, core.running = put("counts", [P, NT * EF], at=at), put("running", [P, NT * EF], at=at)
    core.chosen = put("chosen", [P, 2, 2, CH])
    assert at[0] <= top[0] - 2 * CH * 4
    core.result = put("result", [P, 3, P])
    feed = top[0]
    core.w1f = put("w1f", [P, (EF + 1) * W1F])
    core.late = -(-(top[0] + (E + 1) * W1C * 4 - end) // (W1F * 4))
    mixture = top[0] - core.late * W1F * 4
    top = [mixture]
    core.w1c = put("w1c", [P, (E + 1) * W1C], at=top)
    assert top[0] <= end and core.late > 0

    at = [feed]
    core.l0w = put("l0w", [P, (E + 1) * P], at=at)
    core.maskT = core.l0w[:, E * P:]
    core.cond_all = put("cond_all", [P, E * NSEQ], at=at)
    core.scaled = put("scaled", [P, 2, E, CH], at=at)
    core.l0p = put("l0p", [P, L0P], at=at)
    core.w10, core.w20 = core.l0p[:, 0:E * H0], split(core.l0p[:, E * H0:E * H0 + 2 * P], 2)
    core.lnsT, core.wg0, core.b10, core.l0b = (core.l0p[:, L0P - b:L0P - a] for a, b in (
        (E + 3, 3 * E + 3), (3, E + 3), (1, 3), (0, 1)))
    core.b10s = put("b10s", [P, 2], at=at)
    core.w10s = put("w10s", [P, E * H0], at=at)
    core.w10b = put("w10b", [P, E * H0], at=at)
    core.b20 = put("b20", [E, 3 * P], at=at)
    core.b20p = put("b20p", [E, 3 * P], BF16, at=at)
    core.oh0 = put("oh0", [P, NT * E], BF16, at=at)
    core.ohT = put("ohT", [E, NTOK], BF16, at=at)
    core.h0 = put("h0", [P, 2, 2, CH], at=at)
    core.yT = put("yT", [P, NTOK], at=at)
    core.xhat = put("xhat", [P, NT, P], at=at)
    assert at[0] <= mixture, (at[0], mixture)

    core.bhi = put("bhi", [P, 2, 4 * CH], F32R, at=[mixture])
    core.blo = put("blo", [P, 2, 4 * CH], F32R, at=[mixture + 8 * CH * 4])
    at = [mixture + core.late * W1F * 4]
    core.w3c = put("w3c", [P, E * W3C], at=at)
    core.bias3 = put("bias3", [3, E * W3C], BF16, at=at)
    core.adaT = put("adaT", [P, P], at=at)
    core.wbT = put("wbT", [P, P], at=at)
    core.adbT = put("adbT", [P, P], at=at)
    core.bb2 = put("bb2", [P, P], at=at)
    core.lng2 = put("lng2", [P, 2], at=at)
    core.wraw = put("wraw", [P, P], at=at)
    core.s3 = put("s3", [P, 3], at=at)
    assert at[0] <= end, (at[0], end)
    at = [feed]
    core.wq = put("wq", [P, P], at=at)
    core.b3 = put("b3", [E, B3C], at=at)
    core.b3rest = put("b3rest", [E, 2 * B3C], at=at)
    core.b3p = put("b3p", [E, 3 * B3C], BF16, at=at)
    core.hsT = put("hsT", [P, 2, CH], at=at)
    core.z2 = put("z2", [P, 2, CH], at=at)
    core.kraw = put("kraw", [P, 2 * F3 + 4 * F3 + 4 * P], U8, at=at)
    core.w3a = put("w3a", [P, F3], F32R, at=at)
    core.w3b = put("w3b", [P, 4 * F3], F32R, at=at)
    core.w3d = put("w3d", [P, 4 * P], F32R, at=at)
    core.uhi = put("uhi", [P, 2, CH], F32R, at=at)
    core.ulo = put("ulo", [P, 2, CH], F32R, at=at)
    core.hf = put("hf", [P, 2, CH], at=at)
    core.kf = put("kf", [P, 2 * F3], at=[at[0]])
    core.ahi = put("ahi", [P, 2, 4 * CH], F32R, at=at)
    core.alo = put("alo", [P, 2, 4 * CH], F32R, at=at)
    assert at[0] <= mixture, (at[0], mixture)
    core.bank = [core.ctx.enter_context(nc.psum_tensor(f"bank{i}", [P, CH], F32)) for i in range(8)]
    core.freed = [None] * 8
    core.small_at = core.ints_at = 0
    core.rows_free, core.rowsT_free, core.result_sent = [None] * 4, [None] * 2, [None] * 3
    core.gated_free, core.hid_free, core.hidT_free = [None] * 2, [None] * 2, [None] * 2

    def dram(name, n):
        return nc.dram_tensor(name, [n, P], F32).ap()

    core.x1_rows = dram("x1_rows", NTOK)
    core.mix1_rows = dram("mix1_rows", SPILL1 + P * G1)
    core.sorted_rows = dram("sorted_rows", P * GF)
    core.ffn1_rows = dram("ffn1_rows", P * GF)
    core.x3_rows = dram("x3_rows", NTOK)
    core.mix3_rows = dram("mix3_rows", P * G3)


def c32(core, name, rows=P):
    at, n = core.where32[name]
    return core.cst[0:rows, at:at + n]


def c16(core, name, rows=P):
    at, n = core.where16[name]
    return core.csb[0:rows, at:at + n]


def some(core, n):
    core.small_at += n
    assert core.small_at <= core.small.shape[1], core.small_at
    return core.small[:, core.small_at - n:core.small_at]


def some_ints(core, n):
    core.ints_at += n
    assert core.ints_at <= core.ints.shape[1], core.ints_at
    return core.ints[:, core.ints_at - n:core.ints_at]


def first_loads(core):
    A, sp, act = core.A, core.sp, core.act
    core.got_maps = move(core, act, "l0w", core.l0w[:, :], A["l0w"])
    core.got_xT = [move(core, sp if c % 2 == 0 else act, f"xT_{c}", core.xT[:, c * CH:(c + 1) * CH], A["xT"][:, c * CH:(c + 1) * CH])
                   for c in range(1)]
    core.got_cond_all = move(core, sp, "cond_all", core.cond_all[:, :], A["cond_all"].partition_broadcast(P))
    core.cond2 = some(core, E)
    core.got_cond = [move(core, sp, "cond_a", core.cond2[0:NSEQ, :], A["cond"]),
                     move(core, sp, "cond_b", core.cond2[NSEQ:P, :], A["cond"])]
    core.got0 = move(core, act, "l0p", core.l0p[:, :], A["l0p"])
    core.got_xT += [move(core, sp if c % 2 == 0 else act, f"xT_{c}", core.xT[:, c * CH:(c + 1) * CH], A["xT"][:, c * CH:(c + 1) * CH])
                    for c in range(1, NC)]
    core.got_b20 = move(core, act, "b20", core.b20[:, 0:P], A["b20"])
    core.got_csb = move(core, act, "csb", core.csb[:, :], A["csb"])
    core.got_cst = move(core, sp, "cst", core.cst[:, :], A["cst"])
    core.condT, core.gate_w = some(core, NSEQ), some(core, EF)
    core.got_kept = [move(core, act, "kept", to, of) for to, of in (
        (core.condT[0:E, :], A["condT"]), (core.gate_w, A["gate_w"]))][-1]
    core.got_x = move(core, sp, "x_tok", core.x_tok[:, :, :], tiles_of(A["x"]))
    core.got_w1c = {}
    for e in range(E + 1):
        core.got_w1c[e] = move(core, sp, f"w1c_{e}", core.w1c[:, e * W1C:(e + 1) * W1C], A["w1c"][e])
    core.halves = some(core, NT)
    core.have_halves = core.pool.do(lambda e: e.memset(core.halves, -0.5))
    zero = core.pool.do(lambda e: e.memset(core.rows[:, 0, :], 0.0))
    core.zeroed = move(core, sp, "zeroed", tiles_of(core.sorted_rows), bm(core.rows[:, 0, :], GF), zero)
    core.rows_free[0] = core.zeroed


def first_max(core, logits, m, n, best, tmp, hot, *waits):
    dve, top = core.dve, some(core, m)
    s = dve.do(lambda e: e.tensor_reduce(best, logits, AX_X, ALU.max), *waits)
    yield
    s = dve.do(lambda e: e.tensor_tensor(tmp, logits, bc(best, n), ALU.is_ge), s)
    yield
    s = dve.do(lambda e: e.tensor_tensor(tmp, tmp, bm(c32(core, "rev")[:, 0:n], m), ALU.mult), s)
    yield
    s = dve.do(lambda e: e.tensor_reduce(top, tmp, AX_X, ALU.max), s)
    yield
    yield dve.do(lambda e: e.tensor_tensor(hot, tmp, bc(top, n), ALU.is_equal), s)


def mean_rstd(core, stats, n, eps, *waits):
    dve = core.dve
    v = stats.rearrange("p (j k) -> p k j", k=6)
    total, apart, var, rstd, minus = (some(core, n) for _ in range(5))
    a = dve.do(lambda e: e.tensor_tensor(total, v[:, 1, :], v[:, 4, :], ALU.add), *waits)
    b = dve.do(lambda e: e.tensor_tensor(apart, v[:, 1, :], v[:, 4, :], ALU.subtract))
    c = dve.do(lambda e: e.tensor_tensor(var, v[:, 2, :], v[:, 5, :], ALU.add))
    a = dve.do(lambda e: e.tensor_scalar(minus, total, -0.5, None, ALU.mult), a)
    b = dve.do(lambda e: e.tensor_tensor(apart, apart, apart, ALU.mult), b)
    c = dve.do(lambda e: e.tensor_scalar(var, var, 1.0 / P, eps, ALU.mult, ALU.add), c)
    c = dve.do(lambda e: e.scalar_tensor_tensor(var, apart, 0.25, var, ALU.mult, ALU.add), b, c)
    c = core.pool.do(lambda e: e.tensor_tensor(rstd, var, core.halves[:, 0:n], ALU.pow), c, core.have_halves)
    return [a, c], minus, rstd


def bf16_parts(core, x, parts, rest, *waits):
    dve, n = core.dve, x.shape[-1]
    s = dve.do(lambda e: e.tensor_copy(parts[:, 0:n], x), *waits)
    s = dve.do(lambda e: e.tensor_tensor(rest[:, 0:n], x, parts[:, 0:n], ALU.subtract), s)
    s = dve.do(lambda e: e.tensor_copy(parts[:, n:2 * n], rest[:, 0:n]), s)
    s = dve.do(lambda e: e.tensor_tensor(rest[:, n:2 * n], rest[:, 0:n], parts[:, n:2 * n], ALU.subtract), s)
    return dve.do(lambda e: e.tensor_copy(parts[:, 2 * n:3 * n], rest[:, n:2 * n]), s)


def products(core, make, n, *waits):
    core.pe.wait(*waits)
    for i in range(n - 1):
        core.pe.go(lambda e, i=i: make(e, i))
    return core.pe.do(lambda e: make(e, n - 1))


def transposes(core, k, of, *waits):
    return products(core, lambda e, t: e.transpose(core.bank[k][:, t * P:(t + 1) * P], of(t), c32(core, "ident")),
                    TPC, *waits)


def choose(core):
    dve, act = core.dve, core.act
    cond = core.cond2
    best1, hot1, tmp = some(core, 1), some(core, E), some(core, E)
    h1 = yield from last_of(first_max(core, bm(cond, 1), 1, E, best1, bm(tmp, 1), bm(hot1, 1), core.got_cond, core.got_cst))
    left, best2, hot2 = some(core, E), some(core, 1), some(core, E)
    s = dve.do(lambda e: e.tensor_scalar(left, hot1, -3.0e38, None, ALU.mult), h1)
    s = dve.do(lambda e: e.tensor_tensor(left, left, cond, ALU.add), s)
    h2 = yield from last_of(first_max(core, bm(left, 1), 1, E, best2, bm(tmp, 1), bm(hot2, 1), s))
    minus, ex, total, rw = some(core, 1), some(core, E), some(core, 1), some(core, E)
    s = dve.do(lambda e: e.tensor_scalar(minus, best1, -1.0, None, ALU.mult))
    s = act.do(lambda e: e.activation(ex, cond, ACT.Exp, bias=minus, scale=1.0), s, core.got_cond)
    s = dve.do(lambda e: e.tensor_reduce(total, ex, AX_X, ALU.add), s)
    s = dve.do(lambda e: e.reciprocal(total, total), s)
    s = dve.do(lambda e: e.tensor_scalar(rw, ex, total, None, ALU.mult), s)
    yield
    t1, t2, w, scaled = some(core, E), some(core, E), some(core, 2), some(core, 2)
    a = dve.do(lambda e: e.tensor_tensor(t1, rw, hot1, ALU.mult), s)
    b = dve.do(lambda e: e.tensor_tensor(t2, rw, hot2, ALU.mult), h2)
    a = dve.do(lambda e: e.tensor_reduce(w[:, 0:1], t1, AX_X, ALU.add), a)
    b = dve.do(lambda e: e.tensor_reduce(w[:, 1:2], t2, AX_X, ALU.add), b)
    both = some(core, 1)
    s = dve.do(lambda e: e.tensor_tensor(both, w[:, 0:1], w[:, 1:2], ALU.add), a, b)
    s = dve.do(lambda e: e.reciprocal(both, both), s)
    s = dve.do(lambda e: e.tensor_scalar(w, w, both, None, ALU.mult), s)
    s = dve.do(lambda e: e.tensor_scalar(scaled, w, 1.0 / 12, None, ALU.mult), s)
    s = dve.do(lambda e: e.scalar_tensor_tensor(w, w, 1.0 - 1.0 / 12, scaled, ALU.mult, ALU.add), s)
    yield
    core.wpair, core.hpair, core.hfirst = some(core, 1), some(core, E), some(core, E)
    first, second = c32(core, "first"), c32(core, "second")
    s = dve.do(lambda e: e.tensor_scalar(core.wpair, w[:, 1:2], second, None, ALU.mult), s)
    s = dve.do(lambda e: e.scalar_tensor_tensor(core.wpair, w[:, 0:1], first, core.wpair, ALU.mult, ALU.add), s)
    s = dve.do(lambda e: e.tensor_scalar(core.hpair, hot2, second, None, ALU.mult))
    s = dve.do(lambda e: e.scalar_tensor_tensor(core.hpair, hot1, first, core.hpair, ALU.mult, ALU.add), s)
    core.have_pairs = dve.do(lambda e: e.tensor_scalar(core.hfirst, hot1, first, None, ALU.mult))


def route(core, hot, hotb, at, groups, columns, weights, absent):
    dve = core.dve
    b, k = core.bank[7], 7
    s = dve.do(lambda e: e.tensor_copy(hotb[:, :], hot), core.have_pairs)
    yield
    m = products(core, lambda e, i: e.matmul(b[:, i * E:(i + 1) * E], c16(core, ("before", "ones")[i]), hotb[:, :],
                                              start=True, stop=True), 2, s, core.got_csb, core.freed[k])
    n = core.where32["steps_seq"][1]
    below = core.hidT[:, 0, 0:E * n]
    ngroups, upto, place = some(core, E), some(core, E), some(core, 1)
    start, pos = some(core, E), some(core, E)
    s = dve.do(lambda e: e.tensor_tensor(split(below, E), bc(b[:, E:2 * E], n), bm(c32(core, "steps_seq"), E), ALU.is_gt), m)
    s = dve.do(lambda e: e.tensor_reduce(ngroups, split(below, E), AX_X, ALU.add), s)
    s = dve.do(lambda e: e.tensor_tensor_scan(upto, c32(core, "ones")[:, 0:E], ngroups, 0.0, ALU.mult, ALU.add), s)
    s = dve.do(lambda e: e.tensor_tensor(start, upto, ngroups, ALU.subtract), s)
    s = core.freed[k] = dve.do(lambda e: e.scalar_tensor_tensor(pos, start, float(SPT), b[:, 0:E], ALU.mult, ALU.add), s)
    yield
    s = dve.do(lambda e: e.tensor_tensor(pos, pos, hot, ALU.mult), s)
    s = dve.do(lambda e: e.tensor_reduce(place, pos, AX_X, ALU.add), s)
    if absent:
        s = dve.do(lambda e: e.tensor_tensor(place, place, c32(core, "absent"), ALU.add), s)
    have_place = s
    yield
    s = dve.do(lambda e: e.tensor_scalar(at[:, :], c32(core, "place")[:, 0:SPT * groups], place, None, ALU.is_equal), s)
    at4 = at[:, :].rearrange("p (g r) -> p r g", r=SPT)
    m = products(core, lambda e, i: e.matmul(
        b[:, 64 * (i // SPT):64 * (i // SPT) + groups],
        c16(core, ("pair", "quad")[i // SPT])[:, i % SPT * P:(i % SPT + 1) * P], at4[:, i % SPT, :],
        start=i % SPT == 0, stop=i % SPT == SPT - 1), 2 * SPT, s, core.freed[k])
    pair, filled, high = some(core, groups), some(core, groups), some(core, groups)
    src, first = some_ints(core, groups), some_ints(core, groups)
    s = dve.do(lambda e: e.tensor_copy(pair, b[:, 0:groups]), m)
    f = core.freed[k] = dve.do(lambda e: e.tensor_copy(filled, b[:, 64:64 + groups]))
    s = dve.do(lambda e: e.tensor_scalar(high, pair, float(NSEQ), -float(NSEQ), ALU.is_ge, ALU.mult), s)
    s = dve.do(lambda e: e.tensor_tensor(high, high, pair, ALU.add), s)
    have_src = dve.do(lambda e: e.tensor_scalar(src, high, float(SEQ), c32(core, "within"), ALU.mult, ALU.add), s)
    dst = scale = have_dst = None
    yield
    if weights is not None:
        dst, scale = some_ints(core, groups), some(core, groups)
        spill = c32(core, "spill")
        s = dve.do(lambda e: e.tensor_scalar(pair, pair, float(SEQ), c32(core, "within"), ALU.mult, ALU.add), have_src)
        s = dve.do(lambda e: e.tensor_tensor(pair, pair, spill, ALU.subtract), s)
        s = dve.do(lambda e: e.tensor_tensor(pair, pair, filled, ALU.mult), s, f)
        have_dst = dve.do(lambda e: e.tensor_tensor(dst, pair, spill, ALU.add), s)
        yield
        wquad, atf = core.hid[:, 0, :], core.hid[:, 1, 0:SPT * groups]
        dve.do(lambda e: e.tensor_scalar(wquad, c32(core, "quad"), weights, None, ALU.mult))
        s = dve.do(lambda e: e.tensor_copy(atf, at[:, :]))
        yield
        f4 = atf.rearrange("p (g r) -> p r g", r=SPT)
        m = products(core, lambda e, r: e.matmul(b[:, 0:groups], wquad[:, r * P:(r + 1) * P], f4[:, r, :],
                                                  start=r == 0, stop=r == SPT - 1), SPT, s, core.freed[k])
        core.freed[k] = dve.do(lambda e: e.tensor_copy(scale, b[:, 0:groups]), m)
        have_dst = [have_dst, core.freed[k]]
        yield
    past, expert = core.hidT[:, 1, 0:groups * E], some(core, groups)
    s = dve.do(lambda e: e.tensor_tensor(split(past, groups), bm(upto, groups), bc(c32(core, "group")[:, 0:groups], E), ALU.is_le),
               have_place)
    s = dve.do(lambda e: e.tensor_reduce(expert, split(past, groups), AX_X, ALU.add), s)
    s = dve.do(lambda e: e.tensor_scalar(expert, expert, float(E - 1), float(columns), ALU.min, ALU.mult), s)
    s = dve.do(lambda e: e.tensor_copy(first, expert), s)
    return dict(src=src, dst=dst, scale=scale, first=first, place=place, have_src=have_src,
                have_dst=have_dst, have_first=s, have_place=have_place)


def route_mixtures(core):
    yield from choose(core)
    core.route1 = yield from route(core, core.hpair, core.hotb1, core.at1, G1, W1C, core.wpair, False)
    core.route3 = yield from route(core, core.hfirst, core.hotb3, core.at3, G3, W3C, None, True)
    wplace = core.hid[:, 0, :]
    s = core.dve.do(lambda e: e.tensor_scalar(wplace, c32(core, "quad"), core.route3["place"], None, ALU.mult),
                    core.route3["have_place"], core.pe.last())
    yield
    m = products(core, lambda e, r: e.matmul(core.bank[7][:, 0:NT], wplace[:, r * P:(r + 1) * P],
                                              c32(core, "pick")[:, r * NT:(r + 1) * NT], start=r == 0, stop=r == SPT - 1),
                     SPT, s, core.freed[7])
    core.hid_free, core.hidT_free = [m] * 2, [m] * 2
    core.back3 = some_ints(core, NT)
    core.have_back3 = core.freed[7] = core.dve.do(lambda e: e.tensor_scalar(
        core.back3, core.bank[7][:, 0:NT], float(SEQ), c32(core, "within"), ALU.mult, ALU.add), m)


def layer0(core, routing, following):
    pe, act, dve, pool = core.pe, core.act, core.dve, core.pool
    yT, bank, freed = core.yT, core.bank, core.freed
    ident, nseq = c32(core, "ident"), CH // SEQ
    scaled_free, h0_free, gated_free = [None] * 2, [None] * 2, core.gated_free
    stats, best = some(core, 6 * NT), some(core, NT)
    spread = core.where16["spread"][0]
    core.have_x1 = [None] * NC
    ready = {}

    def first_matrices():
        have_w10s = pool.do(lambda e: e.tensor_tensor(split(core.w10s[:, :], E), split(core.w10, E), bc(core.lnsT[:, 0:E], H0), ALU.mult), core.got0)
        s = pool.do(lambda e: e.tensor_tensor(split(core.w10b[:, :], E), split(core.w10, E), bc(core.lnsT[:, E:2 * E], H0), ALU.mult))
        m = products(core, lambda e, h: e.matmul(bank[6][:, h:h + 1], core.w10b[:, h * P:(h + 1) * P], c32(core, "ones")[:, 0:1],
                                                 start=True, stop=True), 2, s, core.got_cst, freed[6])
        freed[6] = dve.do(lambda e: e.tensor_tensor(core.b10s[:, :], core.b10, bank[6][:, 0:2], ALU.add), m, core.got0)
        ready["first"] = [have_w10s, freed[6]]
        ready["b20"] = bf16_parts(core, core.b20[:, 0:P], core.b20p, core.b20[:, P:3 * P], core.got_b20)

    have_yT = []

    have_scaled = {}

    def scalings():
        for c in range(NC):
            for g in range(E):
                if c == 0:
                    w = core.l0w[:, g * P:(g + 1) * P]
                    dve.do(lambda e, w=w: e.tensor_tensor(w, w, core.maskT, ALU.mult), core.got_maps)
                have_scaled[c, g] = dve.do(lambda e, g=g, c=c: e.tensor_tensor(
                    split(core.scaled[:, c % 2, g, :], nseq), split(core.xT[:, c * CH:(c + 1) * CH], nseq),
                    bc(core.cond_all[:, g * NSEQ + c * nseq:g * NSEQ + (c + 1) * nseq], SEQ), ALU.mult),
                    core.got_xT[c], core.got_cond_all, scaled_free[c % 2])
                if g % 2:
                    yield

    def maps():
        for c in range(NC):
            k = 4 * (c % 2)
            for g in range(E):
                m = products(core, lambda e, _, g=g, c=c, k=k: e.matmul(
                    bank[k][:, :], core.l0w[:, g * P:(g + 1) * P], core.scaled[:, c % 2, g, :], start=g == 0, stop=g == E - 1),
                    1, have_scaled[c, g], freed[k])
                if g < E - 1 and g % 2:
                    yield
            scaled_free[c % 2] = m
            freed[k] = act.do(lambda e, c=c, k=k: e.activation(yT[:, c * CH:(c + 1) * CH], bank[k][:, :], ACT.Identity, bias=core.l0b[:, 0:1], scale=1.0), m, core.got0)
            have_yT.append(freed[k])
            yield

    def chunk(c):
        i = c % 2
        b0, b1, b2, b3 = (4 * i + k for k in range(4))
        cols = slice(c * CH, (c + 1) * CH)
        tiles = range(c * TPC, (c + 1) * TPC)
        if c == 0:
            first_matrices()
        have_lg = products(core, lambda e, t: e.matmul(bank[b2][:, t * E:(t + 1) * E], yT[:, tiles[t] * P:(tiles[t] + 1) * P], core.wg0,
                                                       start=True, stop=True), TPC, have_yT[c], core.got0, freed[b2])
        m = transposes(core, b1, lambda t: yT[:, tiles[t] * P:(tiles[t] + 1) * P], have_yT[c], core.got_cst, freed[b1])
        for t in range(TPC):
            dve.do(lambda e, t=t: e.bn_stats(stats[:, 6 * tiles[t]:6 * tiles[t] + 6], bank[b1][:, t * P:(t + 1) * P]), m)
        ok, minus, rstd = mean_rstd(core, stats[:, 6 * c * TPC:6 * (c + 1) * TPC], TPC, 1e-5, dve.last())
        oh0 = core.oh0[:, c * TPC * E:(c + 1) * TPC * E]
        tmp = some(core, TPC * E)
        hot = run(first_max(core, split(bank[b2][:, 0:TPC * E], TPC), TPC, E, best[:, c * TPC:(c + 1) * TPC], split(tmp, TPC), split(oh0, TPC), have_lg))
        freed[b2] = hot
        for t in range(TPC):
            s = dve.do(lambda e, t=t: e.tensor_scalar(
                core.xhat[:, tiles[t], :], bank[b1][:, t * P:(t + 1) * P], minus[:, t:t + 1], rstd[:, t:t + 1], ALU.add, ALU.mult), ok)
        freed[b1] = s
        yield
        half = bank[b2][0:E, 0:CH // 2].bitcast(BF16)
        m = products(core, lambda e, t: e.transpose(half[:, t * P:(t + 1) * P], oh0[:, t * E:(t + 1) * E], c16(core, "ident")),
                     TPC, hot, core.got_csb, freed[b2])
        have_ohT = freed[b2] = act.do(lambda e: e.activation(core.ohT[:, cols], half, ACT.Copy), m)
        m = transposes(core, b3, lambda t: core.xhat[:, tiles[t], :], s, freed[b3])
        have_xhT = freed[b3] = act.do(lambda e: e.activation(core.xT[:, cols], bank[b3][:, :], ACT.Copy), m)
        yield
        for h, k, k2 in ((0, b0, b2), (1, b3, b1)):
            m = products(core, lambda e, _, h=h, k=k: e.matmul(bank[k][:, :], core.w10s[:, h * P:(h + 1) * P], core.xT[:, cols],
                                                               start=True, stop=True), 1, have_xhT, ready["first"], freed[k])
            m2 = products(core, lambda e, _, h=h, k2=k2: e.matmul(
                bank[k2][:, :], core.csb[0:E, spread + h * P:spread + (h + 1) * P], core.ohT[:, cols],
                start=True, stop=True), 1, have_ohT, freed[k2])
            freed[k] = act.do(lambda e, h=h, k=k: e.activation(
                core.gated[:, h, :], bank[k][:, :], ACT.Gelu, bias=core.b10s[:, h:h + 1], scale=1.0), m, ready["first"], gated_free[h])
            have_h = freed[k2] = gated_free[h] = dve.do(lambda e, h=h, k2=k2: e.tensor_tensor(
                core.h0[:, i, h, :], core.gated[:, h, :], bank[k2][:, :], ALU.mult), freed[k], m2, h0_free[i])
        yield

        def product(e, n):
            t, n = divmod(n, 5)
            j = tiles[t]
            to = bank[b1][:, t * P:(t + 1) * P]
            if n < 2:
                return e.matmul(to, core.h0[:, i, n, t * P:(t + 1) * P], core.w20[:, n, :], start=n == 0, stop=False)
            return e.matmul(to, core.ohT[:, j * P:(j + 1) * P], core.b20p[:, (n - 2) * P:(n - 1) * P], start=False, stop=n == 4)
        m = h0_free[i] = products(core, product, 5 * TPC, have_h, ready["b20"], freed[b1])
        rows = core.x_tok[:, c * TPC:(c + 1) * TPC, :]
        s = core.have_x1[c] = freed[b1] = dve.do(lambda e: e.tensor_tensor(rows, rows, split(bank[b1][:, :], TPC), ALU.add), m, core.got_x)
        core.kept_x1 = move(core, core.sp, "x1_rows", tiles_of(core.x1_rows)[:, c * TPC:(c + 1) * TPC, :], rows, s)

    per = E // 2
    last = 2 + per * NC
    interleave([scalings(), maps(), routing, *(chunk(c) for c in range(NC)), routing, following],
               first=[0, 2, 1, *(2 + per * (c + 1) for c in range(NC)), 1, last])


def experts(core, n, item):
    pe, act, dve, bank, freed = core.pe, core.act, core.dve, core.bank, core.freed
    items, state = [], [dict() for _ in range(n)]
    rowsT_free, gated_free, hid_free, hidT_free = core.rowsT_free, core.gated_free, core.hid_free, core.hidT_free

    def turn(i):
        items.append(item(i))
        it, s = items[i], state[i]
        if "turned" in it:
            s["xT"], s["have_xT"] = it["turned"]
            return
        rows, have = it["rows"]
        m = products(core, lambda e, _: e.transpose(bank[6][:, 0:P], rows, c32(core, "ident")), 1, have, core.freed[6])
        if "slot" in it:
            core.rows_free[it["slot"]] = m
        s["xT"] = core.rowsT[:, i % 2, :]
        s["have_xT"] = freed[6] = dve.do(lambda e: e.tensor_copy(s["xT"], bank[6][:, 0:P]), m, rowsT_free[i % 2])

    def first_products(i):
        it, s = items[i], state[i]
        width, bias = it["width"], it.get("bias")
        g = i % 2
        u, up_at = (g + 2, 0) if width == I1 else (g, width)
        reg = s["first"] = {}
        if not isinstance(it["first"], int):
            column, have = it["first"]
            pe.wait(have)
            pe.go(lambda e: reg.setdefault("v", e.value_load(column, min_val=0, max_val=it["most"])))
        else:
            reg["v"] = it["first"]
        pe.wait(it.get("have_w"), s["have_xT"], freed[g], freed[u])
        if width == I1:
            pe.go(lambda e: e.matmul(bank[g][:, :], s["xT"], it["w"][:, bass.ds(reg["v"], CH)], start=True, stop=True))
            s["gu"] = pe.do(lambda e: e.matmul(bank[u][:, :], s["xT"], it["w"][:, bass.ds(reg["v"] + CH, CH)], start=True, stop=True))
        else:
            if bias is not None:
                pe.go(lambda e: e.matmul(bank[g][:, :], c16(core, "ones")[0:3, :], bias[:, bass.ds(reg["v"], CH)], start=True, stop=False))
            s["gu"] = pe.do(lambda e: e.matmul(bank[g][:, :], s["xT"], it["w"][:, bass.ds(reg["v"], CH)], start=bias is None, stop=True))
        rowsT_free[i % 2] = s["gu"]
        a = act.do(lambda e: e.activation(core.gated[:, i % 2, 0:width], bank[g][:, 0:width], it["func"]), s["gu"], gated_free[i % 2])
        d = dve.do(lambda e: e.tensor_tensor(core.hid[:, i % 2, 0:width], core.gated[:, i % 2, 0:width],
                                             bank[u][:, up_at:up_at + width], ALU.mult), a, hid_free[i % 2])
        gated_free[i % 2] = freed[u] = s["have_hid"] = d
        if g != u:
            freed[g] = a

    def turn_hidden(i):
        s, k, width = state[i], 4 + i % 2, items[i]["width"]
        m = products(core, lambda e, b: e.transpose(bank[k][:, b * P:(b + 1) * P], core.hid[:, i % 2, b * P:(b + 1) * P], c32(core, "ident")),
                     width // P, s["have_hid"], core.freed[k])
        hid_free[i % 2] = m
        s["have_hidT"] = freed[k] = act.do(lambda e: e.activation(core.hidT[:, i % 2, 0:width], bank[k][:, 0:width], ACT.Copy), m, hidT_free[i % 2])

    def second_products(i):
        it, s = items[i], state[i]
        v, width, bias = s["first"], it["width"], it.get("bias")
        to = bank[7][:, 0:P]
        pe.wait(s["have_hidT"], freed[7])
        if bias is not None:
            pe.go(lambda e: e.matmul(to, c16(core, "ones")[0:3, :], bias[:, bass.ds(v["v"] + 2 * width, P)], start=True, stop=False))
        for b in range(width // P):
            s["y"] = pe.do(lambda e, b=b: e.matmul(to, core.hidT[:, i % 2, b * P:(b + 1) * P],
                                                   it["w"][:, bass.ds(v["v"] + 2 * width + b * P, P)],
                                                   start=b == 0 and bias is None, stop=b == width // P - 1))
        hidT_free[i % 2] = s["y"]
        freed[7] = it["sink"](to, s["y"])

    turn(0)
    for i in range(n + 2):
        if i + 1 < n:
            turn(i + 1)
        if i < n:
            first_products(i)
        if 0 <= i - 2 < n:
            second_products(i - 2)
        if 0 <= i - 1 < n:
            turn_hidden(i - 1)
        yield i


def gathered(core, source, route, g, *waits):
    slot = g % 4
    have = gather(core, f"rows_{slot}", core.rows[:, slot, :], source, route["src"][:, g:g + 1],
                       route["have_src"], core.rows_free[slot], *waits)
    return core.rows[:, slot, :], have


def layer1(core):
    pe, act, dve = core.pe, core.act, core.dve
    core.got_w1f, core.have_mixT, have_mix, fetched = [], [None] * NC, [None] * NT, {}
    ahead = NT // 2
    ffn = NT + G1
    groups = ffn + NT

    def mixture_item(i):
        if ahead <= i < ahead + G1:
            g, r = i - ahead, core.route1

            def send(y, m):
                slot = g % 3
                s = dve.do(lambda e: e.tensor_scalar(core.result[:, slot, :], y, r["scale"][:, g:g + 1], None, ALU.mult),
                           m, core.result_sent[slot], r["have_dst"])
                core.result_sent[slot] = scatter(core, f"scattered_{slot}", core.mix1_rows, r["dst"][:, g:g + 1], core.result[:, slot, :], s)
                return s
            return dict(width=I1, func=ACT.Gelu_apprx_tanh, rows=fetched[g], first=(r["first"][0:1, g:g + 1], r["have_first"]), most=(E - 1) * W1C, w=core.w1c[:, W1C:],
                        have_w=[core.got_w1c[e] for e in range(1, E + 1)], sink=send, slot=g % 4)
        j = i if i < ahead else i - G1

        def keep(y, m):
            have_mix[j] = dve.do(lambda e: e.tensor_copy(core.mix[:, j, :], y), m)
            return have_mix[j]
        return dict(width=I1, func=ACT.Gelu_apprx_tanh, rows=(core.x_tok[:, j, :], core.have_x1[j // TPC]), first=0, w=core.w1c, have_w=core.got_w1c[0], sink=keep)

    def ffn_item(i):
        if i < NT:
            def add(y, m):
                return dve.do(lambda e: e.tensor_tensor(core.x_tok[:, i, :], core.x_tok[:, i, :], y, ALU.add), m, core.kept_x1)
            return dict(width=IF, func=ACT.Silu, turned=(core.xT[:, i * P:(i + 1) * P], core.have_mixT[i // TPC]), first=0, w=core.w1f,
                        have_w=core.got_w1f[0], sink=add)
        g = i - NT

        def send(y, m):
            slot = g % 3
            s = dve.do(lambda e: e.tensor_copy(core.result[:, slot, :], y), m, core.result_sent[slot])
            core.result_sent[slot] = move(core, core.sp, f"sent_{slot}", core.ffn1_rows[g * P:(g + 1) * P], core.result[:, slot, :], s)
            return s
        return dict(width=IF, func=ACT.Silu, rows=fetched[g], first=(core.firstF[0:1, g:g + 1], core.have_firstF), most=(EF - 1) * W1F,
                    w=core.w1f[:, W1F:], have_w=core.got_routed, sink=send, slot=g % 4)

    chosen_free = [None] * 2

    def load(c):
        return [move(core, core.sp, f"chosen_{k}_{c % 2}", split(core.chosen[:, c % 2, k, :], TPC),
                     tiles_of(core.mix1_rows[k * NTOK + c * CH:k * NTOK + (c + 1) * CH]), chosen_free[c % 2], core.result_sent)
                for k in range(2)]

    def add(c, got):
        part = core.mix[:, c * TPC:(c + 1) * TPC, :]
        s = dve.do(lambda e: e.tensor_tensor(part, part, split(core.chosen[:, c % 2, 0, :], TPC), ALU.add), got, have_mix[c * TPC:(c + 1) * TPC])
        chosen_free[c % 2] = dve.do(lambda e: e.tensor_tensor(part, part, split(core.chosen[:, c % 2, 1, :], TPC), ALU.add), s)
        return chosen_free[c % 2]

    def turn(c, s):
        k = 4 + c % 2
        m = transposes(core, k, lambda t: core.mix[:, c * TPC + t, :], s, core.freed[k])
        core.have_mixT[c] = core.freed[k] = act.do(lambda e: e.activation(core.xT[:, c * CH:(c + 1) * CH], core.bank[k][:, :], ACT.Copy), m)

    core.bestF = some(core, NT)

    def choose_experts(c):
        tiles, cols = slice(c * TPC, (c + 1) * TPC), slice(c * TPC * EF, (c + 1) * TPC * EF)
        have_lg = products(core, lambda e, t: e.matmul(
            core.bank[6][:, t * EF:(t + 1) * EF], core.xT[:, (c * TPC + t) * P:(c * TPC + t + 1) * P], core.gate_w, start=True, stop=True),
            TPC, core.have_mixT[c], core.got_kept, core.freed[6])
        core.have_hotF = core.freed[6] = run(first_max(
            core, split(core.bank[6][:, 0:TPC * EF], TPC), TPC, EF, core.bestF[:, tiles], split(core.compared[:, cols], TPC),
            split(core.hotF[:, cols], TPC), have_lg))

    def sums():
        got = [load(0), load(1)]
        yield
        yield
        for c in range(2):
            s = add(c, got[c])
            got.append(load(c + 2))
            yield
            turn(c, s)
            yield
            choose_experts(c)
        for c in range(2, NC):
            while have_mix[c * TPC + TPC - 1] is None:
                yield
            s = add(c, got[c])
            yield
            turn(c, s)
            yield
            choose_experts(c)
        core.counts_free = [s, *chosen_free]

    summing, routing = sums(), route_tokens(core)
    for i in experts(core, groups + GF, lambda i: mixture_item(i) if i < ffn else ffn_item(i - ffn)):
        if i == ahead - 4:
            core.layer0_done = [pe.last(), dve.last(), act.last()]
        g = i - (ahead - 4)
        if 0 <= g < G1:
            fetched[g] = gathered(core, core.x1_rows, core.route1, g, core.kept_x1)
        if 0 <= g < EF + 1 - core.late:
            core.got_w1f.append(move(core, core.sp, "w1f" if g else "w1f_shared", core.w1f[:, g * W1F:(g + 1) * W1F], core.A["w1f"][g], core.layer0_done))
        if i > ahead + G1 + 1:
            next(summing, None)
        if i == ffn + 1:
            core.mixture_done = [pe.last(), dve.last(), act.last()]
            run(summing)
            core.mix_turned = pe.last()
            layer1_weights(core)
        if i > ffn + 1:
            for _ in range(6):
                next(routing, None)
        g = i - (groups - 4)
        if g == 0:
            run(routing)
        if 0 <= g < GF:
            slot = g % 4
            have = move(core, core.sp, f"sorted_{slot}", core.rows[:, slot, :], core.sorted_rows[g * P:(g + 1) * P], core.sorts, core.rows_free[slot])
            fetched[g] = (core.rows[:, slot, :], have)
        if i == groups:
            core.xT_free = pe.last()
        yield
    core.ffn1_sent = list(core.result_sent)


def layer1_weights(core):
    A, done = core.A, core.mixture_done
    for i in range(EF + 1 - core.late, EF + 1):
        late = move(core, core.act, "late", core.w1f[:, i * W1F:(i + 1) * W1F], A["w1f"][i], done)
    core.got_routed = [core.got_w1f[-1], late]
    core.got2 = [move(core, core.sp, "w2", to, of, done) for to, of in (
        (core.adaT[:, :], A["adaT"]), (core.wbT[:, :], A["wbT"]), (core.adbT[:, :], A["adbT"]),
        (core.bb2[:, :], A["bb2"].partition_broadcast(P)), (core.lng2[:, :], A["lng2"]), (core.wraw[:, :], A["wraw"]))][-1]
    core.got_s3 = [move(core, core.sp, "s3", core.s3[:, i:i + 1], A[f"s{i}"].partition_broadcast(P), done) for i in range(3)][-1]
    for i in range(E):
        core.got_w3c = move(core, core.sp, "w3c", core.w3c[:, i * W3C:(i + 1) * W3C], A["w3c"][i], done)


def route_tokens(core):
    dve, bank = core.dve, core.bank
    tmp, hotb, hot = core.compared, core.hotF, core.have_hotF
    score = some(core, NT)
    core.sorts = [None] * 4
    s = core.act.do(lambda e: e.activation(score, core.bestF, ACT.Sigmoid), hot)
    before = products(core, lambda e, i: e.matmul(bank[3][:, :], c16(core, "before"), hotb[:, :], start=True, stop=True), 1, hot, core.freed[3])
    total = products(core, lambda e, i: e.matmul(bank[2][:, :], c16(core, "ones"), hotb[:, :], start=True, stop=True), 1, core.freed[2])
    for c in range(NC):
        part = core.mix[:, c * TPC:(c + 1) * TPC, :]
        have_rows = dve.do(lambda e, c=c, part=part: e.tensor_tensor(part, part, bc(score[:, c * TPC:(c + 1) * TPC], P), ALU.mult), s, core.mix_turned)
        yield
    tot, cum = core.counts, core.running
    s = dve.do(lambda e: e.tensor_copy(split(tot[:, :], EF).rearrange("p e j -> p j e"), split(bank[2][:, :], NT)), total, core.counts_free)
    core.freed[2] = s
    yield
    s = dve.do(lambda e: e.tensor_tensor_scan(cum[:, :], c32(core, "inner"), tot[:, :], 0.0, ALU.mult, ALU.add), s)
    yield
    counts = split(cum[:, :], EF)[:, :, NT - 1]
    n = core.where32["steps_tile"][1]
    ngroups, upto, start = some(core, EF), some(core, EF), some(core, EF)
    a = dve.do(lambda e: e.tensor_tensor(split(tmp[:, :], EF), bc(counts, n), bm(c32(core, "steps_tile"), EF), ALU.is_gt), s)
    b = dve.do(lambda e: e.tensor_tensor(tot[:, :], cum[:, :], tot[:, :], ALU.subtract), s)
    yield
    a = dve.do(lambda e: e.tensor_reduce(ngroups, split(tmp[:, :], EF), AX_X, ALU.add), a)
    a = dve.do(lambda e: e.tensor_tensor_scan(upto, c32(core, "ones")[:, 0:EF], ngroups, 0.0, ALU.mult, ALU.add), a)
    a = dve.do(lambda e: e.tensor_tensor(start, upto, ngroups, ALU.subtract), a)
    yield
    a = dve.do(lambda e: e.scalar_tensor_tensor(split(tot[:, :], EF), bc(start, NT), float(P), split(tot[:, :], EF), ALU.mult, ALU.add), a, b)
    yield
    a = dve.do(lambda e: e.tensor_tensor(split(cum[:, :], NT), split(tot[:, :], EF).rearrange("p e j -> p j e"), split(bank[3][:, :], NT), ALU.add), a, before)
    core.freed[3] = a
    yield
    a = dve.do(lambda e: e.tensor_tensor(cum[:, :], cum[:, :], hotb[:, :], ALU.mult), a)
    place, core.placeF = some(core, NT), some_ints(core, NT)
    a = dve.do(lambda e: e.tensor_reduce(place, split(cum[:, :], NT), AX_X, ALU.add), a)
    a = core.have_placeF = dve.do(lambda e: e.tensor_copy(core.placeF, place), a)
    for j in range(NT):
        core.sorted = scatter(core, f"sort_{j % 4}", core.sorted_rows, core.placeF[:, j:j + 1], core.mix[:, j, :], a, have_rows, core.zeroed)
        core.sorts[j % 4] = core.sorted
    yield
    core.firstF = some_ints(core, GF)
    expert = some(core, GF)
    at = 0
    while at < GF:
        m = min(NT, GF - at)
        past = tmp[:, 0:m * EF]
        a = dve.do(lambda e, at=at, m=m, past=past: e.tensor_tensor(
            split(past, m), bm(upto, m), bc(c32(core, "group")[:, at:at + m], EF), ALU.is_le), a)
        a = dve.do(lambda e, at=at, m=m, past=past: e.tensor_reduce(expert[:, at:at + m], split(past, m), AX_X, ALU.add), a)
        at += m
        yield
    a = dve.do(lambda e: e.tensor_scalar(expert, expert, float(EF - 1), float(W1F), ALU.min, ALU.mult), a)
    core.have_firstF = dve.do(lambda e: e.tensor_copy(core.firstF, expert), a)


def layer2(core):
    A, pe, act, dve, bank, freed = core.A, core.pe, core.act, core.dve, core.bank, core.freed
    done = [pe.last(), dve.last(), act.last()]
    core.got_k = [move(core, core.sp, "k", core.kraw[:, at:at + n], A[name], done) for name, at, n in (
        ("k0", 0, 2 * F3), ("k1", 2 * F3, 4 * F3), ("k2", 6 * F3, 4 * P))][-1]
    got_b3 = move(core, core.sp, "b3", core.b3[:, :], A["b3"], done)
    s = bf16_parts(core, core.b3[:, :], core.b3p, core.b3rest, got_b3)
    for part in range(3):
        for i in range(E):
            core.have_bias3 = move(core, core.sp, "bias3", core.bias3[part:part + 1, i * W3C:i * W3C + B3C],
                                        core.b3p[i:i + 1, part * B3C:(part + 1) * B3C], s, core.dve.last())
    wx, absw, beta, inv = some(core, NSEQ), some(core, 1), some(core, 1), some(core, 1)
    m = products(core, lambda e, i: e.matmul(bank[7][:, 0:NSEQ], c32(core, "rank_up", E), core.condT[0:E, :],
                                              start=True, stop=True), 1, core.got_kept, core.freed[7])
    s = freed[7] = dve.do(lambda e: e.tensor_scalar(wx, bank[7][:, 0:NSEQ], 2.0, None, ALU.mult), m)
    have_wx = s
    s = dve.do(lambda e: e.tensor_reduce(absw, core.wraw[:, :], AX_X, ALU.add, apply_absolute_value=True), core.got2)
    m = products(core, lambda e, i: e.matmul(bank[7][:, 0:1], c32(core, "ones"), absw, start=True, stop=True), 1, s, core.freed[7])
    have_beta = freed[7] = dve.do(lambda e: e.tensor_scalar(beta, bank[7][:, 0:1], 1.0 / (P * P), None, ALU.mult), m)
    s = dve.do(lambda e: e.tensor_scalar(inv, beta, 1e-5, None, ALU.add), have_beta)
    s = dve.do(lambda e: e.reciprocal(inv, inv), s)
    magic = 1.5 * 2.0 ** 23
    s = dve.do(lambda e: e.tensor_scalar(core.wq[:, :], core.wraw[:, :], inv, magic, ALU.mult, ALU.add), s)
    s = dve.do(lambda e: e.tensor_scalar(core.wq[:, :], core.wq[:, :], magic, -1.0, ALU.subtract, ALU.max), s)
    have_wq = dve.do(lambda e: e.tensor_scalar(core.wq[:, :], core.wq[:, :], 1.0, None, ALU.min), s)
    y = [core.gated, core.hid]
    peak = some(core, NC)
    y_free = [None] * 2
    core.have_x2 = []
    xnT = core.mix[:, :, :].rearrange("p a b -> p (a b)")
    have_xn = []
    stats = some(core, 6 * NT)
    z_free = [None] * 2
    hs_free = [None] * 2
    have_rows = [None] * NC

    def bring(c):
        have_rows[c] = [gather(core, f"back_{c * TPC + t}", y[c % 2][:, 0, t * P:(t + 1) * P], core.ffn1_rows,
                                    core.placeF[:, c * TPC + t:c * TPC + t + 1], core.ffn1_sent, done, y_free[c % 2], core.have_placeF)
                        for t in range(TPC)]

    def chunk(c):
        i = c % 2
        cols = slice(c * CH, (c + 1) * CH)
        rows = core.x_tok[:, c * TPC:(c + 1) * TPC, :]
        s = y_free[i] = dve.do(lambda e: e.tensor_tensor(rows, rows, split(y[i][:, 0, :], TPC), ALU.add), have_rows[c])
        if c + 2 < NC:
            bring(c + 2)
        m = transposes(core, i, lambda t: core.x_tok[:, c * TPC + t, :], s, core.freed[i])
        have_xT = freed[i] = act.do(lambda e: e.activation(core.xT[:, cols], bank[i][:, :], ACT.Copy), m, core.xT_free)
        yield
        m = products(core, lambda e, _: e.matmul(bank[2 + i][:, :], core.adaT[:, :], core.xT[:, cols], start=True, stop=True), 1, have_xT, core.got2, core.freed[2 + i])
        nseq = CH // SEQ
        have_hs = freed[2 + i] = dve.do(lambda e: e.tensor_tensor(
            split(core.hsT[:, i, :], nseq), split(bank[2 + i][:, :], nseq), bc(wx[:, c * nseq:(c + 1) * nseq], SEQ), ALU.mult),
            m, have_wx, hs_free[i])
        yield

        def product(e, n):
            t, n = divmod(n, 2)
            to = bank[4 + i][:, t * P:(t + 1) * P]
            if n == 0:
                return e.matmul(to, core.xT[:, (c * TPC + t) * P:(c * TPC + t + 1) * P], core.wbT[:, :], start=True, stop=False)
            return e.matmul(to, core.hsT[:, i, t * P:(t + 1) * P], core.adbT[:, :], start=False, stop=True)
        m = hs_free[i] = products(core, product, 2 * TPC, have_hs, core.freed[4 + i])
        z2 = core.z2[:, i, :]
        s = freed[4 + i] = dve.do(lambda e: e.tensor_tensor(
            split(z2, TPC), split(bank[4 + i][:, :], TPC), bm(core.bb2[:, :], TPC), ALU.add), m, z_free[i])
        for t in range(TPC):
            j = c * TPC + t
            dve.do(lambda e, t=t, j=j: e.bn_stats(stats[:, 6 * j:6 * j + 6], z2[:, t * P:(t + 1) * P]), s)
        ok, minus, rstd = mean_rstd(core, stats[:, 6 * c * TPC:6 * (c + 1) * TPC], TPC, 1e-3, dve.last())
        yield
        for t in range(TPC):
            tile = z2[:, t * P:(t + 1) * P]
            s = dve.do(lambda e, t=t, tile=tile: e.tensor_scalar(tile, tile, minus[:, t:t + 1], rstd[:, t:t + 1], ALU.add, ALU.mult), ok)
        m = z_free[i] = transposes(core, 6 + i, lambda t: z2[:, t * P:(t + 1) * P], s, core.freed[6 + i])
        s = freed[6 + i] = act.do(lambda e: e.activation(
            xnT[:, cols], bank[6 + i][:, :], ACT.Identity, bias=core.lng2[:, 1:2], scale=core.lng2[:, 0:1]), m, core.sorts)
        yield
        have_xn.append(dve.do(lambda e: e.tensor_reduce(peak[:, c:c + 1], xnT[:, cols], AX_X, ALU.max, apply_absolute_value=True), s))

    bring(0)
    bring(1)
    interleave([chunk(c) for c in range(NC)], first=[0, 2, 4, 6])
    core.xT_free = pe.last()
    top, topr, gmax, ginv, back = some(core, 1), some(core, 1), some(core, 1), some(core, 1), some(core, 1)
    s = dve.do(lambda e: e.tensor_reduce(top, peak, AX_X, ALU.max), have_xn)
    m = products(core, lambda e, i: e.transpose(bank[6][0:1, 0:P], top, c32(core, "ident")), 1, s, core.freed[6])
    s = freed[6] = dve.do(lambda e: e.tensor_reduce(topr[0:1, :], bank[6][0:1, 0:P], AX_X, ALU.max), m)
    m = products(core, lambda e, i: e.matmul(bank[6][:, 0:1], c32(core, "ones")[0:1, :], topr[0:1, :], start=True, stop=True), 1, s, core.freed[6])
    s = freed[6] = dve.do(lambda e: e.tensor_copy(gmax, bank[6][:, 0:1]), m)
    a = dve.do(lambda e: e.reciprocal(ginv, gmax), s)
    b = dve.do(lambda e: e.scalar_tensor_tensor(back, gmax, 1.0 / 128.0, beta, ALU.mult, ALU.mult), s, have_beta)
    a = dve.do(lambda e: e.tensor_scalar(ginv, ginv, 128.0, None, ALU.mult), a)
    most = float(np.float32(128.0 - 1e-5))
    for c in range(NC):
        cols = slice(c * CH, (c + 1) * CH)
        s = dve.do(lambda e, cols=cols: e.tensor_scalar(xnT[:, cols], xnT[:, cols], ginv, most, ALU.mult, ALU.min), a, have_xn)
        s = dve.do(lambda e, cols=cols: e.tensor_scalar(xnT[:, cols], xnT[:, cols], -most, None, ALU.max), s)
        k = c % 2
        m = products(core, lambda e, t, c=c, k=k: e.matmul(
            bank[k][:, t * P:(t + 1) * P], xnT[:, (c * TPC + t) * P:(c * TPC + t + 1) * P], core.wq[:, :], start=True, stop=True), TPC, s, have_wq, core.freed[k])
        rows = core.x_tok[:, c * TPC:(c + 1) * TPC, :]
        s = freed[k] = dve.do(lambda e, k=k, rows=rows: e.scalar_tensor_tensor(rows, split(bank[k][:, :], TPC), back, rows, ALU.mult, ALU.add), m, b)
        core.have_x2.append(s)
        core.kept_x3 = move(core, core.sp, "x3_rows", tiles_of(core.x3_rows)[:, c * TPC:(c + 1) * TPC, :], rows, s)
    core.mix_free = pe.last()


def signs(core):
    dve, kf = core.dve, core.kf
    s = dve.do(lambda e: e.tensor_scalar(kf[:, :], core.kraw[:, 0:2 * F3], 2.0, None, ALU.mult), core.got_k)
    yield
    dve.do(lambda e: e.tensor_tensor(core.w3a[:, :], kf[:, 0:F3], kf[:, F3:2 * F3], ALU.subtract), s)
    yield
    for i in range(4):
        dve.do(lambda e, i=i: e.tensor_scalar(core.w3b[:, i * F3:(i + 1) * F3], core.kraw[:, (2 + i) * F3:(3 + i) * F3],
                                              2.0, -1.0, ALU.mult, ALU.add))
        yield
    dve.do(lambda e: e.tensor_scalar(core.w3d[:, :], core.kraw[:, 6 * F3:], 2.0, -1.0, ALU.mult, ALU.add))
    yield
    core.have_signs = dve.do(lambda e: e.tensor_scalar(core.s3[:, 1:3], core.s3[:, 1:3], 2.0, None, ALU.mult), core.got_s3)


def layer3_mixture(core):
    r, fetched = core.route3, {}
    making = signs(core)

    def item(g):
        def send(y, m):
            slot = g % 3
            s = core.dve.do(lambda e: e.tensor_copy(core.result[:, slot, :], y), m, core.result_sent[slot])
            core.result_sent[slot] = move(core, core.sp, f"sent_{slot}", core.mix3_rows[g * P:(g + 1) * P], core.result[:, slot, :], s)
            return s
        return dict(width=I3, func=ACT.Silu, bias=core.bias3, rows=fetched[g], first=(r["first"][0:1, g:g + 1], r["have_first"]), most=(E - 1) * W3C, w=core.w3c,
                    have_w=[core.got_w3c, core.have_bias3], sink=send, slot=g % 4)

    def fetch(g):
        if g < G3:
            fetched[g] = gathered(core, core.x3_rows, r, g, core.kept_x3)
    for g in range(4):
        fetch(g)
    for i in experts(core, G3, item):
        fetch(i + 4)
        next(making, None)
    run(making)
    core.mixture3_sent = list(core.result_sent)


def layer3_ffn(core):
    pe, act, dve, bank, freed = core.pe, core.act, core.dve, core.bank, core.freed
    u = core.mix
    got = [gather(core, f"back_{j}", u[:, j, :], core.mix3_rows, core.back3[:, j:j + 1], core.mixture3_sent, core.have_back3, core.mix_free) for j in range(NT)]
    hf_free, ahi_free = [None] * 2, [None] * 2
    count = [0]
    used = [0]

    def next_bank():
        used[0] += 1
        return used[0] % 6

    u_free = [None] * 2
    done = [pe.last(), dve.last(), act.last()]
    have_u = [None] * NC
    have_a = [[None] * 4 for _ in range(NC)]
    have_b = [[None] * 4 for _ in range(NC)]
    a_free, b_free = [done] * 2, [done] * 2
    bhi, blo = core.bhi, core.blo

    def halves_of(to_hi, to_lo, k, m, scale, *waits):
        i = count[0] % 2
        count[0] += 1
        h = act.do(lambda e: e.activation(to_hi, bank[k][:, :], ACT.Relu, scale=scale), m, *waits)
        f = act.do(lambda e: e.activation(core.hf[:, i, :], bank[k][:, :], ACT.Relu, scale=scale), hf_free[i])
        freed[k] = f
        hf_free[i] = dve.do(lambda e: e.tensor_tensor(to_lo, core.hf[:, i, :], to_hi.bitcast(F32), ALU.subtract), f, *waits)
        return hf_free[i]

    def input_(c):
        k = next_bank()
        m = transposes(core, k, lambda t: u[:, c * TPC + t, :], got[c * TPC:(c + 1) * TPC], core.freed[k])
        h = act.do(lambda e: e.activation(core.uhi[:, c % 2, :], bank[k][:, :], ACT.Copy), m, u_free[c % 2])
        have_u[c] = freed[k] = dve.do(lambda e: e.tensor_tensor(core.ulo[:, c % 2, :], bank[k][:, :], core.uhi[:, c % 2, :].bitcast(F32), ALU.subtract), h)

    def first(c):
        for f in range(4):
            k = next_bank()
            m = products(core, lambda e, i, f=f, k=k: e.matmul(
                bank[k][:, :], core.w3a[:, f * P:(f + 1) * P], (core.uhi, core.ulo)[i][:, c % 2, :], start=i == 0, stop=i == 1),
                2, have_u[c], core.have_signs, core.freed[k])
            at = slice(f * CH, (f + 1) * CH)
            have_a[c][f] = halves_of(core.ahi[:, c % 2, at], core.alo[:, c % 2, at], k, m, core.s3[:, 0:1], a_free[c % 2])
        u_free[c % 2] = pe.last()

    def second(c):
        for f in range(4):
            k = next_bank()

            def product(e, i, f=f, k=k):
                b, half = divmod(i, 2)
                return e.matmul(bank[k][:, :], core.w3b[:, b * F3 + f * P:b * F3 + (f + 1) * P],
                                (core.ahi, core.alo)[half][:, c % 2, b * CH:(b + 1) * CH], start=i == 0, stop=i == 7)
            m = products(core, product, 8, have_a[c], core.freed[k])
            at = slice(f * CH, (f + 1) * CH)
            have_b[c][f] = halves_of(bhi[:, c % 2, at], blo[:, c % 2, at], k, m, core.s3[:, 1:2], b_free[c % 2])
        a_free[c % 2] = pe.last()

    def third(c):
        k = 6 + c % 2

        def product(e, i):
            t, n = divmod(i, 8)
            b, half = divmod(n, 2)
            return e.matmul(bank[k][:, t * P:(t + 1) * P], (bhi, blo)[half][:, c % 2, b * CH + t * P:b * CH + (t + 1) * P],
                            core.w3d[:, b * P:(b + 1) * P], start=n == 0, stop=n == 7)
        m = b_free[c % 2] = products(core, product, 8 * TPC, have_b[c], core.freed[k])
        rows = core.x_tok[:, c * TPC:(c + 1) * TPC, :]
        s = freed[k] = dve.do(lambda e: e.scalar_tensor_tensor(rows, split(bank[k][:, :], TPC), core.s3[:, 2:3], rows, ALU.mult, ALU.add), m, core.kept_x3)
        core.stored = move(core, core.sp, "out", tiles_of(core.out)[:, c * TPC:(c + 1) * TPC, :], rows, s)

    input_(0)
    first(0)
    for c in range(NC):
        if c + 1 < NC:
            input_(c + 1)
            first(c + 1)
        if c:
            third(c - 1)
        second(c)
    third(NC - 1)
    core.sp.wait(core.stored)


def build(nc, A, out, where32, where16):
    with ExitStack() as ctx:
        core = start(nc, ctx, A, out, where32, where16)
        first_loads(core)
        layer0(core, route_mixtures(core), layer1(core))
        layer2(core)
        layer3_mixture(core)
        layer3_ffn(core)
        with nc.Block() as block:
            block.sync(core.sp.play)
            block.scalar(core.act.play)
            block.vector(core.dve.play)
            block.gpsimd(core.pool.play)
            block.tensor(core.pe.play)


def laid_out(x):
    def get(n):
        return np.asarray(x[n])

    def side(blocks):
        a = blocks.reshape(*blocks.shape[:-2], -1, P, blocks.shape[-1])
        return np.moveaxis(a, -3, -2).reshape(*blocks.shape[:-2], P, -1)

    def turned(a):
        return np.swapaxes(a, -1, -2)

    (cst, where32), (csb, where16) = constants()
    tokens = get("x").reshape(NTOK, P)
    cond = get("cond_8")
    arrays = {
        "cst": cst, "csb": csb, "x": tokens, "xT": tokens.T, "cond": cond, "condT": cond.T,
        "cond_all": cond.T.reshape(E * NSEQ),
        "l0w": np.concatenate([get("L0_cond_weight").transpose(2, 0, 1).reshape(P, E * P), get("L0_cond_mask").T], 1),
        "l0p": np.concatenate([get("L0_ffn_W1").transpose(1, 0, 2).reshape(P, E * H0), side(get("L0_ffn_W2").reshape(E * H0, P)),
                               get("L0_ffn_ln_scale").T, get("L0_ffn_ln_bias").T, get("L0_ffn_Wg").T,
                               get("L0_ffn_b1").reshape(2, P).T, get("L0_cond_bias").reshape(P, 1)], 1),
        "b20": get("L0_ffn_b2"),
        "gate_w": get("L1_ffn_gate_w"),
        "adaT": get("L2_cond_As").reshape(E * R2, P).T, "wbT": get("L2_cond_W_base").T,
        "adbT": get("L2_cond_Bs").transpose(0, 2, 1).reshape(E * R2, P), "bb2": get("L2_cond_b_base"),
        "lng2": np.stack([get("L2_ffn_ln_gamma"), get("L2_ffn_ln_beta")], 1), "wraw": get("L2_ffn_weight"),
        "w1c": np.concatenate([np.concatenate([get("L1_cond_shared_" + n)[None], get("L1_cond_skill_" + n)])
                               if n != "down" else
                               side(np.concatenate([get("L1_cond_shared_down")[None], get("L1_cond_skill_down")]))
                               for n in ("gate", "up", "down")], 2),
        "w1f": np.concatenate([np.concatenate([get(f"L1_ffn_shared_{n}_w")[None], get(f"L1_ffn_routed_{n}_w")])
                               if n != "down" else
                               side(np.concatenate([get("L1_ffn_shared_down_w")[None], get("L1_ffn_routed_down_w")]))
                               for n in ("gate", "up", "down")], 2),
        "w3c": np.concatenate([turned(get("L3_cond_W_up")), turned(get("L3_cond_W_gate")),
                               side(turned(get("L3_cond_W_down")))], 2),
        "b3": np.concatenate([get("L3_cond_b_up"), get("L3_cond_b_gate"), get("L3_cond_b_down")], 1),
    }
    for i in range(3):
        arrays[f"k{i}"] = side(get(f"L3_ffn_k{i}"))
        arrays[f"s{i}"] = get(f"L3_ffn_s{i}").reshape(1)
    return {n: np.ascontiguousarray(a) for n, a in arrays.items()}, where32, where16


def kernel(**inputs):
    import concourse.bacc as bacc
    from concourse.bass_utils import run_bass_kernel_spmd

    arrays, where32, where16 = laid_out(inputs)
    nc = bacc.Bacc("TRN2", target_bir_lowering=False, num_devices=1)
    A = {n: nc.dram_tensor(f"in_{n}", a.shape, mybir.dt.from_np(a.dtype), kind="ExternalInput").ap()
         for n, a in arrays.items()}
    out = nc.dram_tensor("out_x", (NTOK, P), F32, kind="ExternalOutput").ap()
    build(nc, A, out, where32, where16)
    result = run_bass_kernel_spmd(nc, [{f"in_{n}": a for n, a in arrays.items()}], core_ids=[0]).results[0]["out_x"]
    return result.reshape(NSEQ, SEQ, P)
```

```python
from contextlib import ExitStack

import numpy as np

import concourse.bass as bass
from concourse import mybir

F32 = mybir.dt.float32
F32R = mybir.dt.float32r
BF16 = mybir.dt.bfloat16
I32 = mybir.dt.int32
U8 = mybir.dt.uint8
ALU = mybir.AluOpType
ACT = mybir.ActivationFunctionType
AX_X = mybir.AxisListType.X

P = 128
NSEQ, SEQ = 64, 32
NTOK = NSEQ * SEQ
NT = NTOK // P
SPT = P // SEQ
CH = 512
NC = NTOK // CH
TPC = CH // P
E = 8
H0 = 32
I1 = 512
EF, IF = 32, 256
I3 = 256
R2 = 16
F3 = 512


def worst_groups(rows, experts, size):
    return (rows + experts * (size - 1)) // size


G1 = worst_groups(2 * NSEQ, E, SPT)
GF = worst_groups(NTOK, EF, P)
G3 = worst_groups(NSEQ, E, SPT)
L0P = E * H0 + 2 * P + 3 * E + 3
W1C = 3 * I1
W1F = 3 * IF
W3C = 3 * I3
B3C = 2 * I3 + P
SPILL1 = 2 * NTOK
RING = 6
MAGIC = 1.5 * 2.0 ** 23


def f32_constants():
    p = np.arange(P)[:, None]
    q = np.arange(P)[None, :]
    return {
        "ident": (p == q),
        "ones": np.ones((P, P)),
        "quad": np.concatenate([(q // SEQ == r) & (p >= 0) for r in range(SPT)], 1),
        "rank_up": np.repeat(np.arange(E)[None, :] == p, R2, 1),
        "place": np.tile(np.arange(SPT * G1)[None, :], (P, 1)),
        "group": np.tile(np.arange(max(G1, GF, G3))[None, :], (P, 1)),
        "steps_seq": np.tile(SPT * np.arange(NSEQ // SPT)[None, :], (P, 1)),
        "rev": np.tile(EF - np.arange(EF)[None, :], (P, 1)),
        "spill": SPILL1 + P * np.arange(G1)[None, :] + p,
        "within": p % SEQ,
        "first": p < NSEQ,
        "second": p >= NSEQ,
        "absent": -1000.0 * (p >= NSEQ),
        "inner": np.tile((np.arange(EF * NT)[None, :] % NT != 0), (P, 1)),
    }


def bf16_constants():
    p = np.arange(P)[:, None]
    q = np.arange(P)[None, :]
    return {
        "ident": (p == q),
        "before": (p < q),
        "ones": np.ones((P, P)),
        "quad": np.concatenate([(q // SEQ == r) & (p >= 0) for r in range(SPT)], 1),
        "pair": np.concatenate([p * (q // SEQ == r) for r in range(SPT)], 1),
        "spread": np.repeat(np.arange(E)[None, :] == p, H0, 1),
    }


def packed(parts, dtype):
    at, where = 0, {}
    for name, a in parts.items():
        where[name] = (at, a.shape[1])
        at += a.shape[1]
    return np.ascontiguousarray(np.concatenate([np.asarray(a, np.float32) for a in parts.values()], 1)).astype(dtype), where


def constants():
    return packed(f32_constants(), np.float32), packed(bf16_constants(), mybir.dt.np(BF16))


class Lane:

    def __init__(self, sem):
        self.sem, self.count, self.todo, self.passed = sem, 0, [], {}

    def do(self, make, *waits):
        self.wait(*waits)
        self.count += 1
        self.todo.append(lambda e: make(e).then_inc(self.sem, 1))
        return (self.sem, self.count)

    def go(self, make, *waits):
        self.wait(*waits)
        self.todo.append(make)

    def wait(self, *waits):
        for w in waits:
            if w is None:
                continue
            if isinstance(w, list):
                self.wait(*w)
                continue
            sem, value = w
            if self.passed.get(id(sem), 0) < value:
                self.passed[id(sem)] = value
                self.todo.append(lambda e, sem=sem, value=value: e.wait_ge(sem, value))

    def last(self):
        return (self.sem, self.count) if self.count else None

    def play(self, e):
        for make in self.todo:
            make(e)


class Arrivals:

    def __init__(self, sem):
        self.sem, self.count = sem, 0

    def dma(self, lane, make, *waits):
        lane.wait(*waits)
        self.count += 16
        lane.todo.append(lambda e: make(e).then_inc(self.sem, 16))
        return (self.sem, self.count)


def bc(ap, n):
    return ap.unsqueeze(2).broadcast_to([ap.shape[0], ap.shape[1], n])


def bm(ap, m):
    return ap.unsqueeze(1).broadcast_to([ap.shape[0], m, ap.shape[1]])


def split(ap, m):
    return ap.rearrange("p (m n) -> p m n", m=m)


def tiles_of(ap):
    return ap.rearrange("(t p) d -> p t d", p=P)


def run(steps):
    last = None
    for last in steps:
        pass
    return last


def last_of(steps):
    last = None
    for last in steps:
        yield
    return last


def interleave(chains, first):
    chains, now = list(zip(chains, first)), 0
    while chains:
        chains = [(c, at) for c, at in chains if now < at or next(c, run) is not run]
        now += 1


class Core:
    pass


def start(nc, ctx, A, out, where32, where16):
    core = Core()
    core.nc, core.ctx, core.A, core.out = nc, ctx, A, out
    core.where32, core.where16 = where32, where16
    core.pe, core.act, core.dve, core.pool, core.sp = (
        Lane(semaphore(core, "done_" + n)) for n in ("pe", "act", "dve", "pool", "sp"))
    core.arrivals = {}
    memory(core)
    return core


def semaphore(core, name):
    return core.ctx.enter_context(core.nc.semaphore(name))


def arrival(core, name):
    if name not in core.arrivals:
        core.arrivals[name] = Arrivals(semaphore(core, "moved_" + name))
    return core.arrivals[name]


def move(core, lane, name, to, of, *waits):
    return arrival(core, name).dma(lane, lambda e: e.dma_start(to, of), *waits)


def gather(core, name, to, of, index, *waits):
    at = bass.IndirectOffsetOnAxis(index, 0)
    return arrival(core, name).dma(core.pool, lambda e: e.indirect_dma_start(to, None, of, at), *waits)


def scatter(core, name, to, index, of, *waits):
    at = bass.IndirectOffsetOnAxis(index, 0)
    return arrival(core, name).dma(core.pool, lambda e: e.indirect_dma_start(to, at, of, None), *waits)


def memory(core):
    nc = core.nc
    base = -(-nc.sbuf_base // 64) * 64
    end = nc.sbuf_usable_end
    core.ctx.enter_context(nc.sbuf_tensor("arena", [P, (nc.sbuf_bytes_remaining - 128) // 4], F32))
    size_of = {F32: 4, F32R: 4, BF16: 2, I32: 4, U8: 1}
    top = [base]

    def put(name, shape, dt=F32, at=top):
        tensor = nc.alloc_sbuf_tensor_at(name, shape, dt, offset=at[0])
        at[0] += -(-int(np.prod(shape[1:])) * size_of[dt] // 32) * 32
        return tensor

    core.cst = put("cst", [P, sum(n for _, n in core.where32.values())])
    core.csb = put("csb", [P, sum(n for _, n in core.where16.values())], BF16)
    core.x_tok = put("x_tok", [P, NT, P])
    core.mix = put("mix", [P, NT, P])
    core.xT = put("xT", [P, NTOK])
    core.small = put("small", [P, 1376])
    core.ints = put("ints", [P, 3 * G1 + 3 * G3 + NT + GF], I32)
    core.hotb1 = put("hotb1", [P, E], BF16)
    core.hotb3 = put("hotb3", [P, E], BF16)
    core.at1 = put("at1", [P, SPT * G1], BF16)
    core.at3 = put("at3", [P, SPT * G3], BF16)
    core.rows = put("rows", [P, RING, P])
    core.rowsT = put("rowsT", [P, 3, P])
    core.gated = put("gated", [P, 2, I1])
    core.hid = put("hid", [P, 2, I1])
    core.hidT = put("hidT", [P, 2, I1])
    core.compared = put("compared", [P, NT * EF])
    core.hotF = put("hotF", [P, NT * EF], BF16)
    at = [top[0]]
    core.counts, core.running = put("counts", [P, NT * EF], at=at), put("running", [P, NT * EF], at=at)
    core.chosen = put("chosen", [P, 2, 2, CH])
    assert at[0] <= top[0] - 2 * CH * 4
    core.result = put("result", [P, 3, P])
    feed = top[0]
    core.w1f = put("w1f", [P, (EF + 1) * W1F])
    core.late = -(-(top[0] + (E + 1) * W1C * 4 - end) // (W1F * 4))
    mixture = top[0] - core.late * W1F * 4
    top = [mixture]
    core.w1c = put("w1c", [P, (E + 1) * W1C], at=top)
    assert top[0] <= end and core.late > 0

    at = [feed]
    core.l0w = put("l0w", [P, (E + 1) * P], at=at)
    core.maskT = core.l0w[:, E * P:]
    core.cond_all = put("cond_all", [P, E * NSEQ], at=at)
    core.scaled = put("scaled", [P, 2, E, CH], at=at)
    core.l0p = put("l0p", [P, L0P], at=at)
    core.w10, core.w20 = core.l0p[:, 0:E * H0], split(core.l0p[:, E * H0:E * H0 + 2 * P], 2)
    core.lnsT, core.wg0, core.b10, core.l0b = (core.l0p[:, L0P - b:L0P - a] for a, b in (
        (E + 3, 3 * E + 3), (3, E + 3), (1, 3), (0, 1)))
    core.b10s = put("b10s", [P, 2], at=at)
    core.w10s = put("w10s", [P, E * H0], at=at)
    core.w10b = put("w10b", [P, E * H0], at=at)
    core.b20 = put("b20", [E, 3 * P], at=at)
    core.b20p = put("b20p", [E, 3 * P], BF16, at=at)
    core.oh0 = put("oh0", [P, NT * E], BF16, at=at)
    core.ohT = put("ohT", [E, NTOK], BF16, at=at)
    core.h0 = put("h0", [P, 2, 2, CH], at=at)
    core.yT = put("yT", [P, NTOK], at=at)
    core.xhat = put("xhat", [P, NT, P], at=at)
    assert at[0] <= mixture, (at[0], mixture)

    core.bhi = put("bhi", [P, 2, 4 * CH], F32R, at=[mixture])
    core.blo = put("blo", [P, 2, 4 * CH], F32R, at=[mixture + 8 * CH * 4])
    at = [mixture + core.late * W1F * 4]
    core.w3c = put("w3c", [P, E * W3C], at=at)
    core.bias3 = put("bias3", [3, E * W3C], BF16, at=at)
    core.adaT = put("adaT", [P, P], at=at)
    core.wbT = put("wbT", [P, P], at=at)
    core.adbT = put("adbT", [P, P], at=at)
    core.bb2 = put("bb2", [P, P], at=at)
    core.lng2 = put("lng2", [P, 2], at=at)
    core.wraw = put("wraw", [P, P], at=at)
    core.s3 = put("s3", [P, 3], at=at)
    assert at[0] <= end, (at[0], end)
    at = [feed]
    core.wq = put("wq", [P, P], at=at)
    core.b3 = put("b3", [E, B3C], at=at)
    core.b3rest = put("b3rest", [E, 2 * B3C], at=at)
    core.b3p = put("b3p", [E, 3 * B3C], BF16, at=at)
    core.hsT = put("hsT", [P, NC, CH], at=at)
    core.kraw = put("kraw", [P, 2 * F3 + 4 * F3 + 4 * P], U8, at=at)
    core.w3a = put("w3a", [P, F3], F32R, at=at)
    core.w3b = put("w3b", [P, 4 * F3], F32R, at=at)
    core.w3d = put("w3d", [P, 4 * P], F32R, at=at)
    core.uhi = put("uhi", [P, 2, CH], F32R, at=at)
    core.ulo = put("ulo", [P, 2, CH], F32R, at=at)
    core.kf = put("kf", [P, 2 * F3], at=[at[0]])
    core.ahi = put("ahi", [P, 2, 4 * CH], F32R, at=at)
    core.alo = put("alo", [P, 2, 4 * CH], F32R, at=at)
    assert at[0] <= mixture, (at[0], mixture)
    core.bank = [core.ctx.enter_context(nc.psum_tensor(f"bank{i}", [P, CH], F32)) for i in range(8)]
    core.freed = [None] * 8
    core.small_at = core.ints_at = 0
    core.rows_free, core.rowsT_free, core.result_sent = [None] * RING, [None] * 3, [None] * 3
    core.gated_free, core.hid_free, core.hidT_free = [None] * 2, [None] * 2, [None] * 2

    def dram(name, n):
        return nc.dram_tensor(name, [n, P], F32).ap()

    core.x1_rows = dram("x1_rows", NTOK)
    core.mix_rows = dram("mix_rows", SPILL1 + P * G1)
    core.sorted_rows = dram("sorted_rows", P * GF)
    core.ffn1_rows = dram("ffn1_rows", P * GF)
    core.x3_rows = dram("x3_rows", NTOK)


def c32(core, name, rows=P):
    at, n = core.where32[name]
    return core.cst[0:rows, at:at + n]


def c16(core, name, rows=P):
    at, n = core.where16[name]
    return core.csb[0:rows, at:at + n]


def some(core, n):
    core.small_at += n
    assert core.small_at <= core.small.shape[1], core.small_at
    return core.small[:, core.small_at - n:core.small_at]


def some_ints(core, n):
    core.ints_at += n
    assert core.ints_at <= core.ints.shape[1], core.ints_at
    return core.ints[:, core.ints_at - n:core.ints_at]


def first_loads(core):
    A, sp, act = core.A, core.sp, core.act
    core.got_maps = move(core, act, "l0w", core.l0w[:, :], A["l0w"])
    core.got_xT = [move(core, sp if c % 2 == 0 else act, f"xT_{c}", core.xT[:, c * CH:(c + 1) * CH], A["xT"][:, c * CH:(c + 1) * CH])
                   for c in range(1)]
    core.got_cond_all = move(core, sp, "cond_all", core.cond_all[:, :], A["cond_all"].partition_broadcast(P))
    core.cond2 = some(core, E)
    core.got_cond = [move(core, sp, "cond_a", core.cond2[0:NSEQ, :], A["cond"]),
                     move(core, sp, "cond_b", core.cond2[NSEQ:P, :], A["cond"])]
    core.got0 = move(core, act, "l0p", core.l0p[:, :], A["l0p"])
    core.got_xT += [move(core, sp if c % 2 == 0 else act, f"xT_{c}", core.xT[:, c * CH:(c + 1) * CH], A["xT"][:, c * CH:(c + 1) * CH])
                    for c in range(1, NC)]
    core.got_b20 = move(core, act, "b20", core.b20[:, 0:P], A["b20"])
    core.got_csb = move(core, act, "csb", core.csb[:, :], A["csb"])
    core.got_cst = move(core, sp, "cst", core.cst[:, :], A["cst"])
    core.condT, core.gate_w = some(core, NSEQ), some(core, EF)
    core.got_kept = [move(core, act, "kept", to, of) for to, of in (
        (core.condT[0:E, :], A["condT"]), (core.gate_w, A["gate_w"]))][-1]
    core.got_x = move(core, sp, "x_tok", core.x_tok[:, :, :], tiles_of(A["x"]))
    core.got_w1c = {}
    for e in range(E + 1):
        core.got_w1c[e] = move(core, sp, f"w1c_{e}", core.w1c[:, e * W1C:(e + 1) * W1C], A["w1c"][e])
    core.halves = some(core, NT)
    core.have_halves = core.pool.do(lambda e: e.memset(core.halves, -0.5))
    zero = core.pool.do(lambda e: e.memset(core.rows[:, 0, :], 0.0))
    core.zeroed = move(core, sp, "zeroed", tiles_of(core.sorted_rows), bm(core.rows[:, 0, :], GF), zero)
    core.rows_free[0] = core.zeroed


def first_max(core, logits, m, n, best, tmp, hot, *waits):
    dve, top = core.dve, some(core, m)
    s = dve.do(lambda e: e.tensor_reduce(best, logits, AX_X, ALU.max), *waits)
    yield
    s = dve.do(lambda e: e.tensor_tensor(tmp, logits, bc(best, n), ALU.is_ge), s)
    yield
    s = dve.do(lambda e: e.tensor_tensor(tmp, tmp, bm(c32(core, "rev")[:, 0:n], m), ALU.mult), s)
    yield
    s = dve.do(lambda e: e.tensor_reduce(top, tmp, AX_X, ALU.max), s)
    yield
    yield dve.do(lambda e: e.tensor_tensor(hot, tmp, bc(top, n), ALU.is_equal), s)


def mean_rstd(core, stats, n, eps, *waits):
    dve = core.dve
    v = stats.rearrange("p (j k) -> p k j", k=6)
    total, apart, var, rstd, minus = (some(core, n) for _ in range(5))
    a = dve.do(lambda e: e.tensor_tensor(total, v[:, 1, :], v[:, 4, :], ALU.add), *waits)
    b = dve.do(lambda e: e.tensor_tensor(apart, v[:, 1, :], v[:, 4, :], ALU.subtract))
    c = dve.do(lambda e: e.tensor_tensor(var, v[:, 2, :], v[:, 5, :], ALU.add))
    a = dve.do(lambda e: e.tensor_scalar(minus, total, -0.5, None, ALU.mult), a)
    b = dve.do(lambda e: e.tensor_tensor(apart, apart, apart, ALU.mult), b)
    c = dve.do(lambda e: e.tensor_scalar(var, var, 1.0 / P, eps, ALU.mult, ALU.add), c)
    c = dve.do(lambda e: e.scalar_tensor_tensor(var, apart, 0.25, var, ALU.mult, ALU.add), b, c)
    c = core.pool.do(lambda e: e.tensor_tensor(rstd, var, core.halves[:, 0:n], ALU.pow), c, core.have_halves)
    return [a, c], minus, rstd


def bf16_parts(core, x, parts, rest, *waits):
    dve, n = core.dve, x.shape[-1]
    s = dve.do(lambda e: e.tensor_copy(parts[:, 0:n], x), *waits)
    s = dve.do(lambda e: e.tensor_tensor(rest[:, 0:n], x, parts[:, 0:n], ALU.subtract), s)
    s = dve.do(lambda e: e.tensor_copy(parts[:, n:2 * n], rest[:, 0:n]), s)
    s = dve.do(lambda e: e.tensor_tensor(rest[:, n:2 * n], rest[:, 0:n], parts[:, n:2 * n], ALU.subtract), s)
    return dve.do(lambda e: e.tensor_copy(parts[:, 2 * n:3 * n], rest[:, n:2 * n]), s)


def products(core, make, n, *waits):
    core.pe.wait(*waits)
    for i in range(n - 1):
        core.pe.go(lambda e, i=i: make(e, i))
    return core.pe.do(lambda e: make(e, n - 1))


def transposes(core, k, of, *waits):
    return products(core, lambda e, t: e.transpose(core.bank[k][:, t * P:(t + 1) * P], of(t), c32(core, "ident")),
                    TPC, *waits)


def choose(core):
    dve, act = core.dve, core.act
    cond = core.cond2
    best1, hot1, tmp = some(core, 1), some(core, E), some(core, E)
    h1 = yield from last_of(first_max(core, bm(cond, 1), 1, E, best1, bm(tmp, 1), bm(hot1, 1), core.got_cond, core.got_cst))
    left, best2, hot2 = some(core, E), some(core, 1), some(core, E)
    s = dve.do(lambda e: e.tensor_scalar(left, hot1, -3.0e38, None, ALU.mult), h1)
    s = dve.do(lambda e: e.tensor_tensor(left, left, cond, ALU.add), s)
    h2 = yield from last_of(first_max(core, bm(left, 1), 1, E, best2, bm(tmp, 1), bm(hot2, 1), s))
    minus, ex, total, rw = some(core, 1), some(core, E), some(core, 1), some(core, E)
    s = dve.do(lambda e: e.tensor_scalar(minus, best1, -1.0, None, ALU.mult))
    s = act.do(lambda e: e.activation(ex, cond, ACT.Exp, bias=minus, scale=1.0), s, core.got_cond)
    s = dve.do(lambda e: e.tensor_reduce(total, ex, AX_X, ALU.add), s)
    s = dve.do(lambda e: e.reciprocal(total, total), s)
    s = dve.do(lambda e: e.tensor_scalar(rw, ex, total, None, ALU.mult), s)
    yield
    t1, t2, w, scaled = some(core, E), some(core, E), some(core, 2), some(core, 2)
    a = dve.do(lambda e: e.tensor_tensor(t1, rw, hot1, ALU.mult), s)
    b = dve.do(lambda e: e.tensor_tensor(t2, rw, hot2, ALU.mult), h2)
    a = dve.do(lambda e: e.tensor_reduce(w[:, 0:1], t1, AX_X, ALU.add), a)
    b = dve.do(lambda e: e.tensor_reduce(w[:, 1:2], t2, AX_X, ALU.add), b)
    both = some(core, 1)
    s = dve.do(lambda e: e.tensor_tensor(both, w[:, 0:1], w[:, 1:2], ALU.add), a, b)
    s = dve.do(lambda e: e.reciprocal(both, both), s)
    s = dve.do(lambda e: e.tensor_scalar(w, w, both, None, ALU.mult), s)
    s = dve.do(lambda e: e.tensor_scalar(scaled, w, 1.0 / 12, None, ALU.mult), s)
    s = dve.do(lambda e: e.scalar_tensor_tensor(w, w, 1.0 - 1.0 / 12, scaled, ALU.mult, ALU.add), s)
    yield
    core.wpair, core.hpair, core.hfirst = some(core, 1), some(core, E), some(core, E)
    first, second = c32(core, "first"), c32(core, "second")
    s = dve.do(lambda e: e.tensor_scalar(core.wpair, w[:, 1:2], second, None, ALU.mult), s)
    s = dve.do(lambda e: e.scalar_tensor_tensor(core.wpair, w[:, 0:1], first, core.wpair, ALU.mult, ALU.add), s)
    s = dve.do(lambda e: e.tensor_scalar(core.hpair, hot2, second, None, ALU.mult))
    s = dve.do(lambda e: e.scalar_tensor_tensor(core.hpair, hot1, first, core.hpair, ALU.mult, ALU.add), s)
    core.have_pairs = dve.do(lambda e: e.tensor_scalar(core.hfirst, hot1, first, None, ALU.mult))


def route(core, hot, hotb, at, groups, columns, weights, absent):
    dve = core.dve
    b, k = core.bank[7], 7
    s = dve.do(lambda e: e.tensor_copy(hotb[:, :], hot), core.have_pairs)
    yield
    m = products(core, lambda e, i: e.matmul(b[:, i * E:(i + 1) * E], c16(core, ("before", "ones")[i]), hotb[:, :],
                                              start=True, stop=True), 2, s, core.got_csb, core.freed[k])
    n = core.where32["steps_seq"][1]
    below = core.chosen[:, 0, 0, 0:E * n]
    ngroups, upto, place = some(core, E), some(core, E), some(core, 1)
    start, pos = some(core, E), some(core, E)
    s = dve.do(lambda e: e.tensor_tensor(split(below, E), bc(b[:, E:2 * E], n), bm(c32(core, "steps_seq"), E), ALU.is_gt), m)
    s = dve.do(lambda e: e.tensor_reduce(ngroups, split(below, E), AX_X, ALU.add), s)
    s = dve.do(lambda e: e.tensor_tensor_scan(upto, c32(core, "ones")[:, 0:E], ngroups, 0.0, ALU.mult, ALU.add), s)
    s = dve.do(lambda e: e.tensor_tensor(start, upto, ngroups, ALU.subtract), s)
    s = core.freed[k] = dve.do(lambda e: e.scalar_tensor_tensor(pos, start, float(SPT), b[:, 0:E], ALU.mult, ALU.add), s)
    yield
    s = dve.do(lambda e: e.tensor_tensor(pos, pos, hot, ALU.mult), s)
    s = dve.do(lambda e: e.tensor_reduce(place, pos, AX_X, ALU.add), s)
    if absent:
        s = dve.do(lambda e: e.tensor_tensor(place, place, c32(core, "absent"), ALU.add), s)
    have_place = s
    yield
    s = dve.do(lambda e: e.tensor_scalar(at[:, :], c32(core, "place")[:, 0:SPT * groups], place, None, ALU.is_equal), s)
    at4 = at[:, :].rearrange("p (g r) -> p r g", r=SPT)
    m = products(core, lambda e, i: e.matmul(
        b[:, 64 * (i // SPT):64 * (i // SPT) + groups],
        c16(core, ("pair", "quad")[i // SPT])[:, i % SPT * P:(i % SPT + 1) * P], at4[:, i % SPT, :],
        start=i % SPT == 0, stop=i % SPT == SPT - 1), 2 * SPT, s, core.freed[k])
    pair, filled, high = some(core, groups), some(core, groups), some(core, groups)
    src, first = some_ints(core, groups), some_ints(core, groups)
    s = dve.do(lambda e: e.tensor_copy(pair, b[:, 0:groups]), m)
    f = core.freed[k] = dve.do(lambda e: e.tensor_copy(filled, b[:, 64:64 + groups]))
    s = dve.do(lambda e: e.tensor_scalar(high, pair, float(NSEQ), -float(NSEQ), ALU.is_ge, ALU.mult), s)
    s = dve.do(lambda e: e.tensor_tensor(high, high, pair, ALU.add), s)
    have_src = dve.do(lambda e: e.tensor_scalar(src, high, float(SEQ), c32(core, "within"), ALU.mult, ALU.add), s)
    yield
    dst, spill = some_ints(core, groups), c32(core, "spill")[:, 0:groups]
    s = dve.do(lambda e: e.tensor_scalar(pair, pair, float(SEQ), c32(core, "within"), ALU.mult, ALU.add), have_src)
    s = dve.do(lambda e: e.tensor_tensor(pair, pair, spill, ALU.subtract), s)
    s = dve.do(lambda e: e.tensor_tensor(pair, pair, filled, ALU.mult), s, f)
    have_dst = dve.do(lambda e: e.tensor_tensor(dst, pair, spill, ALU.add), s)
    yield
    scale = None
    if weights is not None:
        scale = some(core, groups)
        wquad, atf = core.chosen[:, 1, 0, :], core.chosen[:, 1, 1, 0:SPT * groups]
        dve.do(lambda e: e.tensor_scalar(wquad, c32(core, "quad"), weights, None, ALU.mult))
        s = dve.do(lambda e: e.tensor_copy(atf, at[:, :]))
        yield
        f4 = atf.rearrange("p (g r) -> p r g", r=SPT)
        m = products(core, lambda e, r: e.matmul(b[:, 0:groups], wquad[:, r * P:(r + 1) * P], f4[:, r, :],
                                                 start=r == 0, stop=r == SPT - 1), SPT, s, core.freed[k])
        core.freed[k] = dve.do(lambda e: e.tensor_copy(scale, b[:, 0:groups]), m)
        have_dst = [have_dst, core.freed[k]]
        yield
    past, expert = core.chosen[:, 0, 1, 0:groups * E], some(core, groups)
    s = dve.do(lambda e: e.tensor_tensor(split(past, groups), bm(upto, groups), bc(c32(core, "group")[:, 0:groups], E), ALU.is_le),
               have_place)
    s = dve.do(lambda e: e.tensor_reduce(expert, split(past, groups), AX_X, ALU.add), s)
    s = dve.do(lambda e: e.tensor_scalar(expert, expert, float(E - 1), float(columns), ALU.min, ALU.mult), s)
    s = dve.do(lambda e: e.tensor_copy(first, expert), s)
    return dict(src=src, dst=dst, scale=scale, first=first, have_src=have_src, have_dst=have_dst, have_first=s)


def route_mixtures(core):
    yield from choose(core)
    core.route1 = yield from route(core, core.hpair, core.hotb1, core.at1, G1, W1C, core.wpair, False)
    core.route3 = yield from route(core, core.hfirst, core.hotb3, core.at3, G3, W3C, None, True)
    core.routed = [core.dve.last(), core.pe.last()]


def layer0(core, routing, following):
    act, dve, pool = core.act, core.dve, core.pool
    yT, bank, freed = core.yT, core.bank, core.freed
    nseq = CH // SEQ
    scaled_free, h0_free, gated_free = [None] * 2, [None] * 2, core.gated_free
    stats, best = some(core, 6 * NT), some(core, NT)
    spread = core.where16["spread"][0]
    core.have_x1 = [None] * NC
    ready = {}

    def first_matrices():
        have_w10s = pool.do(lambda e: e.tensor_tensor(split(core.w10s[:, :], E), split(core.w10, E), bc(core.lnsT[:, 0:E], H0), ALU.mult), core.got0)
        s = pool.do(lambda e: e.tensor_tensor(split(core.w10b[:, :], E), split(core.w10, E), bc(core.lnsT[:, E:2 * E], H0), ALU.mult))
        m = products(core, lambda e, h: e.matmul(bank[6][:, h:h + 1], core.w10b[:, h * P:(h + 1) * P], c32(core, "ones")[:, 0:1],
                                                 start=True, stop=True), 2, s, core.got_cst, freed[6])
        freed[6] = dve.do(lambda e: e.tensor_tensor(core.b10s[:, :], core.b10, bank[6][:, 0:2], ALU.add), m, core.got0)
        ready["first"] = [have_w10s, freed[6]]
        ready["b20"] = bf16_parts(core, core.b20[:, 0:P], core.b20p, core.b20[:, P:3 * P], core.got_b20)

    have_yT = []

    have_scaled = {}

    def scalings():
        for c in range(NC):
            for g in range(E):
                if c == 0:
                    w = core.l0w[:, g * P:(g + 1) * P]
                    dve.do(lambda e, w=w: e.tensor_tensor(w, w, core.maskT, ALU.mult), core.got_maps)
                have_scaled[c, g] = dve.do(lambda e, g=g, c=c: e.tensor_tensor(
                    split(core.scaled[:, c % 2, g, :], nseq), split(core.xT[:, c * CH:(c + 1) * CH], nseq),
                    bc(core.cond_all[:, g * NSEQ + c * nseq:g * NSEQ + (c + 1) * nseq], SEQ), ALU.mult),
                    core.got_xT[c], core.got_cond_all, scaled_free[c % 2])
                if g % 2:
                    yield

    def maps():
        for c in range(NC):
            k = 4 * (c % 2)
            for g in range(E):
                m = products(core, lambda e, _, g=g, c=c, k=k: e.matmul(
                    bank[k][:, :], core.l0w[:, g * P:(g + 1) * P], core.scaled[:, c % 2, g, :], start=g == 0, stop=g == E - 1),
                    1, have_scaled[c, g], freed[k])
                if g < E - 1 and g % 2:
                    yield
            scaled_free[c % 2] = m
            freed[k] = act.do(lambda e, c=c, k=k: e.activation(yT[:, c * CH:(c + 1) * CH], bank[k][:, :], ACT.Identity, bias=core.l0b[:, 0:1], scale=1.0), m, core.got0)
            have_yT.append(freed[k])
            yield

    def chunk(c):
        i = c % 2
        b0, b1, b2, b3 = (4 * i + k for k in range(4))
        cols = slice(c * CH, (c + 1) * CH)
        tiles = range(c * TPC, (c + 1) * TPC)
        if c == 0:
            first_matrices()
        have_lg = products(core, lambda e, t: e.matmul(bank[b2][:, t * E:(t + 1) * E], yT[:, tiles[t] * P:(tiles[t] + 1) * P], core.wg0,
                                                       start=True, stop=True), TPC, have_yT[c], core.got0, freed[b2])
        m = transposes(core, b1, lambda t: yT[:, tiles[t] * P:(tiles[t] + 1) * P], have_yT[c], core.got_cst, freed[b1])
        for t in range(TPC):
            dve.do(lambda e, t=t: e.bn_stats(stats[:, 6 * tiles[t]:6 * tiles[t] + 6], bank[b1][:, t * P:(t + 1) * P]), m)
        ok, minus, rstd = mean_rstd(core, stats[:, 6 * c * TPC:6 * (c + 1) * TPC], TPC, 1e-5, dve.last())
        oh0 = core.oh0[:, c * TPC * E:(c + 1) * TPC * E]
        tmp = some(core, TPC * E)
        hot = run(first_max(core, split(bank[b2][:, 0:TPC * E], TPC), TPC, E, best[:, c * TPC:(c + 1) * TPC], split(tmp, TPC), split(oh0, TPC), have_lg))
        freed[b2] = hot
        for t in range(TPC):
            s = dve.do(lambda e, t=t: e.tensor_scalar(
                core.xhat[:, tiles[t], :], bank[b1][:, t * P:(t + 1) * P], minus[:, t:t + 1], rstd[:, t:t + 1], ALU.add, ALU.mult), ok)
        freed[b1] = s
        yield
        yield
        half = bank[b2][0:E, 0:CH // 2].bitcast(BF16)
        m = products(core, lambda e, t: e.transpose(half[:, t * P:(t + 1) * P], oh0[:, t * E:(t + 1) * E], c16(core, "ident")),
                     TPC, hot, core.got_csb, freed[b2])
        have_ohT = freed[b2] = act.do(lambda e: e.activation(core.ohT[:, cols], half, ACT.Copy), m)
        m = transposes(core, b3, lambda t: core.xhat[:, tiles[t], :], s, freed[b3])
        have_xhT = freed[b3] = act.do(lambda e: e.activation(core.xT[:, cols], bank[b3][:, :], ACT.Copy), m)
        yield
        for h, k, k2 in ((0, b0, b2), (1, b3, b1)):
            m = products(core, lambda e, _, h=h, k=k: e.matmul(bank[k][:, :], core.w10s[:, h * P:(h + 1) * P], core.xT[:, cols],
                                                               start=True, stop=True), 1, have_xhT, ready["first"], freed[k])
            m2 = products(core, lambda e, _, h=h, k2=k2: e.matmul(
                bank[k2][:, :], core.csb[0:E, spread + h * P:spread + (h + 1) * P], core.ohT[:, cols],
                start=True, stop=True), 1, have_ohT, freed[k2])
            freed[k] = act.do(lambda e, h=h, k=k: e.activation(
                core.gated[:, h, :], bank[k][:, :], ACT.Gelu, bias=core.b10s[:, h:h + 1], scale=1.0), m, ready["first"], gated_free[h])
            have_h = freed[k2] = gated_free[h] = dve.do(lambda e, h=h, k2=k2: e.tensor_tensor(
                core.h0[:, i, h, :], core.gated[:, h, :], bank[k2][:, :], ALU.mult), freed[k], m2, h0_free[i])
        yield

        def product(e, n):
            t, n = divmod(n, 5)
            j = tiles[t]
            to = bank[b1][:, t * P:(t + 1) * P]
            if n < 2:
                return e.matmul(to, core.h0[:, i, n, t * P:(t + 1) * P], core.w20[:, n, :], start=n == 0, stop=False)
            return e.matmul(to, core.ohT[:, j * P:(j + 1) * P], core.b20p[:, (n - 2) * P:(n - 1) * P], start=False, stop=n == 4)
        m = h0_free[i] = products(core, product, 5 * TPC, have_h, ready["b20"], freed[b1])
        rows = core.x_tok[:, c * TPC:(c + 1) * TPC, :]
        s = core.have_x1[c] = freed[b1] = dve.do(lambda e: e.tensor_tensor(rows, rows, split(bank[b1][:, :], TPC), ALU.add), m, core.got_x)
        core.kept_x1 = move(core, core.sp, "x1_rows", tiles_of(core.x1_rows)[:, c * TPC:(c + 1) * TPC, :], rows, s)

    per = E // 2
    last = 2 + per * NC
    interleave([scalings(), maps(), routing, *(chunk(c) for c in range(NC)), following],
               first=[0, 2, 1, *(2 + per * (c + 1) for c in range(NC)), last])


def experts(core, n, item):
    pe, act, dve, bank, freed = core.pe, core.act, core.dve, core.bank, core.freed
    items, state = [], [dict() for _ in range(n)]
    rowsT_free, gated_free, hid_free, hidT_free = core.rowsT_free, core.gated_free, core.hid_free, core.hidT_free

    def turn(i):
        items.append(item(i))
        it, s = items[i], state[i]
        if "turned" in it:
            return
        rows, have = it["rows"]
        m = products(core, lambda e, _: e.transpose(bank[6][:, 0:P], rows, c32(core, "ident")), 1, have, core.freed[6])
        if "slot" in it:
            core.rows_free[it["slot"]] = m
        s["xT"] = core.rowsT[:, i % 3, :]
        s["have_xT"] = freed[6] = dve.do(lambda e: e.tensor_copy(s["xT"], bank[6][:, 0:P]), m, rowsT_free[i % 3])

    def first_products(i):
        it, s = items[i], state[i]
        if "turned" in it:
            s["xT"], s["have_xT"] = it["turned"]()
        width, bias = it["width"], it.get("bias")
        g = i % 2
        u, up_at = (g + 2, 0) if width == I1 else (g, width)
        reg = s["first"] = {}
        if not isinstance(it["first"], int):
            column, have = it["first"]
            pe.wait(have)
            pe.go(lambda e: reg.setdefault("v", e.value_load(column, min_val=0, max_val=it["most"])))
        else:
            reg["v"] = it["first"]
        pe.wait(it.get("have_w"), s["have_xT"], freed[g], freed[u])
        if width == I1:
            pe.go(lambda e: e.matmul(bank[g][:, :], s["xT"], it["w"][:, bass.ds(reg["v"], CH)], start=True, stop=True))
            s["gu"] = pe.do(lambda e: e.matmul(bank[u][:, :], s["xT"], it["w"][:, bass.ds(reg["v"] + CH, CH)], start=True, stop=True))
        else:
            if bias is not None:
                pe.go(lambda e: e.matmul(bank[g][:, :], c16(core, "ones")[0:3, :], bias[:, bass.ds(reg["v"], CH)], start=True, stop=False))
            s["gu"] = pe.do(lambda e: e.matmul(bank[g][:, :], s["xT"], it["w"][:, bass.ds(reg["v"], CH)], start=bias is None, stop=True))
        if "turned" not in it:
            rowsT_free[i % 3] = s["gu"]
        a = act.do(lambda e: e.activation(core.gated[:, i % 2, 0:width], bank[g][:, 0:width], it["func"]), s["gu"], gated_free[i % 2])
        d = dve.do(lambda e: e.tensor_tensor(core.hid[:, i % 2, 0:width], core.gated[:, i % 2, 0:width],
                                             bank[u][:, up_at:up_at + width], ALU.mult), a, hid_free[i % 2])
        gated_free[i % 2] = freed[u] = s["have_hid"] = d
        if g != u:
            freed[g] = a

    def turn_hidden(i):
        s, k, width = state[i], 4 + i % 2, items[i]["width"]
        m = products(core, lambda e, b: e.transpose(bank[k][:, b * P:(b + 1) * P], core.hid[:, i % 2, b * P:(b + 1) * P], c32(core, "ident")),
                     width // P, s["have_hid"], core.freed[k])
        hid_free[i % 2] = m
        s["have_hidT"] = freed[k] = act.do(lambda e: e.activation(core.hidT[:, i % 2, 0:width], bank[k][:, 0:width], ACT.Copy), m, hidT_free[i % 2])

    def second_products(i):
        it, s = items[i], state[i]
        v, width, bias = s["first"], it["width"], it.get("bias")
        to = bank[7][:, 0:P]
        pe.wait(s["have_hidT"], freed[7])
        if bias is not None:
            pe.go(lambda e: e.matmul(to, c16(core, "ones")[0:3, :], bias[:, bass.ds(v["v"] + 2 * width, P)], start=True, stop=False))
        for b in range(width // P):
            s["y"] = pe.do(lambda e, b=b: e.matmul(to, core.hidT[:, i % 2, b * P:(b + 1) * P],
                                                   it["w"][:, bass.ds(v["v"] + 2 * width + b * P, P)],
                                                   start=b == 0 and bias is None, stop=b == width // P - 1))
        hidT_free[i % 2] = s["y"]
        freed[7] = it["sink"](to, s["y"])

    turn(0)
    turn(1)
    for i in range(n + 2):
        if i + 2 < n:
            turn(i + 2)
        if i < n:
            first_products(i)
        if 0 <= i - 2 < n:
            second_products(i - 2)
        if 0 <= i - 1 < n:
            turn_hidden(i - 1)
        yield i


def gathered(core, source, route, g, *waits):
    slot = g % RING
    have = gather(core, f"rows_{slot}", core.rows[:, slot, :], source, route["src"][:, g:g + 1],
                       route["have_src"], core.rows_free[slot], *waits)
    return core.rows[:, slot, :], have


def layer1(core):
    pe, act, dve = core.pe, core.act, core.dve
    core.got_w1f, core.have_mixT, have_mix, fetched = [], [None] * NC, [None] * NT, {}
    ahead = NT // 2 + 1
    ffn = NT + G1
    groups = ffn + NT

    def mixture_item(i):
        if ahead <= i < ahead + G1:
            g, r = i - ahead, core.route1

            def send(y, m):
                slot = g % 3
                s = dve.do(lambda e: e.tensor_scalar(core.result[:, slot, :], y, r["scale"][:, g:g + 1], None, ALU.mult),
                           m, core.result_sent[slot], r["have_dst"])
                core.result_sent[slot] = scatter(core, f"scattered_{slot}", core.mix_rows, r["dst"][:, g:g + 1], core.result[:, slot, :], s)
                return s
            return dict(width=I1, func=ACT.Gelu_apprx_tanh, rows=fetched[g], first=(r["first"][0:1, g:g + 1], r["have_first"]), most=(E - 1) * W1C, w=core.w1c[:, W1C:],
                        have_w=[core.got_w1c[e] for e in range(1, E + 1)], sink=send, slot=g % RING)
        j = i if i < ahead else i - G1

        def keep(y, m):
            have_mix[j] = dve.do(lambda e: e.tensor_copy(core.mix[:, j, :], y), m)
            return have_mix[j]
        return dict(width=I1, func=ACT.Gelu_apprx_tanh, rows=(core.x_tok[:, j, :], core.have_x1[j // TPC]), first=0, w=core.w1c, have_w=core.got_w1c[0], sink=keep)

    def ffn_item(i):
        if i < NT:
            def add(y, m):
                return dve.do(lambda e: e.tensor_tensor(core.x_tok[:, i, :], core.x_tok[:, i, :], y, ALU.add), m, core.kept_x1)
            return dict(width=IF, func=ACT.Silu, turned=lambda: (core.xT[:, i * P:(i + 1) * P], core.have_mixT[i // TPC]), first=0, w=core.w1f,
                        have_w=core.got_w1f[0], sink=add)
        g = i - NT

        def send(y, m):
            slot = g % 3
            s = dve.do(lambda e: e.tensor_copy(core.result[:, slot, :], y), m, core.result_sent[slot])
            core.result_sent[slot] = move(core, core.sp, f"sent_{slot}", core.ffn1_rows[g * P:(g + 1) * P], core.result[:, slot, :], s)
            return s
        return dict(width=IF, func=ACT.Silu, rows=fetched[g], first=(core.firstF[0:1, g:g + 1], core.have_firstF), most=(EF - 1) * W1F,
                    w=core.w1f[:, W1F:], have_w=core.got_routed, sink=send, slot=g % RING)

    chosen_free = {}

    def load(c):
        return [move(core, core.sp, f"chosen_{k}_{c % 2}", split(core.chosen[:, c % 2, k, :], TPC),
                     tiles_of(core.mix_rows[k * NTOK + c * CH:k * NTOK + (c + 1) * CH]), chosen_free.get(c % 2, core.routed), core.result_sent)
                for k in range(2)]

    def add(c, got):
        part = core.mix[:, c * TPC:(c + 1) * TPC, :]
        s = dve.do(lambda e: e.tensor_tensor(part, part, split(core.chosen[:, c % 2, 0, :], TPC), ALU.add), got, have_mix[c * TPC:(c + 1) * TPC])
        chosen_free[c % 2] = dve.do(lambda e: e.tensor_tensor(part, part, split(core.chosen[:, c % 2, 1, :], TPC), ALU.add), s)
        return chosen_free[c % 2]

    def turn(c, s):
        k = 4 + c % 2
        m = transposes(core, k, lambda t: core.mix[:, c * TPC + t, :], s, core.freed[k])
        core.have_mixT[c] = core.freed[k] = act.do(lambda e: e.activation(core.xT[:, c * CH:(c + 1) * CH], core.bank[k][:, :], ACT.Copy), m)

    core.bestF = some(core, NT)

    def choose_experts(c):
        tiles, cols = slice(c * TPC, (c + 1) * TPC), slice(c * TPC * EF, (c + 1) * TPC * EF)
        have_lg = products(core, lambda e, t: e.matmul(
            core.bank[6][:, t * EF:(t + 1) * EF], core.xT[:, (c * TPC + t) * P:(c * TPC + t + 1) * P], core.gate_w, start=True, stop=True),
            TPC, core.have_mixT[c], core.got_kept, core.freed[6])
        core.have_hotF = core.freed[6] = run(first_max(
            core, split(core.bank[6][:, 0:TPC * EF], TPC), TPC, EF, core.bestF[:, tiles], split(core.compared[:, cols], TPC),
            split(core.hotF[:, cols], TPC), have_lg))

    def sum_chunk(c):
        s = add(c, loaded[c])
        if c + 2 < NC:
            loaded[c + 2] = load(c + 2)
        yield
        turn(c, s)
        yield
        choose_experts(c)

    begins = {ahead + G1 + 4: 0, ahead + G1 + 5: 1, ahead + G1 + 7: 2, ffn + 1: 3}
    loaded, summing, routing = {}, [], route_tokens(core)
    for i in experts(core, groups + GF, lambda i: mixture_item(i) if i < ffn else ffn_item(i - ffn)):
        if i == ahead - 4:
            assert None not in core.have_x1
            core.layer0_done = [pe.last(), dve.last(), act.last()]
        g = i - (ahead - 4)
        for coming in range(RING - 3) if g == 0 else [g + RING - 4] if g > 0 else []:
            if coming < G1:
                fetched[coming] = gathered(core, core.x1_rows, core.route1, coming, core.kept_x1)
        e, between = divmod(g, 3)
        if not between and 0 <= e < EF + 1 - core.late:
            core.got_w1f.append(move(core, core.sp, "w1f" if e else "w1f_shared", core.w1f[:, e * W1F:(e + 1) * W1F], core.A["w1f"][e],
                                     core.layer0_done, pe.last()))
        if i == ahead + G1 + 2:
            loaded = {0: load(0), 1: load(1)}
        if i in begins:
            summing.append(sum_chunk(begins[i]))
        for chain in summing:
            next(chain, None)
        if i == ffn + 1:
            core.mixture_done = [pe.last(), dve.last(), act.last()]
            layer1_weights(core)
        if i == ffn + 3:
            core.mix_turned, core.counts_free = pe.last(), list(chosen_free.values())
        if i > ffn + 3:
            for _ in range(4):
                next(routing, None)
        g = i - (groups - RING)
        if g == 0:
            run(routing)
        if 0 <= g < GF:
            slot = g % RING
            have = move(core, core.sp, f"sorted_{slot}", core.rows[:, slot, :], core.sorted_rows[g * P:(g + 1) * P], core.sorts, core.rows_free[slot])
            fetched[g] = (core.rows[:, slot, :], have)
        if i == groups:
            core.xT_free = pe.last()
        yield
    core.ffn1_sent = list(core.result_sent)


def layer1_weights(core):
    A, done = core.A, core.mixture_done
    for i in range(EF + 1 - core.late, EF + 1):
        late = move(core, core.sp, "late", core.w1f[:, i * W1F:(i + 1) * W1F], A["w1f"][i], done)
    core.got_routed = [core.got_w1f[-1], late]
    core.got2 = [move(core, core.sp, "w2", to, of, done) for to, of in (
        (core.adaT[:, :], A["adaT"]), (core.wbT[:, :], A["wbT"]), (core.adbT[:, :], A["adbT"]),
        (core.bb2[:, :], A["bb2"].partition_broadcast(P)), (core.lng2[:, :], A["lng2"]), (core.wraw[:, :], A["wraw"]))][-1]
    core.got_s3 = [move(core, core.sp, "s3", core.s3[:, i:i + 1], A[f"s{i}"].partition_broadcast(P), done) for i in range(3)][-1]
    for i in range(E):
        core.got_w3c = move(core, core.sp, "w3c", core.w3c[:, i * W3C:(i + 1) * W3C], A["w3c"][i], done)


def route_tokens(core):
    dve, bank = core.dve, core.bank
    tmp, hotb, hot = core.compared, core.hotF, core.have_hotF
    score = some(core, NT)
    core.sorts = [None] * 4
    have_score = core.act.do(lambda e: e.activation(score, core.bestF, ACT.Sigmoid), hot)
    before = products(core, lambda e, i: e.matmul(bank[3][:, :], c16(core, "before"), hotb[:, :], start=True, stop=True), 1, hot, core.freed[3])
    total = products(core, lambda e, i: e.matmul(bank[2][:, :], c16(core, "ones"), hotb[:, :], start=True, stop=True), 1, core.freed[2])
    tot, cum = core.counts, core.running
    s = core.freed[2] = dve.do(lambda e: e.tensor_copy(split(tot[:, :], EF).rearrange("p e j -> p j e"), split(bank[2][:, :], NT)),
                               total, core.counts_free)
    s = dve.do(lambda e: e.tensor_tensor_scan(cum[:, :], c32(core, "inner"), tot[:, :], 0.0, ALU.mult, ALU.add), s)
    yield
    counts = split(cum[:, :], EF)[:, :, NT - 1]
    ngroups, upto, start = some(core, EF), some(core, EF), some(core, EF)
    b = dve.do(lambda e: e.tensor_tensor(tot[:, :], cum[:, :], tot[:, :], ALU.subtract), s)
    a = dve.do(lambda e: e.tensor_scalar(ngroups, counts, 1.0 / P, (P - 1) / P - 0.498, ALU.mult, ALU.add), s)
    a = dve.do(lambda e: e.tensor_scalar(ngroups, ngroups, MAGIC, None, ALU.add), a)
    a = dve.do(lambda e: e.tensor_scalar(ngroups, ngroups, MAGIC, None, ALU.subtract), a)
    a = dve.do(lambda e: e.tensor_tensor_scan(upto, c32(core, "ones")[:, 0:EF], ngroups, 0.0, ALU.mult, ALU.add), a)
    a = dve.do(lambda e: e.tensor_tensor(start, upto, ngroups, ALU.subtract), a)
    yield
    a = dve.do(lambda e: e.scalar_tensor_tensor(split(tot[:, :], EF), bc(start, NT), float(P), split(tot[:, :], EF), ALU.mult, ALU.add), a, b)
    yield
    a = dve.do(lambda e: e.tensor_tensor(split(cum[:, :], NT), split(tot[:, :], EF).rearrange("p e j -> p j e"), split(bank[3][:, :], NT), ALU.add), a, before)
    core.freed[3] = a
    yield
    a = dve.do(lambda e: e.tensor_tensor(cum[:, :], cum[:, :], hotb[:, :], ALU.mult), a)
    place, core.placeF = some(core, NT), some_ints(core, NT)
    a = dve.do(lambda e: e.tensor_reduce(place, split(cum[:, :], NT), AX_X, ALU.add), a)
    a = core.have_placeF = dve.do(lambda e: e.tensor_copy(core.placeF, place), a)
    for c in range(NC):
        part = core.mix[:, c * TPC:(c + 1) * TPC, :]
        have_rows = dve.do(lambda e, c=c, part=part: e.tensor_tensor(part, part, bc(score[:, c * TPC:(c + 1) * TPC], P), ALU.mult), have_score, core.mix_turned)
        for j in range(c * TPC, (c + 1) * TPC):
            core.sorts[j % 4] = scatter(core, f"sort_{j % 4}", core.sorted_rows, core.placeF[:, j:j + 1], core.mix[:, j, :], a, have_rows, core.zeroed)
    yield
    core.firstF = some_ints(core, GF)
    expert = some(core, GF)
    at = 0
    while at < GF:
        m = min(NT, GF - at)
        past = tmp[:, 0:m * EF]
        a = dve.do(lambda e, at=at, m=m, past=past: e.tensor_tensor(
            split(past, m), bm(upto, m), bc(c32(core, "group")[:, at:at + m], EF), ALU.is_le), a)
        a = dve.do(lambda e, at=at, m=m, past=past: e.tensor_reduce(expert[:, at:at + m], split(past, m), AX_X, ALU.add), a)
        at += m
        yield
    a = dve.do(lambda e: e.tensor_scalar(expert, expert, float(EF - 1), float(W1F), ALU.min, ALU.mult), a)
    core.have_firstF = dve.do(lambda e: e.tensor_copy(core.firstF, expert), a)


def layer2(core):
    A, pe, act, dve, bank, freed = core.A, core.pe, core.act, core.dve, core.bank, core.freed
    done = [pe.last(), dve.last(), act.last()]
    core.got_k = [move(core, core.sp, "k", core.kraw[:, at:at + n], A[name], done) for name, at, n in (
        ("k0", 0, 2 * F3), ("k1", 2 * F3, 4 * F3), ("k2", 6 * F3, 4 * P))][-1]
    got_b3 = move(core, core.sp, "b3", core.b3[:, :], A["b3"], done)
    s = bf16_parts(core, core.b3[:, :], core.b3p, core.b3rest, got_b3)
    for part in range(3):
        for i in range(E):
            core.have_bias3 = move(core, core.sp, "bias3", core.bias3[part:part + 1, i * W3C:i * W3C + B3C],
                                        core.b3p[i:i + 1, part * B3C:(part + 1) * B3C], s, core.dve.last())
    wx, absw, beta, inv = some(core, NSEQ), some(core, 1), some(core, 1), some(core, 1)
    m = products(core, lambda e, i: e.matmul(bank[7][:, 0:NSEQ], c32(core, "rank_up", E), core.condT[0:E, :],
                                              start=True, stop=True), 1, core.got_kept, core.freed[7])
    s = freed[7] = dve.do(lambda e: e.tensor_scalar(wx, bank[7][:, 0:NSEQ], 2.0, None, ALU.mult), m)
    have_wx = s
    s = dve.do(lambda e: e.tensor_reduce(absw, core.wraw[:, :], AX_X, ALU.add, apply_absolute_value=True), core.got2)
    m = products(core, lambda e, i: e.matmul(bank[7][:, 0:1], c32(core, "ones"), absw, start=True, stop=True), 1, s, core.freed[7])
    have_beta = freed[7] = dve.do(lambda e: e.tensor_scalar(beta, bank[7][:, 0:1], 1.0 / (P * P), None, ALU.mult), m)
    s = dve.do(lambda e: e.tensor_scalar(inv, beta, 1e-5, None, ALU.add), have_beta)
    s = dve.do(lambda e: e.reciprocal(inv, inv), s)
    s = dve.do(lambda e: e.tensor_scalar(core.wq[:, :], core.wraw[:, :], inv, MAGIC, ALU.mult, ALU.add), s)
    s = dve.do(lambda e: e.tensor_scalar(core.wq[:, :], core.wq[:, :], MAGIC, -1.0, ALU.subtract, ALU.max), s)
    have_wq = dve.do(lambda e: e.tensor_scalar(core.wq[:, :], core.wq[:, :], 1.0, None, ALU.min), s)
    y = [(core.gated, core.hid)[c % 2][:, c // 2, :] for c in range(NC)]
    peak = some(core, NC)
    xnT = core.mix[:, :, :].rearrange("p a b -> p (a b)")
    have_xn = []
    stats = some(core, 6 * NT)
    have_rows = [None] * NC

    def bring(c):
        have_rows[c] = [gather(core, f"back_{c * TPC + t}", y[c][:, t * P:(t + 1) * P], core.ffn1_rows,
                               core.placeF[:, c * TPC + t:c * TPC + t + 1], core.ffn1_sent, done, core.have_placeF)
                        for t in range(TPC)]

    def chunk(c):
        b0, b1, nseq = 2 * c, 2 * c + 1, CH // SEQ
        tiles, cols = range(c * TPC, (c + 1) * TPC), slice(c * CH, (c + 1) * CH)
        rows = core.x_tok[:, c * TPC:(c + 1) * TPC, :]
        s = dve.do(lambda e: e.tensor_tensor(rows, rows, split(y[c], TPC), ALU.add), have_rows[c])
        yield
        m = transposes(core, b0, lambda t: core.x_tok[:, tiles[t], :], s, freed[b0])
        yield
        have_xT = freed[b0] = act.do(lambda e: e.activation(core.xT[:, cols], bank[b0][:, :], ACT.Copy), m, core.xT_free)
        yield
        m = products(core, lambda e, _: e.matmul(bank[b1][:, :], core.adaT[:, :], core.xT[:, cols], start=True, stop=True), 1, have_xT, core.got2, freed[b1])
        yield
        have_hs = freed[b1] = dve.do(lambda e: e.tensor_tensor(
            split(core.hsT[:, c, :], nseq), split(bank[b1][:, :], nseq), bc(wx[:, c * nseq:(c + 1) * nseq], SEQ), ALU.mult), m, have_wx)
        yield

        def product(e, n):
            t, n = divmod(n, 2)
            to = bank[b0][:, t * P:(t + 1) * P]
            if n == 0:
                return e.matmul(to, core.xT[:, tiles[t] * P:(tiles[t] + 1) * P], core.wbT[:, :], start=True, stop=False)
            return e.matmul(to, core.hsT[:, c, t * P:(t + 1) * P], core.adbT[:, :], start=False, stop=True)
        m = products(core, product, 2 * TPC, have_hs, freed[b0])
        yield
        s = freed[b0] = dve.do(lambda e: e.tensor_tensor(
            split(y[c], TPC), split(bank[b0][:, :], TPC), bm(core.bb2[:, :], TPC), ALU.add), m)
        for t in range(TPC):
            dve.do(lambda e, t=t: e.bn_stats(stats[:, 6 * tiles[t]:6 * tiles[t] + 6], y[c][:, t * P:(t + 1) * P]), s)
        ok, minus, rstd = mean_rstd(core, stats[:, 6 * c * TPC:6 * (c + 1) * TPC], TPC, 1e-3, dve.last())
        yield
        yield
        for t in range(TPC):
            tile = y[c][:, t * P:(t + 1) * P]
            s = dve.do(lambda e, t=t, tile=tile: e.tensor_scalar(tile, tile, minus[:, t:t + 1], rstd[:, t:t + 1], ALU.add, ALU.mult), ok)
        yield
        m = transposes(core, b1, lambda t: y[c][:, t * P:(t + 1) * P], s, freed[b1])
        yield
        s = freed[b1] = act.do(lambda e: e.activation(
            xnT[:, cols], bank[b1][:, :], ACT.Identity, bias=core.lng2[:, 1:2], scale=core.lng2[:, 0:1]), m, core.sorts)
        yield
        have_xn.append(dve.do(lambda e: e.tensor_reduce(peak[:, c:c + 1], xnT[:, cols], AX_X, ALU.max, apply_absolute_value=True), s))

    for c in range(NC):
        bring(c)
    interleave([chunk(c) for c in range(NC)], first=[2 * c for c in range(NC)])
    core.xT_free = pe.last()
    top, topr, gmax, ginv, back = some(core, 1), some(core, 1), some(core, 1), some(core, 1), some(core, 1)
    s = dve.do(lambda e: e.tensor_reduce(top, peak, AX_X, ALU.max), have_xn)
    m = products(core, lambda e, i: e.transpose(bank[6][0:1, 0:P], top, c32(core, "ident")), 1, s, core.freed[6])
    s = freed[6] = dve.do(lambda e: e.tensor_reduce(topr[0:1, :], bank[6][0:1, 0:P], AX_X, ALU.max), m)
    m = products(core, lambda e, i: e.matmul(bank[6][:, 0:1], c32(core, "ones")[0:1, :], topr[0:1, :], start=True, stop=True), 1, s, core.freed[6])
    s = freed[6] = dve.do(lambda e: e.tensor_copy(gmax, bank[6][:, 0:1]), m)
    a = dve.do(lambda e: e.reciprocal(ginv, gmax), s)
    b = dve.do(lambda e: e.scalar_tensor_tensor(back, gmax, 1.0 / 128.0, beta, ALU.mult, ALU.mult), s, have_beta)
    a = dve.do(lambda e: e.tensor_scalar(ginv, ginv, 128.0, None, ALU.mult), a)
    most = float(np.float32(128.0 - 1e-5))

    def quantised(c):
        cols, k = slice(c * CH, (c + 1) * CH), c % 2
        s = act.do(lambda e: e.activation(xnT[:, cols], xnT[:, cols], ACT.Copy, scale=ginv), a, have_xn)
        yield
        s = dve.do(lambda e: e.tensor_scalar(xnT[:, cols], xnT[:, cols], most, -most, ALU.min, ALU.max), s)
        m = products(core, lambda e, t: e.matmul(
            bank[k][:, t * P:(t + 1) * P], xnT[:, (c * TPC + t) * P:(c * TPC + t + 1) * P], core.wq[:, :], start=True, stop=True),
            TPC, s, have_wq, core.freed[k])
        yield
        rows = core.x_tok[:, c * TPC:(c + 1) * TPC, :]
        s = freed[k] = dve.do(lambda e: e.scalar_tensor_tensor(rows, split(bank[k][:, :], TPC), back, rows, ALU.mult, ALU.add), m, b)
        core.kept_x3 = move(core, core.sp, "x3_rows", tiles_of(core.x3_rows)[:, c * TPC:(c + 1) * TPC, :], rows, s)

    interleave([quantised(c) for c in reversed(range(NC))], first=reversed(range(NC)))
    core.mix_free = pe.last()


def signs(core):
    dve, kf, s3 = core.dve, core.kf, core.s3
    sign, twice, minus, size = (some(core, 2) for _ in range(4))
    core.last_scale = some(core, 1)
    s = dve.do(lambda e: e.tensor_scalar(sign, s3[:, 0:2], 0.0, 2.0, ALU.is_ge, ALU.mult), core.got_s3)
    s = dve.do(lambda e: e.tensor_scalar(minus, sign, -1.0, 1.0, ALU.mult, ALU.add), s)
    s = dve.do(lambda e: e.tensor_scalar(twice, minus, -2.0, None, ALU.mult), s)
    t = dve.do(lambda e: e.tensor_scalar(size, s3[:, 0:2], -1.0, None, ALU.mult))
    t = dve.do(lambda e: e.tensor_tensor(size, size, s3[:, 0:2], ALU.max), t)
    t = dve.do(lambda e: e.scalar_tensor_tensor(core.last_scale, size[:, 0:1], 4.0, size[:, 1:2], ALU.mult, ALU.mult), t)
    dve.do(lambda e: e.tensor_tensor(core.last_scale, core.last_scale, s3[:, 2:3], ALU.mult), t)
    yield
    s = dve.do(lambda e: e.tensor_scalar(kf[:, :], core.kraw[:, 0:2 * F3], twice[:, 0:1], None, ALU.mult), core.got_k, s)
    yield
    dve.do(lambda e: e.tensor_tensor(core.w3a[:, :], kf[:, 0:F3], kf[:, F3:2 * F3], ALU.subtract), s)
    yield
    for i in range(4):
        dve.do(lambda e, i=i: e.tensor_scalar(core.w3b[:, i * F3:(i + 1) * F3], core.kraw[:, (2 + i) * F3:(3 + i) * F3],
                                              twice[:, 1:2], minus[:, 1:2], ALU.mult, ALU.add))
        yield
    core.have_signs = dve.do(lambda e: e.tensor_scalar(core.w3d[:, :], core.kraw[:, 6 * F3:], 2.0, -1.0, ALU.mult, ALU.add))


def layer3_mixture(core):
    r, fetched = core.route3, {}
    making = signs(core)

    def item(g):
        def send(y, m):
            slot = g % 3
            s = core.dve.do(lambda e: e.tensor_copy(core.result[:, slot, :], y), m, core.result_sent[slot], r["have_dst"])
            core.result_sent[slot] = scatter(core, f"scattered_{slot}", core.mix_rows, r["dst"][:, g:g + 1], core.result[:, slot, :], s)
            return s
        return dict(width=I3, func=ACT.Silu, bias=core.bias3, rows=fetched[g], first=(r["first"][0:1, g:g + 1], r["have_first"]), most=(E - 1) * W3C, w=core.w3c,
                    have_w=[core.got_w3c, core.have_bias3], sink=send, slot=g % RING)

    def fetch(g):
        if g < G3:
            fetched[g] = gathered(core, core.x3_rows, r, g, core.kept_x3)
    for g in range(RING):
        fetch(g)
    for i in experts(core, G3, item):
        fetch(i + RING)
        next(making, None)
    run(making)
    core.mixture3_sent = list(core.result_sent)


def layer3_ffn(core):
    pe, act, dve, bank, freed = core.pe, core.act, core.dve, core.bank, core.freed
    u = core.mix
    got = [move(core, core.sp, f"mixed_{c}", u[:, c * TPC:(c + 1) * TPC, :], tiles_of(core.mix_rows[c * CH:(c + 1) * CH]),
                core.mixture3_sent, core.mix_free) for c in range(NC)]
    used = [0]

    def next_bank():
        used[0] += 1
        return used[0] % 6

    u_free = [None] * 2
    done = [pe.last(), dve.last(), act.last()]
    have_u = [None] * NC
    have_a = [[None] * 4 for _ in range(NC)]
    have_b = [[None] * 4 for _ in range(NC)]
    a_free, b_free = [done] * 2, [done] * 2
    bhi, blo = core.bhi, core.blo

    def halves_of(to_hi, to_lo, k, m, *waits):
        s = act.do(lambda e: e.activation(to_hi, bank[k][:, :], ACT.Relu), m, *waits)
        freed[k] = dve.do(lambda e: e.scalar_tensor_tensor(to_lo, bank[k][:, :], 0.0, to_hi.bitcast(F32), ALU.max, ALU.subtract), s)
        return freed[k]

    def input_(c):
        k = next_bank()
        m = transposes(core, k, lambda t: u[:, c * TPC + t, :], got[c], core.freed[k])
        h = act.do(lambda e: e.activation(core.uhi[:, c % 2, :], bank[k][:, :], ACT.Copy), m, u_free[c % 2])
        have_u[c] = freed[k] = dve.do(lambda e: e.tensor_tensor(core.ulo[:, c % 2, :], bank[k][:, :], core.uhi[:, c % 2, :].bitcast(F32), ALU.subtract), h)

    def first(c, f):
        k = next_bank()
        m = products(core, lambda e, i: e.matmul(
            bank[k][:, :], core.w3a[:, f * P:(f + 1) * P], (core.uhi, core.ulo)[i][:, c % 2, :], start=i == 0, stop=i == 1),
            2, have_u[c], core.have_signs, core.freed[k])
        at = slice(f * CH, (f + 1) * CH)
        have_a[c][f] = halves_of(core.ahi[:, c % 2, at], core.alo[:, c % 2, at], k, m, a_free[c % 2])
        u_free[c % 2] = m

    def second(c, f):
        k = next_bank()

        def product(e, i):
            b, half = divmod(i, 2)
            return e.matmul(bank[k][:, :], core.w3b[:, b * F3 + f * P:b * F3 + (f + 1) * P],
                            (core.ahi, core.alo)[half][:, c % 2, b * CH:(b + 1) * CH], start=i == 0, stop=i == 7)
        m = products(core, product, 8, have_a[c], core.freed[k])
        at = slice(f * CH, (f + 1) * CH)
        have_b[c][f] = halves_of(bhi[:, c % 2, at], blo[:, c % 2, at], k, m, b_free[c % 2])
        if f == 3:
            a_free[c % 2] = m

    def third(c):
        k = 6 + c % 2

        def product(e, i):
            t, n = divmod(i, 8)
            b, half = divmod(n, 2)
            return e.matmul(bank[k][:, t * P:(t + 1) * P], (bhi, blo)[half][:, c % 2, b * CH + t * P:b * CH + (t + 1) * P],
                            core.w3d[:, b * P:(b + 1) * P], start=n == 0, stop=n == 7)
        m = b_free[c % 2] = products(core, product, 8 * TPC, have_b[c], core.freed[k])
        rows = core.x_tok[:, c * TPC:(c + 1) * TPC, :]
        s = freed[k] = dve.do(lambda e: e.scalar_tensor_tensor(rows, split(bank[k][:, :], TPC), core.last_scale, rows, ALU.mult, ALU.add), m, core.kept_x3)
        core.stored = move(core, core.sp, "out", tiles_of(core.out)[:, c * TPC:(c + 1) * TPC, :], rows, s)

    input_(0)
    for f in range(4):
        first(0, f)
    for c in range(NC):
        if c + 1 < NC:
            input_(c + 1)
        for f in range(4):
            second(c, f)
            for g in ((0, 1), (2,), (3,), ())[f]:
                if c + 1 < NC:
                    first(c + 1, g)
        if c:
            third(c - 1)
    third(NC - 1)
    core.sp.wait(core.stored)


def build(nc, A, out, where32, where16):
    with ExitStack() as ctx:
        core = start(nc, ctx, A, out, where32, where16)
        first_loads(core)
        layer0(core, route_mixtures(core), layer1(core))
        layer2(core)
        layer3_mixture(core)
        layer3_ffn(core)
        with nc.Block() as block:
            block.sync(core.sp.play)
            block.scalar(core.act.play)
            block.vector(core.dve.play)
            block.gpsimd(core.pool.play)
            block.tensor(core.pe.play)


def laid_out(x):
    def get(n):
        return np.asarray(x[n])

    def side(blocks):
        a = blocks.reshape(*blocks.shape[:-2], -1, P, blocks.shape[-1])
        return np.moveaxis(a, -3, -2).reshape(*blocks.shape[:-2], P, -1)

    def turned(a):
        return np.swapaxes(a, -1, -2)

    (cst, where32), (csb, where16) = constants()
    tokens = get("x").reshape(NTOK, P)
    cond = get("cond_8")
    arrays = {
        "cst": cst, "csb": csb, "x": tokens, "xT": tokens.T, "cond": cond, "condT": cond.T,
        "cond_all": cond.T.reshape(E * NSEQ),
        "l0w": np.concatenate([get("L0_cond_weight").transpose(2, 0, 1).reshape(P, E * P), get("L0_cond_mask").T], 1),
        "l0p": np.concatenate([get("L0_ffn_W1").transpose(1, 0, 2).reshape(P, E * H0), side(get("L0_ffn_W2").reshape(E * H0, P)),
                               get("L0_ffn_ln_scale").T, get("L0_ffn_ln_bias").T, get("L0_ffn_Wg").T,
                               get("L0_ffn_b1").reshape(2, P).T, get("L0_cond_bias").reshape(P, 1)], 1),
        "b20": get("L0_ffn_b2"),
        "gate_w": get("L1_ffn_gate_w"),
        "adaT": get("L2_cond_As").reshape(E * R2, P).T, "wbT": get("L2_cond_W_base").T,
        "adbT": get("L2_cond_Bs").transpose(0, 2, 1).reshape(E * R2, P), "bb2": get("L2_cond_b_base"),
        "lng2": np.stack([get("L2_ffn_ln_gamma"), get("L2_ffn_ln_beta")], 1), "wraw": get("L2_ffn_weight"),
        "w1c": np.concatenate([np.concatenate([get("L1_cond_shared_" + n)[None], get("L1_cond_skill_" + n)])
                               if n != "down" else
                               side(np.concatenate([get("L1_cond_shared_down")[None], get("L1_cond_skill_down")]))
                               for n in ("gate", "up", "down")], 2),
        "w1f": np.concatenate([np.concatenate([get(f"L1_ffn_shared_{n}_w")[None], get(f"L1_ffn_routed_{n}_w")])
                               if n != "down" else
                               side(np.concatenate([get("L1_ffn_shared_down_w")[None], get("L1_ffn_routed_down_w")]))
                               for n in ("gate", "up", "down")], 2),
        "w3c": np.concatenate([turned(get("L3_cond_W_up")), turned(get("L3_cond_W_gate")),
                               side(turned(get("L3_cond_W_down")))], 2),
        "b3": np.concatenate([get("L3_cond_b_up"), get("L3_cond_b_gate"), get("L3_cond_b_down")], 1),
    }
    for i in range(3):
        arrays[f"k{i}"] = side(get(f"L3_ffn_k{i}"))
        arrays[f"s{i}"] = get(f"L3_ffn_s{i}").reshape(1)
    return {n: np.ascontiguousarray(a) for n, a in arrays.items()}, where32, where16


def kernel(**inputs):
    import concourse.bacc as bacc
    from concourse.bass_utils import run_bass_kernel_spmd

    arrays, where32, where16 = laid_out(inputs)
    nc = bacc.Bacc("TRN2", target_bir_lowering=False, num_devices=1)
    A = {n: nc.dram_tensor(f"in_{n}", a.shape, mybir.dt.from_np(a.dtype), kind="ExternalInput").ap()
         for n, a in arrays.items()}
    out = nc.dram_tensor("out_x", (NTOK, P), F32, kind="ExternalOutput").ap()
    build(nc, A, out, where32, where16)
    result = run_bass_kernel_spmd(nc, [{f"in_{n}": a for n, a in arrays.items()}], core_ids=[0]).results[0]["out_x"]
    return result.reshape(NSEQ, SEQ, P)
```
